# Optimizing a Trainium2 kernel written in Bass

```python
import numpy as np
import jax
import jax.numpy as jnp

def _softmax(x, axis=-1):
    return jax.nn.softmax(x, axis=axis)

def _gelu(x):
    return jax.nn.gelu(x, approximate=True)

def _silu(x):
    return jax.nn.silu(x)

def _sigmoid(x):
    return jax.nn.sigmoid(x)

def _layernorm(x, axis=-1, eps=1e-05):
    m = jnp.mean(x, axis=axis, keepdims=True)
    v = jnp.var(x, axis=axis, keepdims=True)
    return (x - m) / jnp.sqrt(v + eps)

def _scatter_add(tgt, idx, src, axis=0):
    return tgt.at[idx].add(src)

def _segment_sum(src, seg, n):
    return jax.ops.segment_sum(src, seg, n)
kernel_name = 'mk_cond_seq_d2_seqx_r4_5a59b3'

def setup_inputs(seed: int=0):
    np.random.seed(seed)
    _w = jnp.asarray

    def _rec_inputs():
        import jax
        import jax.numpy as jnp
        _rk = jax.random.key(seed)
        x = 7.22e-05 + 1 * jax.random.normal(jax.random.fold_in(_rk, 1), (16, 256, 256), jnp.float32)
        _lenS = 256 - jax.random.randint(jax.random.fold_in(_rk, 7), (16,), 0, max(1, 256 // 4) + 1, jnp.int32)
        _lenS2 = 256 - jax.random.randint(jax.random.fold_in(_rk, 8), (16,), 0, max(1, 256 // 4) + 1, jnp.int32)
        cond_1024 = 0.00386106 + 1.00199 * jax.random.normal(jax.random.fold_in(_rk, 11), (16, 256), jnp.float32)
        fside_BxSxS_0 = -1.39393e-06 + 0.999914 * jax.random.normal(jax.random.fold_in(_rk, 12), (16, 256, 256), jnp.float32)
        _validS = jnp.arange(256)[None, :] < _lenS[:, None]
        _validS2 = jnp.arange(256)[None, :] < _lenS2[:, None]
        _causal = jnp.tril(jnp.ones((256, 256), dtype=bool))
        mask_BxS_bk0 = jnp.logical_not(jnp.broadcast_to(_validS[:, :], (16, 256)))
        return (x, cond_1024, fside_BxSxS_0, mask_BxS_bk0)
    x, cond_1024, fside_BxSxS_0, mask_BxS_bk0 = _rec_inputs()

    def _L0_cond_setup():
        import jax, jax.numpy as jnp
        import numpy as np
        K = 15
        KNUM = 8
        BN_EPS = 1e-05

        def _gaussian_kernel1d(sigma, center):
            half = (K - 1) * 0.5
            t = jnp.linspace(-half, half, K)
            pdf = jnp.exp(-0.5 * ((t - center) / (sigma + 0.001)) ** 2)
            return pdf / (pdf.sum() + 0.01)

        def _forward(x, q, sigmas, center_shift, gamma, beta):
            B, C, L = x.shape
            qfft = jnp.fft.fft(q, axis=-1)[:, None, :]
            xfft = jnp.fft.fft(x, axis=-1)
            s = jnp.pad(x.sum(axis=1), ((0, 0), (K // 2, K // 2)), mode='edge')
            outs = []
            for i in range(KNUM):
                g = _gaussian_kernel1d(sigmas[i, 0], center_shift[i, 0])
                blur = jax.lax.conv_general_dilated(s[:, None, :], g[None, None, :], (1,), 'VALID')[:, 0, :]
                x_shift = jnp.broadcast_to(blur[:, None, :], (B, C, L))
                vfft = jnp.fft.fft(x_shift, axis=-1)
                mx = jnp.mean(vfft)
                my = jnp.mean(qfft)
                cov = (vfft - mx) * (qfft - my)
                a = jnp.sum((vfft - mx) ** 2, axis=2, keepdims=True)
                b = jnp.sum((qfft - mx) ** 2, axis=2, keepdims=True)
                rho = cov / (a * b + 0.001)
                w = 1.0 - jnp.exp(-jnp.abs(rho) * 0.1)
                vfilt = qfft * (1.0 - w) + xfft * w
                outs.append(jnp.abs(jnp.fft.ifft(vfilt, axis=-1)) + x)
            o = jnp.stack(outs, axis=2)
            mean = jnp.mean(o, axis=(0, 1, 2))
            var = jnp.var(o, axis=(0, 1, 2))
            o = (o - mean) * jax.lax.rsqrt(var + BN_EPS) * gamma + beta
            scores = jnp.einsum('bl,bckl->bck', q, o)
            attn = jax.nn.softmax(scores, axis=-1)
            return jnp.einsum('bck,bckl->bcl', attn, o)
        key = jax.random.key(seed)
        ks = jax.random.split(key, 4)
        B, C, L = (16, 128, 256)
        x = jax.random.normal(ks[0], (B, C, L), dtype=jnp.float32)
        q = jax.random.normal(ks[1], (B, L), dtype=jnp.float32)
        sigmas = jax.random.uniform(ks[2], (KNUM, 1), dtype=jnp.float32)
        center_shift = jax.random.uniform(ks[3], (KNUM, 1), dtype=jnp.float32)
        gamma = jnp.ones((L,), jnp.float32)
        beta = jnp.zeros((L,), jnp.float32)
        return {'x': x, 'q': q, 'sigmas': sigmas, 'center_shift': center_shift, 'gamma': gamma, 'beta': beta}
    _L0_cond_all = _L0_cond_setup()
    _L0_cond_in = {k: v for k, v in _L0_cond_all.items() if k in ('sigmas', 'center_shift', 'gamma', 'beta')}
    del _L0_cond_all

    def _L1_cond_setup():
        import math
        import jax, jax.numpy as jnp
        import numpy as np
        B, S, L = (4, 256, 256)
        D, H = (256, 16)
        HD = D // H
        HIDDEN = 4 * D
        ROPE_BASE = 10000.0
        EPS = 1e-06

        def rmsnorm(x, w):
            return x * jax.lax.rsqrt(jnp.mean(x * x, axis=-1, keepdims=True) + EPS) * w

        def safe_key_padding_mask(mask):
            all_pad = jnp.all(mask, axis=-1, keepdims=True)
            return jnp.where(all_pad, False, mask)

        def split_heads(x):
            b, t, _ = x.shape
            return x.reshape(b, t, H, HD).transpose(0, 2, 1, 3)

        def merge_heads(x):
            b, _, t, _ = x.shape
            return x.transpose(0, 2, 1, 3).reshape(b, t, H * HD)

        def apply_rope(x):
            t = x.shape[-2]
            pos = jnp.arange(t, dtype=jnp.float32)[:, None]
            freqs = jnp.exp(jnp.arange(0, HD, 2, dtype=jnp.float32) * (-math.log(ROPE_BASE) / HD))
            ang = pos * freqs[None, :]
            sin = jnp.sin(ang).astype(x.dtype)
            cos = jnp.cos(ang).astype(x.dtype)
            even, odd = (x[..., 0::2], x[..., 1::2])
            rot = jnp.stack((even * cos - odd * sin, even * sin + odd * cos), axis=-1)
            return rot.reshape(x.shape)

        def masked_attn(q, k, v, valid_keys):
            scores = jnp.einsum('bhqd,bhkd->bhqk', q, k) / math.sqrt(HD)
            scores = jnp.where(valid_keys[:, None, None, :], scores, jnp.finfo(scores.dtype).min)
            return jnp.einsum('bhqk,bhkd->bhqd', jax.nn.softmax(scores, axis=-1), v)
        key = jax.random.key(seed)
        ks = jax.random.split(key, 30)
        sc = 0.02
        n = lambda k, shp: jax.random.normal(k, shp, jnp.float32)
        inp = {'tokens': n(ks[0], (B, S, D)), 'seq_tokens': n(ks[1], (B, L, D)), 'modulation': n(ks[2], (B, D)), 'attn_norm_w': jnp.ones((D,), jnp.float32), 'qkv_w': n(ks[3], (3 * D, D)) * sc, 'qkv_b': jnp.zeros((3 * D,), jnp.float32), 'out_w': n(ks[4], (D, D)) * sc, 'out_b': jnp.zeros((D,), jnp.float32), 'film_w': n(ks[5], (2 * D, D)) * sc, 'film_b': jnp.zeros((2 * D,), jnp.float32), 'sq_norm_w': jnp.ones((D,), jnp.float32), 's_norm_w': jnp.ones((D,), jnp.float32), 'mha_in_w': n(ks[6], (3 * D, D)) * sc, 'mha_in_b': jnp.zeros((3 * D,), jnp.float32), 'mha_out_w': n(ks[7], (D, D)) * sc, 'mha_out_b': jnp.zeros((D,), jnp.float32), 'gate_w': n(ks[8], (D, 2 * D)) * sc, 'gate_b': jnp.zeros((D,), jnp.float32), 'ffn_norm_w': jnp.ones((D,), jnp.float32), 'gu_w': n(ks[9], (2 * HIDDEN, D)) * sc, 'gu_b': jnp.zeros((2 * HIDDEN,), jnp.float32), 'down_w': n(ks[10], (D, HIDDEN)) * sc, 'down_b': jnp.zeros((D,), jnp.float32), 'padding_mask': jax.random.bernoulli(ks[11], 0.1, (B, S)), 'seq_mask': jax.random.bernoulli(ks[12], 0.1, (B, L))}
        return inp
    _L1_cond_all = _L1_cond_setup()
    _L1_cond_in = {k: v for k, v in _L1_cond_all.items() if k in ('attn_norm_w', 'qkv_w', 'qkv_b', 'out_w', 'out_b', 'film_w', 'film_b', 'sq_norm_w', 's_norm_w', 'mha_in_w', 'mha_in_b', 'mha_out_w', 'mha_out_b', 'gate_w', 'gate_b', 'ffn_norm_w', 'gu_w', 'gu_b', 'down_w', 'down_b')}
    del _L1_cond_all
    return {'x': x, 'cond_1024': cond_1024, 'fside_BxSxS_0': fside_BxSxS_0, 'mask_BxS_bk0': mask_BxS_bk0, 'L0_cond_sigmas': _L0_cond_in['sigmas'], 'L0_cond_center_shift': _L0_cond_in['center_shift'], 'L0_cond_gamma': _L0_cond_in['gamma'], 'L0_cond_beta': _L0_cond_in['beta'], 'L1_cond_attn_norm_w': _L1_cond_in['attn_norm_w'], 'L1_cond_qkv_w': _L1_cond_in['qkv_w'], 'L1_cond_qkv_b': _L1_cond_in['qkv_b'], 'L1_cond_out_w': _L1_cond_in['out_w'], 'L1_cond_out_b': _L1_cond_in['out_b'], 'L1_cond_film_w': _L1_cond_in['film_w'], 'L1_cond_film_b': _L1_cond_in['film_b'], 'L1_cond_sq_norm_w': _L1_cond_in['sq_norm_w'], 'L1_cond_s_norm_w': _L1_cond_in['s_norm_w'], 'L1_cond_mha_in_w': _L1_cond_in['mha_in_w'], 'L1_cond_mha_in_b': _L1_cond_in['mha_in_b'], 'L1_cond_mha_out_w': _L1_cond_in['mha_out_w'], 'L1_cond_mha_out_b': _L1_cond_in['mha_out_b'], 'L1_cond_gate_w': _L1_cond_in['gate_w'], 'L1_cond_gate_b': _L1_cond_in['gate_b'], 'L1_cond_ffn_norm_w': _L1_cond_in['ffn_norm_w'], 'L1_cond_gu_w': _L1_cond_in['gu_w'], 'L1_cond_gu_b': _L1_cond_in['gu_b'], 'L1_cond_down_w': _L1_cond_in['down_w'], 'L1_cond_down_b': _L1_cond_in['down_b']}

def reference(x, cond_1024, fside_BxSxS_0, mask_BxS_bk0, L0_cond_sigmas, L0_cond_center_shift, L0_cond_gamma, L0_cond_beta, L1_cond_attn_norm_w, L1_cond_qkv_w, L1_cond_qkv_b, L1_cond_out_w, L1_cond_out_b, L1_cond_film_w, L1_cond_film_b, L1_cond_sq_norm_w, L1_cond_s_norm_w, L1_cond_mha_in_w, L1_cond_mha_in_b, L1_cond_mha_out_w, L1_cond_mha_out_b, L1_cond_gate_w, L1_cond_gate_b, L1_cond_ffn_norm_w, L1_cond_gu_w, L1_cond_gu_b, L1_cond_down_w, L1_cond_down_b):
    import jax
    import jax.numpy as jnp

    def _L0_cond_ref(x, q, sigmas, center_shift, gamma, beta):
        import jax, jax.numpy as jnp
        import numpy as np
        K = 15
        KNUM = 8
        BN_EPS = 1e-05

        def _gaussian_kernel1d(sigma, center):
            half = (K - 1) * 0.5
            t = jnp.linspace(-half, half, K)
            pdf = jnp.exp(-0.5 * ((t - center) / (sigma + 0.001)) ** 2)
            return pdf / (pdf.sum() + 0.01)

        def _forward(x, q, sigmas, center_shift, gamma, beta):
            B, C, L = x.shape
            qfft = jnp.fft.fft(q, axis=-1)[:, None, :]
            xfft = jnp.fft.fft(x, axis=-1)
            s = jnp.pad(x.sum(axis=1), ((0, 0), (K // 2, K // 2)), mode='edge')
            outs = []
            for i in range(KNUM):
                g = _gaussian_kernel1d(sigmas[i, 0], center_shift[i, 0])
                blur = jax.lax.conv_general_dilated(s[:, None, :], g[None, None, :], (1,), 'VALID')[:, 0, :]
                x_shift = jnp.broadcast_to(blur[:, None, :], (B, C, L))
                vfft = jnp.fft.fft(x_shift, axis=-1)
                mx = jnp.mean(vfft)
                my = jnp.mean(qfft)
                cov = (vfft - mx) * (qfft - my)
                a = jnp.sum((vfft - mx) ** 2, axis=2, keepdims=True)
                b = jnp.sum((qfft - mx) ** 2, axis=2, keepdims=True)
                rho = cov / (a * b + 0.001)
                w = 1.0 - jnp.exp(-jnp.abs(rho) * 0.1)
                vfilt = qfft * (1.0 - w) + xfft * w
                outs.append(jnp.abs(jnp.fft.ifft(vfilt, axis=-1)) + x)
            o = jnp.stack(outs, axis=2)
            mean = jnp.mean(o, axis=(0, 1, 2))
            var = jnp.var(o, axis=(0, 1, 2))
            o = (o - mean) * jax.lax.rsqrt(var + BN_EPS) * gamma + beta
            scores = jnp.einsum('bl,bckl->bck', q, o)
            attn = jax.nn.softmax(scores, axis=-1)
            return jnp.einsum('bck,bckl->bcl', attn, o)
        return _forward(x, q, sigmas, center_shift, gamma, beta)

    def _L1_cond_ref(tokens, seq_tokens, modulation, attn_norm_w, qkv_w, qkv_b, out_w, out_b, film_w, film_b, sq_norm_w, s_norm_w, mha_in_w, mha_in_b, mha_out_w, mha_out_b, gate_w, gate_b, ffn_norm_w, gu_w, gu_b, down_w, down_b, padding_mask, seq_mask):
        import math
        import jax, jax.numpy as jnp
        import numpy as np
        B, S, L = (4, 256, 256)
        D, H = (256, 16)
        HD = D // H
        HIDDEN = 4 * D
        ROPE_BASE = 10000.0
        EPS = 1e-06

        def rmsnorm(x, w):
            return x * jax.lax.rsqrt(jnp.mean(x * x, axis=-1, keepdims=True) + EPS) * w

        def safe_key_padding_mask(mask):
            all_pad = jnp.all(mask, axis=-1, keepdims=True)
            return jnp.where(all_pad, False, mask)

        def split_heads(x):
            b, t, _ = x.shape
            return x.reshape(b, t, H, HD).transpose(0, 2, 1, 3)

        def merge_heads(x):
            b, _, t, _ = x.shape
            return x.transpose(0, 2, 1, 3).reshape(b, t, H * HD)

        def apply_rope(x):
            t = x.shape[-2]
            pos = jnp.arange(t, dtype=jnp.float32)[:, None]
            freqs = jnp.exp(jnp.arange(0, HD, 2, dtype=jnp.float32) * (-math.log(ROPE_BASE) / HD))
            ang = pos * freqs[None, :]
            sin = jnp.sin(ang).astype(x.dtype)
            cos = jnp.cos(ang).astype(x.dtype)
            even, odd = (x[..., 0::2], x[..., 1::2])
            rot = jnp.stack((even * cos - odd * sin, even * sin + odd * cos), axis=-1)
            return rot.reshape(x.shape)

        def masked_attn(q, k, v, valid_keys):
            scores = jnp.einsum('bhqd,bhkd->bhqk', q, k) / math.sqrt(HD)
            scores = jnp.where(valid_keys[:, None, None, :], scores, jnp.finfo(scores.dtype).min)
            return jnp.einsum('bhqk,bhkd->bhqd', jax.nn.softmax(scores, axis=-1), v)
        x = rmsnorm(tokens, attn_norm_w)
        scale, shift = jnp.split(modulation @ film_w.T + film_b, 2, axis=-1)
        x = x * (1.0 + 0.1 * jnp.tanh(scale))[:, None, :] + shift[:, None, :]
        q, k, v = jnp.split(x @ qkv_w.T + qkv_b, 3, axis=-1)
        q, k, v = (split_heads(q), split_heads(k), split_heads(v))
        q, k = (apply_rope(q), apply_rope(k))
        valid = ~safe_key_padding_mask(padding_mask)
        tokens = tokens + merge_heads(masked_attn(q, k, v, valid)) @ out_w.T + out_b
        query = rmsnorm(tokens, sq_norm_w)
        src = rmsnorm(seq_tokens, s_norm_w)
        wq, wk, wv = jnp.split(mha_in_w, 3, axis=0)
        bq, bk, bv = jnp.split(mha_in_b, 3, axis=0)
        cq = split_heads(query @ wq.T + bq)
        ck = split_heads(src @ wk.T + bk)
        cv = split_heads(src @ wv.T + bv)
        svalid = ~safe_key_padding_mask(seq_mask)
        attended = merge_heads(masked_attn(cq, ck, cv, svalid)) @ mha_out_w.T + mha_out_b
        valid_rows = jnp.any(~seq_mask, axis=1).astype(attended.dtype)[:, None, None]
        update = attended * valid_rows
        gate = jax.nn.sigmoid(jnp.concatenate([tokens, update], axis=-1) @ gate_w.T + gate_b)
        tokens = tokens + gate * update
        h = rmsnorm(tokens, ffn_norm_w)
        g, val = jnp.split(h @ gu_w.T + gu_b, 2, axis=-1)
        return tokens + jax.nn.silu(g) * val @ down_w.T + down_b
    x = _L0_cond_ref(x, cond_1024, L0_cond_sigmas, L0_cond_center_shift, L0_cond_gamma, L0_cond_beta)
    x = _L1_cond_ref(x, fside_BxSxS_0, cond_1024, L1_cond_attn_norm_w, L1_cond_qkv_w, L1_cond_qkv_b, L1_cond_out_w, L1_cond_out_b, L1_cond_film_w, L1_cond_film_b, L1_cond_sq_norm_w, L1_cond_s_norm_w, L1_cond_mha_in_w, L1_cond_mha_in_b, L1_cond_mha_out_w, L1_cond_mha_out_b, L1_cond_gate_w, L1_cond_gate_b, L1_cond_ffn_norm_w, L1_cond_gu_w, L1_cond_gu_b, L1_cond_down_w, L1_cond_down_b, mask_BxS_bk0, mask_BxS_bk0)
    return x

_drawn_inputs = setup_inputs


def setup_inputs(seed=0):
    import zlib

    import numpy as np

    out = dict(_drawn_inputs(seed))
    spreads = {'L0_cond_gamma': (1.0, 0.2),
     'L0_cond_beta': (0.0, 0.1),
     'L1_cond_attn_norm_w': (1.0, 0.6),
     'L1_cond_qkv_b': (0.0, 0.293),
     'L1_cond_out_b': (0.0, 0.1),
     'L1_cond_film_b': (0.0, 0.8),
     'L1_cond_sq_norm_w': (1.0, 0.6),
     'L1_cond_s_norm_w': (1.0, 0.6),
     'L1_cond_mha_in_b': (0.0, 0.551),
     'L1_cond_mha_out_b': (0.0, 0.1),
     'L1_cond_gate_b': (0.0, 0.8),
     'L1_cond_ffn_norm_w': (1.0, 0.6),
     'L1_cond_gu_b': (0.0, 0.54),
     'L1_cond_down_b': (0.0, 0.1)}
    factors = {'fside_BxSxS_0': 8.0,
     'L0_cond_sigmas': 8.0,
     'L0_cond_center_shift': 8.0,
     'L1_cond_mha_in_w': 8.0,
     'L1_cond_mha_out_w': 4.101,
     'L1_cond_gate_w': 7.254}
    for name, (base, spread) in spreads.items():
        noise = np.random.default_rng([zlib.crc32(name.encode()), seed]).standard_normal(out[name].shape)
        drawn = base * np.exp(spread * noise) if base else spread * noise
        out[name] = jnp.asarray(drawn.astype(out[name].dtype))
    for name, factor in factors.items():
        out[name] = (out[name] * factor).astype(out[name].dtype)
    return out
```

```python
import math
from contextlib import ExitStack

import numpy as np
import concourse.bass as bass
from concourse import mybir

F32 = mybir.dt.float32
U8 = mybir.dt.uint8
ALU = mybir.AluOpType
ACT = mybir.ActivationFunctionType
AX = mybir.AxisListType

P = 128
B = 16
L = 256
C = 256
KN = 8
TAPS = 15
NT = 2
H = 16
HD = 16
HP = 32
HID = 1024
MT = HID // P
NPAIR = KN // 2
BN_EPS = 1e-5
RMS_EPS = 1e-6
NEG = -1e30
ONE_COL, VW = 16, 17


def shape_tables():
    l = np.arange(L)
    F = np.zeros((L, L))
    k = np.arange(P)
    F[:P] = np.cos(2 * np.pi * ((k[:, None] * l[None]) % L) / L) * math.sqrt(2.0 / L)
    F[0] = math.sqrt(1.0 / L)
    F[P] = np.where(l % 2, -1.0, 1.0) * math.sqrt(1.0 / L)
    F[P + 1:] = np.sin(2 * np.pi * ((k[1:, None] * l[None]) % L) / L) * math.sqrt(2.0 / L)
    W = np.zeros((L, L))
    kk = np.arange(P + 1)
    W[:, :P + 1] = np.cos(2 * np.pi * ((l[:, None] * kk[None]) % L) / L)
    W[:, P + 1:] = np.sin(2 * np.pi * ((l[:, None] * kk[None, 1:P]) % L) / L)
    taps = np.broadcast_to(np.linspace(-7.0, 7.0, TAPS), (P, TAPS))
    avg = np.kron(np.eye(KN), np.full((B, B), 1.0 / B))
    pos = np.arange(C, dtype=np.float32)[:, None]
    freq = np.exp(np.arange(0, HD, 2, dtype=np.float32) * np.float32(-math.log(10000.0) / HD))
    ang = (pos * freq[None]).astype(np.float32)
    cos, sin = np.cos(ang), np.sin(ang)
    c16 = np.repeat(cos, 2, axis=1)
    s16 = np.stack((-sin, sin), axis=-1).reshape(C, HD)

    def rope(t):
        return np.concatenate([np.tile(t, (1, H)) * 0.25, np.tile(t, (1, H))], axis=1)

    out = {"t_F": F, "t_FT": F.T, "t_W": W, "t_taps": taps, "t_avg": avg, "t_eye": np.eye(P),
           "t_cos": rope(c16), "t_sin": rope(s16)}
    return {n: np.ascontiguousarray(a.astype(np.float32)) for n, a in out.items()}


def tiles(v):
    return v.rearrange("(t p) n -> p t n", p=P)


def at(b, per, n):
    return b * per + n


def build(nc, d, out):
    with ExitStack() as ctx:
        ps = [ctx.enter_context(nc.psum_tensor(f"bank{i}", [P, 512], F32)) for i in range(8)]

        def sb(name, shape, dt=F32):
            return ctx.enter_context(nc.sbuf_tensor(name, shape, dt))

        def sem(name):
            return ctx.enter_context(nc.semaphore(name))

        D = sb("D", [P, B, NT, C])
        Fm = sb("Fm", [P, NT, L])
        eye = sb("eye", [P, P])
        wT = sb("wT", [P, NT, KN, B])
        QR = sb("QR", [P, NT, B])
        qg = sb("qg", [P, NT, B])
        RG = sb("RG", [P, L])
        BP = sb("BP", [P, L])
        filmG = sb("filmG", [P, NT, B])
        filmS = sb("filmS", [P, NT, B])
        keybias = sb("keybias", [P, NT, B])
        vrow = sb("vrow", [P, B])
        w_qkv = sb("w_qkv", [P, NT, 3 * L])
        w_out = sb("w_out", [P, NT, L])
        w_min = sb("w_min", [P, NT, 3 * L])
        w_mout = sb("w_mout", [P, NT, L])
        w_gate = sb("w_gate", [P, 4, L])
        w_gu = sb("w_gu", [P, NT, 2 * HID])
        w_down = sb("w_down", [P, MT, L])
        b_qkv = sb("b_qkv", [P, 3 * L])
        b_out = sb("b_out", [P, L])
        b_min = sb("b_min", [P, 3 * L])
        b_mout = sb("b_mout", [P, L])
        b_gate = sb("b_gate", [P, L])
        b_gu = sb("b_gu", [P, 2 * MT])
        b_guh = sb("b_guh", [P, 2 * MT])
        b_down = sb("b_down", [P, L])
        n_sq = sb("n_sq", [P, NT])
        n_s = sb("n_s", [P, NT])
        n_ffn = sb("n_ffn", [P, NT])
        mhalf = sb("mhalf", [P, NT])

        weights_in = sem("weights_in")
        layer1 = [(w_qkv[:], tiles(d["qkv_wT"])), (w_out[:], tiles(d["out_wT"])),
                  (w_min[:], tiles(d["mha_in_wT"])), (w_mout[:], tiles(d["mha_out_wT"])),
                  (w_gate[:], tiles(d["gate_wT"])), (w_gu[:], tiles(d["gu_wT"])),
                  (w_down[:], tiles(d["down_wT"])),
                  (b_qkv[:], d["qkv_b"].partition_broadcast(P)), (b_out[:], d["out_b"].partition_broadcast(P)),
                  (b_min[:], d["mha_in_b"].partition_broadcast(P)), (b_mout[:], d["mha_out_b"].partition_broadcast(P)),
                  (b_gate[:], d["gate_b"].partition_broadcast(P)), (b_down[:], d["down_b"].partition_broadcast(P)),
                  (b_gu[:], d["gu_b"]), (n_sq[:], d["sq_norm_w"]),
                  (n_s[:], d["s_norm_w"]), (n_ffn[:], d["ffn_norm_w"])]

        with ExitStack() as first_ctx:
            def sb1(name, shape, dt=F32):
                return first_ctx.enter_context(nc.sbuf_tensor(name, shape, dt))

            def sem1(name):
                return first_ctx.enter_context(nc.semaphore(name))

            FT = sb1("FT", [P, NT, L])
            Wt = sb1("Wt", [P, NT, L])
            taps = sb1("taps", [P, TAPS])
            avg = sb1("avg", [P, P])
            q16 = sb1("q16", [B, L])
            m8 = sb1("m8", [B, C], U8)
            sig = sb1("sig", [P, 1])
            cen = sb1("cen", [P, 1])
            gamma = sb1("gamma", [P, NT])
            beta = sb1("beta", [P, NT])
            n_attn = sb1("n_attn", [P, NT])
            filmW = sb1("filmW", [P, NT, 2 * L])
            filmB = sb1("filmB", [P, 4])
            ones = sb1("ones", [P, 1])
            xb = sb1("xb", [P, 2, NT, L])
            xT = sb1("xT", [P, B, NT, C])
            xq = sb1("xq", [P, NT, C])
            qT = sb1("qT", [P, NT, B])
            sT8 = sb1("sT8", [P, NT, KN, B])
            qT8 = sb1("qT8", [P, NT, KN, B])
            spad = sb1("spad", [P, L + TAPS - 1])
            g = sb1("g", [P, TAPS])
            gs = sb1("gs", [P, 8])
            blur = sb1("blur", [P, L])
            blurT = sb1("blurT", [P, NT, P])
            V = sb1("V", [P, L])
            QV = sb1("QV", [P, L])
            qy = sb1("qy", [P, L])
            at0 = sb1("at0", [P, 2])
            means = sb1("means", [P, 2])
            tot = sb1("tot", [P, 8])
            w = sb1("w", [P, P + 1])
            w_hi = sb1("w_hi", [P, P])
            half = sb1("half", [P, P + 1])
            mf = sb1("mf", [B, C])
            allpad = sb1("allpad", [B, 2])
            film = sb1("film", [P, 2, NT, B])
            E = sb1("E", [P, 2, NT, 2, C])
            o = sb1("o", [P, 4, 2, C])
            sums = sb1("sums", [P, NT, B * NPAIR])
            squares = sb1("squares", [P, NT, B * NPAIR])
            st = sb1("st", [P, 8, NT])

            tables_in = sem1("tables_in")
            x_in = [sem1(f"x_in{i}") for i in range(2)]
            x_free = sem1("x_free")
            xT_ps, xT_sb, xq_ok = sem1("xT_ps"), sem1("xT_sb"), sem1("xq_ok")
            D_ps, D_sb = sem1("D_ps"), sem1("D_sb")
            consts = sem1("consts")
            q_ps, q_sb, qr_ps, qr_sb = sem1("q_ps"), sem1("q_sb"), sem1("qr_ps"), sem1("qr_sb")
            film_ps, film_th = sem1("film_ps"), sem1("film_th")
            mask_ok, maskT_ps, maskT_sb = sem1("mask_ok"), sem1("maskT_ps"), sem1("maskT_sb")
            s_ps, s_sb, sb_ps = sem1("s_ps"), sem1("s_sb"), sem1("sb_ps")
            step = sem1("step")
            gz_ok, ge_ok = sem1("gz_ok"), sem1("ge_ok")
            blur_ok, blurT_ps, blurT_sb = sem1("blur_ok"), sem1("blurT_ps"), sem1("blurT_sb")
            V_ps, at0_ok, mean_ps = sem1("V_ps"), sem1("at0_ok"), sem1("mean_ps")
            prod_ok, root_ok, th_ok = sem1("prod_ok"), sem1("root_ok"), sem1("th_ok")
            w_ok, wT_ps, wT_sb = sem1("w_ok"), sem1("wT_ps"), sem1("wT_sb")
            E_ok = sem1("E_ok")
            y_ps, o_ok = sem1("y_ps"), sem1("o_ok")
            abs_ok, o_free = sem1("abs_ok"), sem1("o_free")
            var_ok, rstd_ok, bn_ok, bn_ps = sem1("var_ok"), sem1("rstd_ok"), sem1("bn_ok"), sem1("bn_ps")

            small = [(q16[:], d["cond"]), (eye[:], d["t_eye"]), (FT[:], tiles(d["t_FT"])),
                     (Fm[:], tiles(d["t_F"])), (Wt[:], tiles(d["t_W"])), (taps[:], d["t_taps"]),
                     (avg[:], d["t_avg"]), (m8[:], d["mask"]),
                     (gamma[:], d["gamma"]), (beta[:], d["beta"]),
                     (n_attn[:], d["attn_norm_w"]), (filmW[:], tiles(d["film_wT"])),
                     (filmB[:], d["film_b"])]
            for i in range(KN):
                small += [(sig[i * B:(i + 1) * B, :], d["sigmas"][i].partition_broadcast(B)),
                          (cen[i * B:(i + 1) * B, :], d["centers"][i].partition_broadcast(B))]
            ALL_TABLES = 16 * len(small)

            block = first_ctx.enter_context(nc.Block())

            @block.sync
            def _(sp):
                for dst, src in small:
                    sp.dma_start(dst, src).then_inc(tables_in, 16)
                with sp.Fori(0, B // 2) as two:
                    for s in range(2):
                        sp.wait_ge(x_free, two * 2 + s + 1)
                        sp.dma_start(xb[:, s], tiles(d["x"][two * 2 + s])).then_inc(x_in[s], 16)

            @block.gpsimd
            def _(pool):
                nc.gpsimd.memset(ones[:], 1.0).then_inc(consts, 1)
                nc.gpsimd.memset(mhalf[:], -0.5).then_inc(consts, 1)
                nc.gpsimd.memset(half[:], 0.5).then_inc(consts, 1)
                for dst, src in layer1:
                    pool.dma_start(dst, src).then_inc(weights_in, 16)

                pool.wait_ge(prod_ok, 1)
                pool.wait_ge(consts, 3)
                nc.gpsimd.tensor_tensor(w[:], w[:], half[:], ALU.pow).then_inc(root_ok, 1)

                pool.wait_ge(var_ok, 1)
                nc.gpsimd.tensor_tensor(st[:, 4, :], st[:, 3, :], mhalf[:], ALU.pow).then_inc(rstd_ok, 1)

            @block.scalar
            def _(act):
                act.wait_ge(tables_in, ALL_TABLES)
                act.wait_ge(film_ps, 1)
                for ft in range(NT):
                    nc.scalar.activation(film[:, 0, ft, :], ps[6][:, ft * B:(ft + 1) * B], ACT.Tanh,
                                         bias=filmB[:, ft:ft + 1]).then_inc(film_th, 1)
                for ft in range(NT):
                    a = nc.scalar.activation(filmS[:, ft, :], ps[6][:, (2 + ft) * B:(3 + ft) * B], ACT.Identity,
                                             bias=filmB[:, 2 + ft:3 + ft])
                a.then_inc(film_th, 1)

                with act.Fori(0, B) as b:
                    act.wait_ge(xT_ps, b + 1)
                    nc.scalar.activation(xT[:, bass.ds(b, 1), :, :], ps[0][:], ACT.Copy).then_inc(xT_sb, 1)
                    act.wait_ge(D_ps, b + 2)
                    nc.scalar.activation(D[:, bass.ds(b, 1), :, :], ps[1][:], ACT.Copy).then_inc(D_sb, 1)

                act.wait_ge(gz_ok, 1)
                nc.scalar.activation(g[:], g[:], ACT.Exp, scale=-0.5, accum_out=gs[:, 3:4]).then_inc(ge_ok, 1)
                act.wait_ge(root_ok, 1)
                nc.scalar.activation(w[:], w[:], ACT.Tanh, scale=0.05).then_inc(th_ok, 1)

                with act.Fori(0, B) as b:
                    for n in range(2 * NPAIR + 2):
                        if n < 2 * NPAIR:
                            act.wait_ge(y_ps, at(b, 8, n + 1) + 4)
                            act.wait_ge(o_free, at(b, 8, n + 1))
                            nc.scalar.activation(o[:, n % 4], ps[n % 4][:], ACT.Abs).then_inc(abs_ok, 1)
                        if n >= 2:
                            act.wait_ge(o_ok, at(b, 8, n - 1))
                            nc.scalar.activation(
                                o[:, (n - 2) % 4], o[:, (n - 2) % 4], ACT.Square,
                                accum_out=squares[:, n % 2, bass.ds(b * NPAIR + (n - 2) // 2, 1)]).then_inc(o_free, 1)

            @block.tensor
            def _(pe):
                pe.wait_ge(tables_in, ALL_TABLES)
                for lt in range(NT):
                    m = nc.tensor.transpose(ps[7][:, lt * B:(lt + 1) * B], q16[:, lt * P:(lt + 1) * P], eye[0:B, 0:B])
                m.then_inc(q_ps, 1)
                pe.wait_ge(mask_ok, 1)
                for t in range(NT):
                    m = nc.tensor.transpose(ps[5][:, t * B:(t + 1) * B], mf[:, t * P:(t + 1) * P], eye[0:B, 0:B])
                m = nc.tensor.matmul(ps[5][:, 2 * B:3 * B], allpad[:, 1:2].broadcast_to([B, P]), eye[0:B, 0:B],
                                     start=True, stop=True)
                m.then_inc(maskT_ps, 1)
                pe.wait_ge(q_sb, 1)
                for mt in range(4):
                    for kt in range(NT):
                        m = nc.tensor.matmul(ps[6][:, mt * B:(mt + 1) * B], filmW[:, kt, mt * P:(mt + 1) * P],
                                             qT[:, kt, :], start=(kt == 0), stop=(kt == 1))
                m.then_inc(film_ps, 1)
                for rt in range(NT):
                    for kt in range(NT):
                        m = nc.tensor.matmul(ps[4][:, rt * B:(rt + 1) * B], FT[:, kt, rt * P:(rt + 1) * P],
                                             qT[:, kt, :], start=(kt == 0), stop=(kt == 1))
                m.then_inc(qr_ps, 1)

                pe.wait_ge(consts, 1)
                pe.wait_ge(q_sb, 1)
                with pe.Fori(0, B // 2) as two:
                    for s in range(2):
                        pe.wait_ge(x_in[s], at(two, 16, 16))
                        for lt in range(NT):
                            for ct in range(NT):
                                m = nc.tensor.transpose(ps[0][:, lt * C + ct * P:lt * C + (ct + 1) * P],
                                                        xb[:, s, ct, lt * P:(lt + 1) * P], eye[:])
                        m.then_inc(xT_ps, 1)
                        for lt in range(NT):
                            for ct in range(NT):
                                m = nc.tensor.matmul(ps[2][:, bass.ds(two * 2 + (lt * B + s), 1)],
                                                     xb[:, s, ct, lt * P:(lt + 1) * P], ones[:],
                                                     start=(ct == 0), stop=(ct == 1))
                        m.then_inc(x_free, 1)
                        pe.wait_ge(xq_ok, two * 2 + s + 1)
                        for rt in range(NT):
                            for kt in range(NT):
                                m = nc.tensor.matmul(ps[1][:, rt * C:(rt + 1) * C], FT[:, kt, rt * P:(rt + 1) * P],
                                                     xq[:, kt, :], start=(kt == 0), stop=(kt == 1))
                        m.then_inc(D_ps, 1)
                pe.wait_ge(s_sb, 1)
                for lt in range(NT):
                    m = nc.tensor.matmul(ps[3][:, lt * P:(lt + 1) * P],
                                         sT8[:, lt].rearrange("p i b -> p (i b)"), eye[:],
                                         start=True, stop=True)
                m.then_inc(sb_ps, 1)
                pe.wait_ge(blur_ok, 1)
                for lt in range(NT):
                    m = nc.tensor.transpose(ps[4][:, lt * P:(lt + 1) * P], blur[:, lt * P:(lt + 1) * P], eye[:])
                m.then_inc(blurT_ps, 1)
                pe.wait_ge(blurT_sb, 1)
                for lt in range(NT):
                    m = nc.tensor.matmul(ps[5][:, 0:L], blurT[:, lt, :], Wt[:, lt, :], start=(lt == 0), stop=(lt == 1))
                m.then_inc(V_ps, 1)
                for lt in range(NT):
                    m = nc.tensor.matmul(ps[6][:, 0:L], qT8[:, lt].rearrange("p i b -> p (i b)"),
                                         Wt[:, lt, :], start=(lt == 0), stop=(lt == 1))
                m = nc.tensor.matmul(ps[7][:, 0:1], qT8[:, 0].rearrange("p i b -> p (i b)"), eye[:, 0:1],
                                     start=True, stop=True)
                m.then_inc(V_ps, 1)
                pe.wait_ge(at0_ok, 2)
                m = nc.tensor.matmul(ps[4][:, 0:2], avg[:], at0[:], start=True, stop=True)
                m.then_inc(mean_ps, 1)
                pe.wait_ge(w_ok, 3)
                nc.tensor.transpose(ps[3][:, 0:P], w[:, 0:P], eye[:])
                m = nc.tensor.transpose(ps[3][:, P:2 * P], w_hi[:], eye[:])
                m.then_inc(wT_ps, 1)

                pe.wait_ge(wT_sb, 2)
                with pe.Fori(0, B) as b:
                    for pr in range(NPAIR):
                        pe.wait_ge(E_ok, at(b, NPAIR, pr + 1))
                        for lt in range(NT):
                            pe.wait_ge(abs_ok, at(b, 8, 2 * pr + lt + 1))
                            for kt in range(NT):
                                m = nc.tensor.matmul(ps[(pr % 2) * 2 + lt][:], Fm[:, kt, lt * P:(lt + 1) * P],
                                                     E[:, pr % 2, kt, :, :], start=(kt == 0), stop=(kt == 1))
                            m.then_inc(y_ps, 1)

                pe.wait_ge(bn_ok, 2)
                for n in range(2):
                    for lt in range(NT):
                        m = nc.tensor.matmul(ps[4 + n][:, lt * P:(lt + 1) * P],
                                             st[:, 5 + n, lt:lt + 1].broadcast_to([P, P]), eye[:],
                                             start=True, stop=True)
                m.then_inc(bn_ps, 1)

            @block.vector
            def _(dve):
                n = [0]

                def link(ins):
                    n[0] += 1
                    ins.then_inc(step, 1)
                    dve.wait_ge(step, n[0])

                dve.sem_inc(x_free, 2)
                dve.sem_inc(D_ps, 1)
                dve.sem_inc(y_ps, 4)
                dve.sem_inc(abs_ok, 4)
                dve.sem_inc(o_free, 4)
                dve.wait_ge(tables_in, ALL_TABLES)
                link(nc.vector.tensor_copy(mf[:], m8[:]))
                link(nc.vector.tensor_reduce(allpad[:, 0:1], mf[:], AX.X, ALU.min))
                link(nc.vector.tensor_scalar(allpad[:, 1:2], allpad[:, 0:1], -1.0, 1.0, ALU.mult, ALU.add))
                nc.vector.tensor_scalar(mf[:], mf[:], allpad[:, 1:2], NEG, ALU.mult, ALU.mult).then_inc(mask_ok, 1)
                dve.wait_ge(q_ps, 1)
                nc.vector.tensor_copy(qT[:], ps[7][:, 0:2 * B]).then_inc(q_sb, 1)
                dve.wait_ge(maskT_ps, 1)
                nc.vector.tensor_copy(keybias[:], ps[5][:, 0:2 * B]).then_inc(maskT_sb, 1)
                nc.vector.tensor_copy(vrow[:], ps[5][:, 2 * B:3 * B]).then_inc(maskT_sb, 1)
                dve.wait_ge(qr_ps, 1)
                nc.vector.tensor_copy(QR[:], ps[4][:, 0:2 * B]).then_inc(qr_sb, 1)
                dve.wait_ge(film_th, 3)
                link(nc.vector.tensor_scalar(film[:, 1], film[:, 0], 0.1, 1.0, ALU.mult, ALU.add))
                for ft in range(NT):
                    nc.vector.tensor_scalar(filmG[:, ft, :], film[:, 1, ft, :], n_attn[:, ft:ft + 1], None, ALU.mult)
                dve.wait_ge(q_sb, 1)
                with dve.Fori(0, B) as b:
                    dve.wait_ge(xT_sb, b + 1)
                    dve.wait_ge(D_ps, b + 1)
                    for lt in range(NT):
                        v = nc.vector.tensor_scalar(xq[:, lt, :], xT[:, bass.ds(b, 1), lt, :],
                                                    qT[:, lt, bass.ds(b, 1)], None, ALU.subtract)
                    v.then_inc(xq_ok, 1)

                dve.wait_ge(D_ps, B + 1)
                for lt in range(NT):
                    nc.vector.tensor_copy(qT8[:, lt], qT[:, lt, :].unsqueeze(1).broadcast_to([P, KN, B]))
                    v = nc.vector.tensor_copy(
                        sT8[:, lt], ps[2][:, lt * B:(lt + 1) * B].unsqueeze(1).broadcast_to([P, KN, B]))
                v.then_inc(s_sb, 1)
                link(nc.vector.tensor_scalar(gs[:, 0:1], sig[:], 0.001, None, ALU.add))
                link(nc.vector.reciprocal(gs[:, 1:2], gs[:, 0:1]))
                link(nc.vector.tensor_scalar(g[:], taps[:], cen[:, 0:1], gs[:, 1:2], ALU.subtract, ALU.mult))
                nc.vector.tensor_tensor(g[:], g[:], g[:], ALU.mult).then_inc(gz_ok, 1)
                dve.wait_ge(ge_ok, 1)
                link(nc.vector.tensor_scalar(gs[:, 4:5], gs[:, 3:4], 0.01, None, ALU.add))
                link(nc.vector.reciprocal(gs[:, 5:6], gs[:, 4:5]))
                link(nc.vector.tensor_scalar(g[:], g[:], gs[:, 5:6], None, ALU.mult))
                dve.wait_ge(sb_ps, 1)
                half_k = TAPS // 2
                link(nc.vector.tensor_copy(spad[:, half_k:half_k + L], ps[3][:, 0:L]))
                nc.vector.tensor_copy(spad[:, 0:half_k], spad[:, half_k:half_k + 1].broadcast_to([P, half_k]))
                link(nc.vector.tensor_copy(spad[:, half_k + L:], spad[:, half_k + L - 1:half_k + L].broadcast_to([P, half_k])))
                link(nc.vector.tensor_scalar(blur[:], spad[:, 0:L], g[:, 0:1], None, ALU.mult))
                for t in range(1, TAPS):
                    v = nc.vector.scalar_tensor_tensor(out=blur[:], in0=spad[:, t:t + L], scalar=g[:, t:t + 1],
                                                       in1=blur[:], op0=ALU.mult, op1=ALU.add)
                    if t < TAPS - 1:
                        link(v)
                v.then_inc(blur_ok, 1)
                dve.wait_ge(blurT_ps, 1)
                nc.vector.tensor_copy(blurT[:], ps[4][:, 0:2 * P]).then_inc(blurT_sb, 1)
                dve.wait_ge(blur_ok, 1)
                nc.vector.tensor_copy(at0[:, 0:1], blur[:, 0:1]).then_inc(at0_ok, 1)
                dve.wait_ge(V_ps, 2)
                nc.vector.tensor_copy(at0[:, 1:2], ps[7][:, 0:1]).then_inc(at0_ok, 1)
                dve.wait_ge(mean_ps, 1)
                link(nc.vector.tensor_copy(means[:], ps[4][:, 0:2]))
                NC = P + 1
                nc.vector.tensor_scalar(V[:, 0:NC], ps[5][:, 0:NC], means[:, 0:1], None, ALU.subtract)
                nc.vector.tensor_copy(V[:, NC:L], ps[5][:, NC:L])
                nc.vector.tensor_scalar(QV[:, 0:NC], ps[6][:, 0:NC], means[:, 0:1], None, ALU.subtract)
                nc.vector.tensor_copy(QV[:, NC:L], ps[6][:, NC:L])
                link(nc.vector.tensor_scalar(qy[:, 0:NC], ps[6][:, 0:NC], means[:, 1:2], None, ALU.subtract))
                nc.vector.tensor_tensor(V[:], V[:], V[:], ALU.mult)
                nc.vector.tensor_tensor(QV[:], QV[:], QV[:], ALU.mult)
                link(nc.vector.tensor_tensor(qy[:, 0:NC], qy[:, 0:NC], qy[:, 0:NC], ALU.mult))
                for m, z in enumerate((V, QV)):
                    nc.vector.tensor_reduce(tot[:, 4 * m:4 * m + 1], z[:, 1:P], AX.X, ALU.add)
                    nc.vector.tensor_reduce(tot[:, 4 * m + 1:4 * m + 2], z[:, NC:L], AX.X, ALU.add)
                    link(nc.vector.tensor_tensor(tot[:, 4 * m + 2:4 * m + 3], z[:, 0:1], z[:, P:NC], ALU.add))
                for m in range(2):
                    link(nc.vector.tensor_tensor(tot[:, 4 * m:4 * m + 1], tot[:, 4 * m:4 * m + 1],
                                                 tot[:, 4 * m + 1:4 * m + 2], ALU.subtract))
                    link(nc.vector.scalar_tensor_tensor(out=tot[:, 4 * m + 3:4 * m + 4], in0=tot[:, 4 * m:4 * m + 1],
                                                        scalar=2.0, in1=tot[:, 4 * m + 2:4 * m + 3],
                                                        op0=ALU.mult, op1=ALU.add))
                link(nc.vector.tensor_tensor(gs[:, 6:7], tot[:, 3:4], tot[:, 7:8], ALU.mult))
                link(nc.vector.tensor_scalar(gs[:, 6:7], gs[:, 6:7], 0.001, None, ALU.add))
                link(nc.vector.reciprocal(gs[:, 7:8], gs[:, 6:7]))
                nc.vector.tensor_tensor(V[:, 1:P], V[:, 1:P], V[:, NC:L], ALU.add)
                link(nc.vector.tensor_tensor(qy[:, 1:P], qy[:, 1:P], QV[:, NC:L], ALU.add))
                nc.vector.tensor_scalar(V[:, 0:NC], V[:, 0:NC], gs[:, 7:8], None, ALU.mult)
                link(nc.vector.tensor_scalar(qy[:, 0:NC], qy[:, 0:NC], gs[:, 7:8], None, ALU.mult))
                nc.vector.tensor_tensor(w[:], V[:, 0:NC], qy[:, 0:NC], ALU.mult).then_inc(prod_ok, 1)
                dve.wait_ge(th_ok, 1)
                link(nc.vector.tensor_scalar(half[:], w[:], 1.0, None, ALU.add))
                link(nc.vector.reciprocal(V[:, 0:NC], half[:]))
                nc.vector.scalar_tensor_tensor(out=w[:], in0=w[:], scalar=2.0, in1=V[:, 0:NC],
                                               op0=ALU.mult, op1=ALU.mult).then_inc(w_ok, 1)
                dve.wait_ge(w_ok, 1)
                nc.vector.tensor_copy(w_hi[:, 0:1], w[:, P:P + 1]).then_inc(w_ok, 1)
                nc.vector.tensor_copy(w_hi[:, 1:P], w[:, 1:P]).then_inc(w_ok, 1)
                dve.wait_ge(wT_ps, 1)
                nc.vector.tensor_copy(wT[:, 0], ps[3][:, 0:P]).then_inc(wT_sb, 1)
                nc.vector.tensor_copy(wT[:, 1], ps[3][:, P:2 * P]).then_inc(wT_sb, 1)

                dve.wait_ge(qr_sb, 1)
                dve.wait_ge(wT_sb, 2)
                dve.wait_ge(D_sb, B)
                with dve.Fori(0, B) as b:
                    for pr in range(NPAIR + 1):
                        if pr < NPAIR:
                            dve.wait_ge(y_ps, at(b, 8, 2 * pr + 2))
                            for kt in range(NT):
                                for j in range(2):
                                    e = nc.vector.tensor_scalar(
                                        E[:, pr % 2, kt, j, :], D[:, bass.ds(b, 1), kt, :],
                                        wT[:, kt, 2 * pr + j, bass.ds(b, 1)], QR[:, kt, bass.ds(b, 1)],
                                        ALU.mult, ALU.add)
                            e.then_inc(E_ok, 1)
                        pr -= 1
                        if pr < 0:
                            continue
                        for lt in range(NT):
                            slot = 2 * (pr % 2) + lt
                            dve.wait_ge(abs_ok, at(b, 8, 2 * pr + lt + 1) + 4)
                            nc.vector.scalar_tensor_tensor(
                                out=o[:, slot], in0=o[:, slot], scalar=1.0,
                                in1=xT[:, bass.ds(b, 1), lt, :].broadcast_to([P, 2, C]),
                                op0=ALU.mult, op1=ALU.add,
                                accum_out=sums[:, lt, bass.ds(b * NPAIR + pr, 1)]).then_inc(o_ok, 1)
                dve.wait_ge(o_free, 4 + 8 * B)
                N = float(B * C * KN)
                nc.vector.tensor_reduce(st[:, 0, :], sums[:], AX.X, ALU.add)
                link(nc.vector.tensor_reduce(st[:, 1, :], squares[:], AX.X, ALU.add))
                nc.vector.tensor_scalar(st[:, 0, :], st[:, 0, :], 1.0 / N, None, ALU.mult)
                link(nc.vector.tensor_scalar(st[:, 1, :], st[:, 1, :], 1.0 / N, BN_EPS, ALU.mult, ALU.add))
                link(nc.vector.tensor_tensor(st[:, 2, :], st[:, 0, :], st[:, 0, :], ALU.mult))
                nc.vector.tensor_tensor(st[:, 3, :], st[:, 1, :], st[:, 2, :], ALU.subtract).then_inc(var_ok, 1)
                dve.wait_ge(rstd_ok, 1)
                nc.vector.tensor_tensor(st[:, 5, :], st[:, 4, :], gamma[:], ALU.mult).then_inc(bn_ok, 1)
                dve.wait_ge(bn_ok, 1)
                link(nc.vector.tensor_tensor(st[:, 7, :], st[:, 0, :], st[:, 5, :], ALU.mult))
                nc.vector.tensor_tensor(st[:, 6, :], beta[:], st[:, 7, :], ALU.subtract).then_inc(bn_ok, 1)
                for lt in range(NT):
                    nc.vector.tensor_scalar(qg[:, lt, :], qT[:, lt, :], st[:, 5, lt:lt + 1], None, ALU.mult)
                dve.wait_ge(bn_ps, 1)
                nc.vector.tensor_copy(RG[:], ps[4][:, 0:L])
                nc.vector.tensor_copy(BP[:], ps[5][:, 0:L])
                dve.wait_ge(weights_in, 16 * len(layer1))
                nc.vector.tensor_scalar(b_guh[:], b_gu[:], 0.5, None, ALU.mult)
                nc.vector.tensor_scalar(b_min[:, 0:L], b_min[:, 0:L], 0.25, None, ALU.mult)

        with ExitStack() as second_ctx:
            def sb2(name, shape, dt=F32):
                return second_ctx.enter_context(nc.sbuf_tensor(name, shape, dt))

            def sem2(name):
                return second_ctx.enter_context(nc.semaphore(name))

            rope_cos = sb2("rope_cos", [P, NT, 2 * L])
            rope_sin = sb2("rope_sin", [P, NT, 2 * L])
            x2 = sb2("x2", [P, NT, L])
            src = sb2("src", [P, NT, L])
            E2 = sb2("E2", [P, 4, NT, C])
            o2 = sb2("o2", [P, KN, NT, L])
            dead = sb2("dead", [P, NT, L])
            deadA = sb2("deadA", [P, NT, L])
            qgs = sb2("qgs", [P, NT])
            QGB = sb2("QGB", [P, L])
            score = sb2("score", [P, NT, KN])
            smax = sb2("smax", [P, NT])
            ssum = sb2("ssum", [P, NT])
            srec = sb2("srec", [P, NT])
            tok0 = sb2("tok0", [P, NT, L])
            tok0b = sb2("tok0b", [P, NT, L])
            tok1 = sb2("tok1", [P, NT, L])
            tok2 = sb2("tok2", [P, NT, L])
            tok2b = sb2("tok2b", [P, NT, L])
            X = sb2("X", [P, NT, L])
            XT = sb2("XT", [P, NT, C])
            srcT = sb2("srcT", [P, NT, C])
            tok1T = sb2("tok1T", [P, NT, C])
            updT = sb2("updT", [P, NT, C])
            upd = sb2("upd", [P, NT, L])
            z = sb2("z", [P, NT, L])
            res = sb2("res", [P, NT, L])
            ss = sb2("ss", [P, 4, NT])
            ms = sb2("ms", [P, 4, NT])
            rms_eps = sb2("rms_eps", [P, NT])
            rstd = sb2("rstd", [P, 4, NT])
            rq = sb2("rq", [P, NT])
            mobv = sb2("mobv", [P, L])
            QK = o2[:, 0:2].rearrange("p t s l -> p t (s l)")
            QKr = o2[:, 2:4].rearrange("p t s l -> p t (s l)")
            QP = [sb2(f"QP{a}", [P, NT, 2 * H, HP]) for a in range(2)]
            VP = [sb2(f"VP{a}", [P, NT, H, VW]) for a in range(2)]
            QKT = sb2("QKT", [P, 4, 2 * C])
            nmax = sb2("nmax", [P, 4, NT])
            Pr = sb2("Pr", [P, 2, NT, C])
            PrT = sb2("PrT", [P, 2, NT, C])
            orec = sb2("orec", [P, 2, NT * 8])
            O = sb2("O", [P, NT, L])
            OT = sb2("OT", [P, NT, C])
            th = sb2("th", [P, 2, C])
            val = sb2("val", [P, 2, C])
            hid = o2[:, :, 0, :]

            rope_in, x2_in, src_in, out_done = sem2("rope_in"), sem2("x2_in"), sem2("src_in"), sem2("out_done")
            pads_ok, qgs_ok, QGB_ps, QGB_ok = sem2("pads_ok"), sem2("qgs_ok"), sem2("QGB_ps"), sem2("QGB_ok")
            E2_ok, y2_ps, abs2_ok, o2_ok = sem2("E2_ok"), sem2("y2_ps"), sem2("abs2_ok"), sem2("o2_ok")
            score_ok, sexp_ok, tok0_ok = sem2("score_ok"), sem2("sexp_ok"), sem2("tok0_ok")
            step2 = sem2("step2")
            poolstep = sem2("poolstep")
            ss_ok = [sem2(f"ss_ok{i}") for i in range(4)]
            rstd_ok2 = [sem2(f"rstd_ok2_{i}") for i in range(4)]
            kb_ok, mobv_ok, tok0b_ok, tok2b_ok = sem2("kb_ok"), sem2("mobv_ok"), sem2("tok0b_ok"), sem2("tok2b_ok")
            srcT_ps, srcT_ok, kv_ps, kv_ok = sem2("srcT_ps"), sem2("srcT_ok"), sem2("kv_ps"), sem2("kv_ok")
            X1_ok, X1T_ps, X1T_ok = sem2("X1_ok"), sem2("X1T_ps"), sem2("X1T_ok")
            qkv_ps, qk_ok, v_ok, rsin_ok, qp_ok = sem2("qkv_ps"), sem2("qk_ok"), sem2("v_ok"), sem2("rsin_ok"), sem2("qp_ok")
            QKT_ps, QKT_ok = sem2("QKT_ps"), sem2("QKT_ok")
            S_ps, max_ok, Pr_ok, PrT_ps, PrT_ok, O_ps = (sem2(n) for n in
                ("S_ps", "max_ok", "Pr_ok", "PrT_ps", "PrT_ok", "O_ps"))
            dot_ok = sem2("dot_ok")
            rcos_ok, div_ok, prod_ok2 = sem2("rcos_ok"), sem2("div_ok"), sem2("prod_ok2")
            O_ok, OT_ps, OT_ok = sem2("O_ok"), sem2("OT_ps"), sem2("OT_ok")
            att_ps, tok1_ok, tok1T_ps, tok1T_ok = sem2("att_ps"), sem2("tok1_ok"), sem2("tok1T_ps"), sem2("tok1T_ok")
            X2T_ok, cq_ps, cq_ok = sem2("X2T_ok"), sem2("cq_ps"), sem2("cq_ok")
            upd_ps, upd_ok, updT_ps, updT_ok = sem2("upd_ps"), sem2("upd_ok"), sem2("updT_ps"), sem2("updT_ok")
            gate_ps, z_ok2, zt_ok, tok2_ok = sem2("gate_ps"), sem2("z_ok2"), sem2("zt_ok"), sem2("tok2_ok")
            X3_ok, X3T_ps, X3T_ok = sem2("X3_ok"), sem2("X3T_ps"), sem2("X3T_ok")
            gu_ps, act_ok, hid_ok, down_ps, res_ok = (sem2(n) for n in ("gu_ps", "act_ok", "hid_ok", "down_ps", "res_ok"))
            NH = 2 * H

            block = second_ctx.enter_context(nc.Block())

            @block.sync
            def _(sp):
                sp.dma_start(rope_cos[:], tiles(d["t_cos"])).then_inc(rope_in, 16)
                sp.dma_start(rope_sin[:], tiles(d["t_sin"])).then_inc(rope_in, 16)
                sp.dma_start(x2[:], tiles(d["x"][0])).then_inc(x2_in, 16)
                sp.dma_start(src[:], tiles(d["fside"][0])).then_inc(src_in, 16)
                with sp.Fori(0, B - 1) as b:
                    sp.wait_ge(o2_ok, at(b, KN, KN))
                    sp.dma_start(x2[:], tiles(d["x"][b + 1])).then_inc(x2_in, 16)
                    sp.wait_ge(kv_ok, at(b, 2, 2))
                    sp.dma_start(src[:], tiles(d["fside"][b + 1])).then_inc(src_in, 16)

            @block.gpsimd
            def _(pool):
                for a in range(2):
                    nc.gpsimd.memset(QP[a][:], 0.0).then_inc(poolstep, 1)
                    nc.gpsimd.memset(VP[a][:, :, :, ONE_COL:VW], 1.0).then_inc(pads_ok, 1)
                nc.gpsimd.memset(rms_eps[:], RMS_EPS).then_inc(pads_ok, 1)
                pool.wait_ge(poolstep, 2)
                for a in range(2):
                    nc.gpsimd.memset(QP[a][:, :, 0:H, ONE_COL:ONE_COL + 1], 1.0).then_inc(pads_ok, 1)

                def mean_to_rstd(b, n):
                    pool.wait_ge(ss_ok[n], b * 2 + 2)
                    nc.gpsimd.tensor_tensor(ms[:, n], ss[:, n], rms_eps[:], ALU.add).then_inc(poolstep, 1)
                    pool.wait_ge(poolstep, at(b, 4, n + 1) + 2)
                    nc.gpsimd.tensor_tensor(rstd[:, n], ms[:, n], mhalf[:], ALU.pow).then_inc(rstd_ok2[n], 1)

                with pool.Fori(0, B) as b:
                    pool.wait_ge(x2_in, at(b, 16, 16))
                    for i in range(KN):
                        pool.wait_ge(abs2_ok, at(b, KN, i + 1))
                        nc.gpsimd.tensor_tensor(o2[:, i], o2[:, i], x2[:], ALU.add).then_inc(o2_ok, 1)
                    pool.wait_ge(pads_ok, 5)
                    for a in range(2):
                        for t in range(NT):
                            c = nc.gpsimd.tensor_copy(
                                QP[a][:, t, H:2 * H, ONE_COL:ONE_COL + 1],
                                keybias[:, t, bass.ds(b, 1)].unsqueeze(1).broadcast_to([P, H, 1]))
                    c.then_inc(kb_ok, 1)
                    mean_to_rstd(b, 0)
                    mean_to_rstd(b, 1)
                    pool.wait_ge(tok0_ok, b + 1)
                    nc.gpsimd.tensor_tensor(tok0b[:], tok0[:], b_out[:].unsqueeze(1).broadcast_to([P, NT, L]),
                                            ALU.add).then_inc(tok0b_ok, 1)
                    pool.wait_ge(rope_in, 32)
                    for t in range(NT):
                        pool.wait_ge(qk_ok, at(b, 2, t + 1))
                        for e in range(2):
                            qk = QK[:, t, :].rearrange("p (n e) -> p n e", e=2)
                            r = nc.gpsimd.tensor_tensor(
                                QKr[:, t, :].rearrange("p (n e) -> p n e", e=2)[:, :, e], qk[:, :, 1 - e],
                                rope_sin[:, t, :].rearrange("p (n e) -> p n e", e=2)[:, :, e], ALU.mult)
                        r.then_inc(rsin_ok, 1)
                    mean_to_rstd(b, 2)
                    mean_to_rstd(b, 3)
                    pool.wait_ge(tok2_ok, b + 1)
                    nc.gpsimd.tensor_tensor(tok2b[:], tok2[:], b_down[:].unsqueeze(1).broadcast_to([P, NT, L]),
                                            ALU.add).then_inc(tok2b_ok, 1)

            @block.scalar
            def _(act):
                def squares_of(b, n, t):
                    for tt in range(NT):
                        nc.scalar.activation(deadA[:, tt], t[:, tt, :], ACT.Square, scale=L ** -0.5,
                                             accum_out=ss[:, n, tt:tt + 1]).then_inc(ss_ok[n], 1)

                def heads_T_out(b, a):
                    for g4 in range(4):
                        act.wait_ge(QKT_ps, at(b, 8, 4 * a + g4 + 1))
                        nc.scalar.activation(QKT[:, g4, :], ps[4 + g4 % 2][:], ACT.Copy).then_inc(QKT_ok, 1)

                def exps(b, a):
                    for h in range(H):
                        act.wait_ge(max_ok, at(b, NH, a * H + h + 1))
                        if h >= 2:
                            act.wait_ge(PrT_ps, at(b, NH, a * H + h - 1))
                        for qt in range(NT):
                            e = nc.scalar.activation(Pr[:, h % 2, qt, :], ps[h % 4][:, qt * C:(qt + 1) * C], ACT.Exp,
                                                     bias=nmax[:, h % 4, qt:qt + 1])
                        e.then_inc(Pr_ok, 1)

                with act.Fori(0, B) as b:
                    for i in range(-4, KN):
                        if i >= 0:
                            act.wait_ge(y2_ps, at(b, KN, i + 1))
                            nc.scalar.activation(o2[:, i], ps[i % 4][:], ACT.Abs).then_inc(abs2_ok, 1)
                        k_ = i + 4
                        if k_ < KN:
                            for kt in range(NT):
                                e = nc.scalar.activation(E2[:, k_ % 4, kt, :], D[:, bass.ds(b, 1), kt, :], ACT.Identity,
                                                         scale=wT[:, kt, k_, bass.ds(b, 1)], bias=QR[:, kt, bass.ds(b, 1)])
                            e.then_inc(E2_ok, 1)
                    act.wait_ge(src_in, at(b, 16, 16))
                    squares_of(b, 0, src)
                    act.wait_ge(srcT_ps, b + 1)
                    for ft in range(NT):
                        a_ = nc.scalar.activation(srcT[:, ft, :], ps[7][:, ft * C:(ft + 1) * C], ACT.Copy,
                                                  scale=n_s[:, ft:ft + 1])
                    a_.then_inc(srcT_ok, 1)
                    act.wait_ge(score_ok, b + 1)
                    for ct in range(NT):
                        a_ = nc.scalar.activation(score[:, ct, :], score[:, ct, :], ACT.Exp, bias=smax[:, ct:ct + 1],
                                                  accum_out=ssum[:, ct:ct + 1])
                    a_.then_inc(sexp_ok, 1)
                    act.wait_ge(tok0_ok, b + 1)
                    squares_of(b, 1, tok0)
                    act.wait_ge(X1T_ps, b + 1)
                    for ft in range(NT):
                        a_ = nc.scalar.activation(XT[:, ft, :], ps[7][:, ft * C:(ft + 1) * C], ACT.Identity,
                                                  scale=filmG[:, ft, bass.ds(b, 1)], bias=filmS[:, ft, bass.ds(b, 1)])
                    a_.then_inc(X1T_ok, 1)
                    heads_T_out(b, 0)
                    exps(b, 0)
                    act.wait_ge(OT_ps, at(b, 2, 1))
                    nc.scalar.activation(OT[:], ps[7][:], ACT.Copy).then_inc(OT_ok, 1)
                    act.wait_ge(tok1_ok, b + 1)
                    squares_of(b, 2, tok1)
                    act.wait_ge(tok1T_ps, b + 1)
                    nc.scalar.activation(tok1T[:], ps[7][:], ACT.Copy).then_inc(tok1T_ok, 1)
                    heads_T_out(b, 1)
                    exps(b, 1)
                    act.wait_ge(OT_ps, at(b, 2, 2))
                    nc.scalar.activation(OT[:], ps[7][:], ACT.Copy).then_inc(OT_ok, 1)
                    act.wait_ge(updT_ps, b + 1)
                    nc.scalar.activation(updT[:], ps[7][:], ACT.Copy).then_inc(updT_ok, 1)
                    act.wait_ge(z_ok2, b + 1)
                    nc.scalar.activation(z[:], z[:], ACT.Tanh, scale=0.5).then_inc(zt_ok, 1)
                    act.wait_ge(tok2_ok, b + 1)
                    squares_of(b, 3, tok2)
                    act.wait_ge(X3T_ps, b + 1)
                    for ft in range(NT):
                        a_ = nc.scalar.activation(XT[:, ft, :], ps[7][:, ft * C:(ft + 1) * C], ACT.Copy,
                                                  scale=n_ffn[:, ft:ft + 1])
                    a_.then_inc(X3T_ok, 1)
                    for m in range(MT):
                        act.wait_ge(gu_ps, at(b, MT, m + 1))
                        if m >= 2:
                            act.wait_ge(hid_ok, at(b, MT, m - 1))
                        nc.scalar.activation(th[:, m % 2, :], ps[m % 4][:, 0:C], ACT.Tanh, scale=0.5,
                                             bias=b_guh[:, m:m + 1])
                        nc.scalar.activation(val[:, m % 2, :], ps[m % 4][:, C:2 * C], ACT.Identity, scale=0.5,
                                             bias=b_guh[:, MT + m:MT + m + 1]).then_inc(act_ok, 1)
                    act.wait_ge(res_ok, b + 1)
                    act.dma_start(tiles(out[b]), res[:]).then_inc(out_done, 16)
                act.wait_ge(out_done, 16 * B + 16)

            @block.tensor
            def _(pe):
                def turn(bank, t, done):
                    for ft in range(NT):
                        for tt in range(NT):
                            m = nc.tensor.transpose(ps[bank][:, ft * C + tt * P:ft * C + (tt + 1) * P],
                                                    t[:, tt, ft * P:(ft + 1) * P], eye[:])
                    m.then_inc(done, 1)

                def project(bank, xT, wt, lo, n, done, col=0, tts=(0, 1), stride=L, first=0, kts=NT):
                    for tt in tts:
                        for kt in range(kts):
                            m = nc.tensor.matmul(ps[bank][:, col:col + n], xT[:, kt, tt * P:(tt + 1) * P],
                                                 wt[:, kt, lo:lo + n], start=(kt == 0), stop=(kt == kts - 1))
                        col += stride
                    m.then_inc(done, 1)

                def turn_heads(b, a):
                    for g4 in range(4):
                        if g4 >= 2:
                            pe.wait_ge(QKT_ok, at(b, 8, 4 * a + g4 - 1))
                        for part in range(2):
                            for tt in range(NT):
                                h0 = part * H + 4 * g4
                                m = nc.tensor.transpose(
                                    ps[4 + g4 % 2][:, part * C + tt * P:part * C + (tt + 1) * P],
                                    QP[a][:, tt, h0:h0 + 4, :].rearrange("p h e -> p (h e)"), eye[:])
                        m.then_inc(QKT_ps, 1)

                def attention(b, a):
                    pe.wait_ge(QKT_ok, at(b, 8, 4 * a + 4))
                    for n in range(H + 3):
                        if n < H:
                            g4, j = n // 4, n % 4
                            if n >= 4:
                                pe.wait_ge(Pr_ok, at(b, NH, a * H + n - 3))
                            for qt in range(NT):
                                m = nc.tensor.matmul(ps[j][:, qt * C:(qt + 1) * C],
                                                     QKT[j * HP:(j + 1) * HP, g4, qt * P:(qt + 1) * P],
                                                     QKT[j * HP:(j + 1) * HP, g4, C:2 * C], start=True, stop=True)
                            m.then_inc(S_ps, 1)
                        h = n - 2
                        if 0 <= h < H:
                            pe.wait_ge(Pr_ok, at(b, NH, a * H + h + 1))
                            if h >= 2:
                                pe.wait_ge(PrT_ok, at(b, NH, a * H + h - 1))
                            for kt in range(NT):
                                for qt in range(NT):
                                    m = nc.tensor.transpose(ps[4 + h % 2][:, kt * C + qt * P:kt * C + (qt + 1) * P],
                                                            Pr[:, h % 2, qt, kt * P:(kt + 1) * P], eye[:])
                            m.then_inc(PrT_ps, 1)
                        h = n - 3
                        if h >= 0:
                            pe.wait_ge(PrT_ok, at(b, NH, a * H + h + 1))
                            if h == 8:
                                pe.wait_ge(O_ok, at(b, 4, 2 * a + 1))
                            for qt in range(NT):
                                for kt in range(NT):
                                    c0 = (qt * 8 + h % 8) * HP
                                    m = nc.tensor.matmul(ps[6][:, c0:c0 + VW], PrT[:, h % 2, kt, qt * P:(qt + 1) * P],
                                                         VP[a][:, kt, h, :], start=(kt == 0), stop=(kt == 1))
                            m.then_inc(O_ps, 1)

                with pe.Fori(0, B) as b:
                    pe.wait_ge(qgs_ok, b + 1)
                    for lt in range(NT):
                        m = nc.tensor.matmul(ps[4][:, lt * P:(lt + 1) * P], qgs[:, lt:lt + 1].broadcast_to([P, P]),
                                             eye[:], start=True, stop=True)
                    m.then_inc(QGB_ps, 1)
                    for i in range(KN):
                        pe.wait_ge(E2_ok, at(b, KN, i + 1))
                        if i >= 4:
                            pe.wait_ge(abs2_ok, at(b, KN, i - 3))
                        for ct in range(NT):
                            for kt in range(NT):
                                m = nc.tensor.matmul(ps[i % 4][:, ct * L:(ct + 1) * L],
                                                     E2[:, i % 4, kt, ct * P:(ct + 1) * P], Fm[:, kt, :],
                                                     start=(kt == 0), stop=(kt == 1))
                        m.then_inc(y2_ps, 1)
                    pe.wait_ge(src_in, at(b, 16, 16))
                    turn(7, src, srcT_ps)
                    pe.wait_ge(srcT_ok, b + 1)
                    project(5, srcT, w_min, L, 2 * L, kv_ps, tts=(0,))
                    project(6, srcT, w_min, L, 2 * L, kv_ps, tts=(1,))
                    pe.wait_ge(X1_ok, b + 1)
                    turn(7, X, X1T_ps)
                    pe.wait_ge(X1T_ok, b + 1)
                    for tt in range(NT):
                        project(2 * tt, XT, w_qkv, 0, 2 * L, qkv_ps, tts=(tt,))
                        project(2 * tt + 1, XT, w_qkv, 2 * L, L, qkv_ps, tts=(tt,))
                    pe.wait_ge(qp_ok, at(b, 2, 2))
                    pe.wait_ge(kb_ok, b + 1)
                    pe.wait_ge(v_ok, at(b, 2, 2))
                    pe.wait_ge(kv_ok, at(b, 2, 2))
                    turn_heads(b, 0)
                    attention(b, 0)
                    pe.wait_ge(O_ok, at(b, 4, 2))
                    turn(7, O, OT_ps)
                    pe.wait_ge(OT_ok, at(b, 2, 1))
                    project(0, OT, w_out, 0, L, att_ps)
                    pe.wait_ge(tok1_ok, b + 1)
                    turn(7, tok1, tok1T_ps)
                    pe.wait_ge(X2T_ok, b + 1)
                    project(0, XT, w_min, 0, L, cq_ps)
                    pe.wait_ge(cq_ok, b + 1)
                    turn_heads(b, 1)
                    attention(b, 1)
                    pe.wait_ge(O_ok, at(b, 4, 4))
                    turn(7, O, OT_ps)
                    pe.wait_ge(OT_ok, at(b, 2, 2))
                    project(0, OT, w_mout, 0, L, upd_ps)
                    pe.wait_ge(upd_ok, b + 1)
                    turn(7, upd, updT_ps)
                    pe.wait_ge(updT_ok, b + 1)
                    for tt in range(NT):
                        for kt in range(4):
                            xT_ = tok1T if kt < 2 else updT
                            m = nc.tensor.matmul(ps[0][:, tt * L:(tt + 1) * L], xT_[:, kt % 2, tt * P:(tt + 1) * P],
                                                 w_gate[:, kt, :], start=(kt == 0), stop=(kt == 3))
                    m.then_inc(gate_ps, 1)
                    pe.wait_ge(X3_ok, b + 1)
                    turn(7, X, X3T_ps)
                    pe.wait_ge(X3T_ok, b + 1)
                    for m_ in range(MT + 2):
                        if m_ < MT:
                            if m_ >= 4:
                                pe.wait_ge(hid_ok, at(b, MT, m_ - 3))
                            for part in range(2):
                                for kt in range(NT):
                                    c0 = part * HID + m_ * P
                                    m = nc.tensor.matmul(ps[m_ % 4][:, part * C:(part + 1) * C],
                                                         w_gu[:, kt, c0:c0 + P], XT[:, kt, :],
                                                         start=(kt == 0), stop=(kt == 1))
                            m.then_inc(gu_ps, 1)
                        k_ = m_ - 2
                        if k_ >= 0:
                            pe.wait_ge(hid_ok, at(b, MT, k_ + 1))
                            for tt in range(NT):
                                m = nc.tensor.matmul(ps[6 + tt][:, 0:L], hid[:, k_, tt * P:(tt + 1) * P],
                                                     w_down[:, k_, :], start=(k_ == 0), stop=(k_ == MT - 1))
                    m.then_inc(down_ps, 1)

            @block.vector
            def _(dve):
                LINKS = 12

                def attention(b, a):
                    for n in range(H + 4):
                        if n < H:
                            dve.wait_ge(S_ps, at(b, NH, a * H + n + 1))
                            nc.vector.tensor_reduce(nmax[:, n % 4, :], ps[n % 4][:].rearrange("p (t k) -> p t k", t=NT),
                                                    AX.X, ALU.max, negate=True).then_inc(max_ok, 1)
                        h = n - 2
                        if 0 <= h < H:
                            dve.wait_ge(PrT_ps, at(b, NH, a * H + h + 1))
                            if h >= 2:
                                dve.wait_ge(O_ps, at(b, NH, a * H + h - 1))
                            nc.vector.tensor_copy(PrT[:, h % 2], ps[4 + h % 2][:]).then_inc(PrT_ok, 1)
                        h = n - 4
                        if h == 7 or h == 15:
                            hh = h // 8
                            dve.wait_ge(O_ps, at(b, NH, a * H + h + 1))
                            ov = ps[6][:].rearrange("p (n e) -> p n e", e=HP)
                            nc.vector.reciprocal(orec[:, hh, :], ov[:, :, ONE_COL]).then_inc(div_ok, 1)
                            dve.wait_ge(div_ok, at(b, 4, 2 * a + hh + 1))
                            nc.vector.tensor_tensor(
                                O[:, :, hh * P:(hh + 1) * P].rearrange("p t (h e) -> p t h e", e=HD),
                                ps[6][:].rearrange("p (t h e) -> p t h e", t=NT, e=HP)[:, :, :, 0:HD],
                                orec[:, hh, :].rearrange("p (t h) -> p t h", t=NT).unsqueeze(3).broadcast_to([P, NT, 8, HD]),
                                ALU.mult).then_inc(O_ok, 1)

                dve.sem_inc(out_done, 16)
                with dve.Fori(0, B) as b:
                    n_link = [0]

                    def link(ins):
                        n_link[0] += 1
                        ins.then_inc(step2, 1)
                        dve.wait_ge(step2, at(b, LINKS, n_link[0]))

                    nc.vector.tensor_copy(qgs[:], qg[:, :, bass.ds(b, 1)]).then_inc(qgs_ok, 1)
                    nc.vector.tensor_scalar(mobv[:], b_mout[:], vrow[:, bass.ds(b, 1)], None, ALU.mult).then_inc(mobv_ok, 1)
                    dve.wait_ge(QGB_ps, b + 1)
                    nc.vector.tensor_copy(QGB[:], ps[4][:, 0:L]).then_inc(QGB_ok, 1)
                    dve.wait_ge(QGB_ok, b + 1)
                    for i in range(KN + 1):
                        if i >= 1:
                            dve.wait_ge(o2_ok, at(b, KN, i))
                            for ct in range(NT):
                                if i >= 2:
                                    dve.wait_ge(dot_ok, at(b, NT * KN, NT * (i - 2) + ct + 1))
                                nc.vector.tensor_tensor_reduce(dead[:, ct], o2[:, i - 1, ct, :], QGB[:], 1.0, 0.0,
                                                               ALU.mult, ALU.add,
                                                               score[:, ct, i - 1:i]).then_inc(dot_ok, 1)
                    dve.wait_ge(dot_ok, at(b, NT * KN, NT * KN))
                    nc.vector.tensor_reduce(smax[:], score[:], AX.X, ALU.max, negate=True).then_inc(score_ok, 1)
                    dve.wait_ge(sexp_ok, b + 1)
                    link(nc.vector.reciprocal(srec[:], ssum[:]))
                    for i in range(KN):
                        for ct in range(NT):
                            if i == 0:
                                v = nc.vector.tensor_scalar(tok0[:, ct, :], o2[:, 0, ct, :], score[:, ct, 0:1], None, ALU.mult)
                            else:
                                v = nc.vector.scalar_tensor_tensor(out=tok0[:, ct, :], in0=o2[:, i, ct, :],
                                                                   scalar=score[:, ct, i:i + 1], in1=tok0[:, ct, :],
                                                                   op0=ALU.mult, op1=ALU.add)
                        link(v)
                    for ct in range(NT):
                        v = nc.vector.scalar_tensor_tensor(out=tok0[:, ct, :], in0=tok0[:, ct, :],
                                                           scalar=srec[:, ct:ct + 1], in1=RG[:],
                                                           op0=ALU.mult, op1=ALU.mult)
                    link(v)
                    nc.vector.tensor_tensor(tok0[:], tok0[:], BP[:].unsqueeze(1).broadcast_to([P, NT, L]),
                                            ALU.add).then_inc(tok0_ok, 1)

                    dve.wait_ge(rstd_ok2[0], b + 1)
                    dve.wait_ge(pads_ok, 5)
                    for tt in range(NT):
                        dve.wait_ge(kv_ps, at(b, 2, tt + 1))
                        bank = ps[5 + tt]
                        nc.vector.scalar_tensor_tensor(
                            out=QP[1][:, tt, H:2 * H, 0:HD], in0=bank[:, 0:L].rearrange("p (h e) -> p h e", e=HD),
                            scalar=rstd[:, 0, tt:tt + 1], in1=b_min[:, L:2 * L].rearrange("p (h e) -> p h e", e=HD),
                            op0=ALU.mult, op1=ALU.add)
                        nc.vector.scalar_tensor_tensor(
                            out=VP[1][:, tt, :, 0:HD], in0=bank[:, L:2 * L].rearrange("p (h e) -> p h e", e=HD),
                            scalar=rstd[:, 0, tt:tt + 1], in1=b_min[:, 2 * L:3 * L].rearrange("p (h e) -> p h e", e=HD),
                            op0=ALU.mult, op1=ALU.add).then_inc(kv_ok, 1)

                    dve.wait_ge(rstd_ok2[1], b + 1)
                    dve.wait_ge(tok0_ok, b + 1)
                    for tt in range(NT):
                        v = nc.vector.tensor_scalar(X[:, tt, :], tok0[:, tt, :], rstd[:, 1, tt:tt + 1], None, ALU.mult)
                    v.then_inc(X1_ok, 1)
                    for tt in range(NT):
                        dve.wait_ge(qkv_ps, at(b, 4, 2 * tt + 1))
                        nc.vector.tensor_tensor(QK[:, tt, :], ps[2 * tt][:], b_qkv[:, 0:2 * L], ALU.add).then_inc(qk_ok, 1)
                        dve.wait_ge(qkv_ps, at(b, 4, 2 * tt + 2))
                        nc.vector.tensor_tensor(VP[0][:, tt, :, 0:HD],
                                                ps[2 * tt + 1][:, 0:L].rearrange("p (h e) -> p h e", e=HD),
                                                b_qkv[:, 2 * L:3 * L].rearrange("p (h e) -> p h e", e=HD),
                                                ALU.add).then_inc(v_ok, 1)
                    dve.wait_ge(rope_in, 32)
                    for tt in range(NT):
                        dve.wait_ge(qk_ok, at(b, 2, tt + 1))
                        dve.wait_ge(rsin_ok, at(b, 2, tt + 1))
                        nc.vector.tensor_tensor(QK[:, tt, :], QK[:, tt, :], rope_cos[:, tt, :], ALU.mult).then_inc(rcos_ok, 1)
                        dve.wait_ge(rcos_ok, at(b, 2, tt + 1))
                        nc.vector.tensor_tensor(QP[0][:, tt, :, 0:HD], QK[:, tt, :].rearrange("p (h e) -> p h e", e=HD),
                                                QKr[:, tt, :].rearrange("p (h e) -> p h e", e=HD),
                                                ALU.add).then_inc(qp_ok, 1)
                    attention(b, 0)
                    dve.wait_ge(tok0b_ok, b + 1)
                    dve.wait_ge(att_ps, b + 1)
                    nc.vector.tensor_tensor(tok1[:], ps[0][:], tok0b[:], ALU.add).then_inc(tok1_ok, 1)

                    dve.wait_ge(tok1T_ok, b + 1)
                    for ft in range(NT):
                        v = nc.vector.tensor_scalar(XT[:, ft, :], tok1T[:, ft, :], n_sq[:, ft:ft + 1], None, ALU.mult)
                    v.then_inc(X2T_ok, 1)
                    dve.wait_ge(rstd_ok2[2], b + 1)
                    link(nc.vector.tensor_scalar(rq[:], rstd[:, 2], HD ** -0.5, None, ALU.mult))
                    dve.wait_ge(cq_ps, b + 1)
                    for tt in range(NT):
                        v = nc.vector.scalar_tensor_tensor(
                            out=QP[1][:, tt, 0:H, 0:HD], in0=ps[0][:, tt * L:(tt + 1) * L].rearrange("p (h e) -> p h e", e=HD),
                            scalar=rq[:, tt:tt + 1], in1=b_min[:, 0:L].rearrange("p (h e) -> p h e", e=HD),
                            op0=ALU.mult, op1=ALU.add)
                    v.then_inc(cq_ok, 1)
                    attention(b, 1)
                    dve.wait_ge(upd_ps, b + 1)
                    dve.wait_ge(mobv_ok, b + 1)
                    for tt in range(NT):
                        v = nc.vector.scalar_tensor_tensor(out=upd[:, tt, :], in0=ps[0][:, tt * L:(tt + 1) * L],
                                                           scalar=vrow[:, bass.ds(b, 1)], in1=mobv[:],
                                                           op0=ALU.mult, op1=ALU.add)
                    v.then_inc(upd_ok, 1)
                    dve.wait_ge(gate_ps, b + 1)
                    nc.vector.tensor_tensor(z[:], ps[0][:].rearrange("p (t l) -> p t l", t=NT),
                                            b_gate[:].unsqueeze(1).broadcast_to([P, NT, L]), ALU.add).then_inc(z_ok2, 1)
                    dve.wait_ge(zt_ok, b + 1)
                    link(nc.vector.scalar_tensor_tensor(out=z[:], in0=z[:], scalar=1.0, in1=upd[:],
                                                        op0=ALU.add, op1=ALU.mult))
                    nc.vector.scalar_tensor_tensor(out=tok2[:], in0=z[:], scalar=0.5, in1=tok1[:],
                                                   op0=ALU.mult, op1=ALU.add).then_inc(tok2_ok, 1)

                    dve.wait_ge(rstd_ok2[3], b + 1)
                    dve.wait_ge(tok2_ok, b + 1)
                    for tt in range(NT):
                        v = nc.vector.tensor_scalar(X[:, tt, :], tok2[:, tt, :], rstd[:, 3, tt:tt + 1], None, ALU.mult)
                    v.then_inc(X3_ok, 1)
                    for m in range(MT):
                        dve.wait_ge(act_ok, at(b, MT, m + 1))
                        nc.vector.scalar_tensor_tensor(out=th[:, m % 2, :], in0=th[:, m % 2, :], scalar=1.0,
                                                       in1=val[:, m % 2, :], op0=ALU.add, op1=ALU.mult).then_inc(prod_ok2, 1)
                        dve.wait_ge(prod_ok2, at(b, MT, m + 1))
                        nc.vector.scalar_tensor_tensor(out=hid[:, m, :], in0=ps[m % 4][:, 0:C], scalar=b_gu[:, m:m + 1],
                                                       in1=th[:, m % 2, :], op0=ALU.add, op1=ALU.mult).then_inc(hid_ok, 1)
                    dve.wait_ge(tok2b_ok, b + 1)
                    dve.wait_ge(down_ps, b + 1)
                    dve.wait_ge(out_done, at(b, 16, 16))
                    for tt in range(NT):
                        v = nc.vector.tensor_tensor(res[:, tt, :], ps[6 + tt][:, 0:L], tok2b[:, tt, :], ALU.add)
                    v.then_inc(res_ok, 1)
                    assert n_link[0] == LINKS, n_link[0]


_PLAIN = {"x": "x", "cond": "cond_1024", "fside": "fside_BxSxS_0", "sigmas": "L0_cond_sigmas",
          "centers": "L0_cond_center_shift", "gamma": "L0_cond_gamma", "beta": "L0_cond_beta",
          "attn_norm_w": "L1_cond_attn_norm_w", "qkv_b": "L1_cond_qkv_b", "out_b": "L1_cond_out_b",
          "film_b": "L1_cond_film_b", "sq_norm_w": "L1_cond_sq_norm_w", "s_norm_w": "L1_cond_s_norm_w",
          "mha_in_b": "L1_cond_mha_in_b", "mha_out_b": "L1_cond_mha_out_b", "gate_b": "L1_cond_gate_b",
          "ffn_norm_w": "L1_cond_ffn_norm_w", "gu_b": "L1_cond_gu_b", "down_b": "L1_cond_down_b"}
_COLUMNS = ("gamma", "beta", "attn_norm_w", "film_b", "gu_b", "sq_norm_w", "s_norm_w", "ffn_norm_w")
_TURNED = {"qkv_wT": "L1_cond_qkv_w", "out_wT": "L1_cond_out_w", "film_wT": "L1_cond_film_w",
           "mha_in_wT": "L1_cond_mha_in_w", "mha_out_wT": "L1_cond_mha_out_w",
           "gate_wT": "L1_cond_gate_w", "gu_wT": "L1_cond_gu_w", "down_wT": "L1_cond_down_w"}


def kernel(**inputs):
    import numpy as _np
    import concourse.bacc as _bacc
    from concourse import mybir as _mybir
    from concourse.bass_utils import run_bass_kernel_spmd as _run

    nc = _bacc.Bacc("TRN2", target_bir_lowering=False, num_devices=1)
    arrays = {n: _np.ascontiguousarray(inputs[s]) for n, s in _PLAIN.items()}
    arrays.update({n: _np.ascontiguousarray(_np.asarray(inputs[s]).T) for n, s in _TURNED.items()})
    for n in _COLUMNS:
        arrays[n] = _np.ascontiguousarray(arrays[n].reshape(-1, P).T)
    arrays["mask"] = _np.ascontiguousarray(inputs["mask_BxS_bk0"])
    arrays.update(shape_tables())
    feed, d = {}, {}
    for n, a in arrays.items():
        feed[f"in_{n}"] = a
        d[n] = nc.dram_tensor(f"in_{n}", a.shape, _mybir.dt.from_np(a.dtype), kind="ExternalInput").ap()
    out = nc.dram_tensor("out_dram", (B, C, L), _mybir.dt.float32, kind="ExternalOutput").ap()
    build(nc, d, out)
    r = _run(nc, [feed], core_ids=[0])
    return r.results[0]["out_dram"]
```

```python
import math
from contextlib import ExitStack

import numpy as np
import concourse.bass as bass
from concourse import mybir

F32 = mybir.dt.float32
U8 = mybir.dt.uint8
ALU = mybir.AluOpType
ACT = mybir.ActivationFunctionType
AX = mybir.AxisListType

P = 128
B = 16
L = 256
C = 256
KN = 8
TAPS = 15
NT = 2
H = 16
HD = 16
HP = 32
HID = 1024
MT = HID // P
NPAIR = KN // 2
BN_EPS = 1e-5
RMS_EPS = 1e-6
NEG = -1e30
ONE_COL, VW = 16, 17


def shape_tables():
    l = np.arange(L)
    F = np.zeros((L, L))
    k = np.arange(P)
    F[:P] = np.cos(2 * np.pi * ((k[:, None] * l[None]) % L) / L) * math.sqrt(2.0 / L)
    F[0] = math.sqrt(1.0 / L)
    F[P] = np.where(l % 2, -1.0, 1.0) * math.sqrt(1.0 / L)
    F[P + 1:] = np.sin(2 * np.pi * ((k[1:, None] * l[None]) % L) / L) * math.sqrt(2.0 / L)
    W = np.zeros((L, L))
    kk = np.arange(P + 1)
    W[:, :P + 1] = np.cos(2 * np.pi * ((l[:, None] * kk[None]) % L) / L)
    W[:, P + 1:] = np.sin(2 * np.pi * ((l[:, None] * kk[None, 1:P]) % L) / L)
    taps = np.broadcast_to(np.linspace(-7.0, 7.0, TAPS), (P, TAPS))
    avg = np.kron(np.eye(KN), np.full((B, B), 1.0 / B))
    pos = np.arange(C, dtype=np.float32)[:, None]
    freq = np.exp(np.arange(0, HD, 2, dtype=np.float32) * np.float32(-math.log(10000.0) / HD))
    ang = (pos * freq[None]).astype(np.float32)
    cos, sin = np.cos(ang), np.sin(ang)
    c16 = np.repeat(cos, 2, axis=1)
    s16 = np.stack((-sin, sin), axis=-1).reshape(C, HD)

    def rope(t):
        return np.concatenate([np.tile(t, (1, H)) * 0.25, np.tile(t, (1, H))], axis=1)

    out = {"t_F": F, "t_FT": F.T, "t_W": W, "t_taps": taps, "t_avg": avg, "t_eye": np.eye(P),
           "t_cos": rope(c16), "t_sin": rope(s16)}
    return {n: np.ascontiguousarray(a.astype(np.float32)) for n, a in out.items()}


def tiles(v):
    return v.rearrange("(t p) n -> p t n", p=P)


def at(b, per, n):
    return b * per + n


def build(nc, d, out):
    with ExitStack() as ctx:
        ps = [ctx.enter_context(nc.psum_tensor(f"bank{i}", [P, 512], F32)) for i in range(8)]

        def sb(name, shape, dt=F32):
            return ctx.enter_context(nc.sbuf_tensor(name, shape, dt))

        def sem(name):
            return ctx.enter_context(nc.semaphore(name))

        D = sb("D", [P, B, NT, C])
        Fm = sb("Fm", [P, NT, L])
        eye = sb("eye", [P, P])
        wT = sb("wT", [P, NT, KN, B])
        QR = sb("QR", [P, NT, B])
        qg = sb("qg", [P, NT, B])
        RG = sb("RG", [P, L])
        BP = sb("BP", [P, L])
        filmG = sb("filmG", [P, NT, B])
        filmS = sb("filmS", [P, NT, B])
        keybias = sb("keybias", [P, NT, B])
        vrow = sb("vrow", [P, B])
        w_qkv = sb("w_qkv", [P, NT, 3 * L])
        w_out = sb("w_out", [P, NT, L])
        w_min = sb("w_min", [P, NT, 3 * L])
        w_mout = sb("w_mout", [P, NT, L])
        w_gate = sb("w_gate", [P, 4, L])
        w_gu = sb("w_gu", [P, NT, 2 * HID])
        w_down = sb("w_down", [P, MT, L])
        b_qkv = sb("b_qkv", [P, 3 * L])
        b_out = sb("b_out", [P, L])
        b_min = sb("b_min", [P, 3 * L])
        b_mout = sb("b_mout", [P, L])
        b_gate = sb("b_gate", [P, L])
        b_gu = sb("b_gu", [P, 2 * MT])
        b_guh = sb("b_guh", [P, 2 * MT])
        b_down = sb("b_down", [P, L])
        n_sq = sb("n_sq", [P, NT])
        n_s = sb("n_s", [P, NT])
        n_ffn = sb("n_ffn", [P, NT])
        mhalf = sb("mhalf", [P, NT])

        weights_in = sem("weights_in")
        layer1 = [(w_qkv[:], tiles(d["qkv_wT"])), (w_out[:], tiles(d["out_wT"])),
                  (w_min[:], tiles(d["mha_in_wT"])), (w_mout[:], tiles(d["mha_out_wT"])),
                  (w_gate[:], tiles(d["gate_wT"])), (w_gu[:], tiles(d["gu_wT"])),
                  (w_down[:], tiles(d["down_wT"])),
                  (b_qkv[:], d["qkv_b"].partition_broadcast(P)), (b_out[:], d["out_b"].partition_broadcast(P)),
                  (b_min[:], d["mha_in_b"].partition_broadcast(P)), (b_mout[:], d["mha_out_b"].partition_broadcast(P)),
                  (b_gate[:], d["gate_b"].partition_broadcast(P)), (b_down[:], d["down_b"].partition_broadcast(P)),
                  (b_gu[:], d["gu_b"]), (n_sq[:], d["sq_norm_w"]),
                  (n_s[:], d["s_norm_w"]), (n_ffn[:], d["ffn_norm_w"])]

        with ExitStack() as first_ctx:
            def sb1(name, shape, dt=F32):
                return first_ctx.enter_context(nc.sbuf_tensor(name, shape, dt))

            def sem1(name):
                return first_ctx.enter_context(nc.semaphore(name))

            FT = sb1("FT", [P, NT, L])
            Wt = sb1("Wt", [P, NT, L])
            taps = sb1("taps", [P, TAPS])
            avg = sb1("avg", [P, P])
            q16 = sb1("q16", [B, L])
            m8 = sb1("m8", [B, C], U8)
            sig = sb1("sig", [P, 1])
            cen = sb1("cen", [P, 1])
            gamma = sb1("gamma", [P, NT])
            beta = sb1("beta", [P, NT])
            n_attn = sb1("n_attn", [P, NT])
            filmW = sb1("filmW", [P, NT, 2 * L])
            filmB = sb1("filmB", [P, 4])
            xb = sb1("xb", [P, 2, NT, L])
            xT = sb1("xT", [P, B, NT, C])
            csum = sb1("csum", [P, NT, B])
            qT = sb1("qT", [P, NT, B])
            sT8 = sb1("sT8", [P, NT, KN, B])
            qT8 = sb1("qT8", [P, NT, KN, B])
            spad = sb1("spad", [P, L + TAPS - 1])
            g = sb1("g", [P, TAPS])
            gs = sb1("gs", [P, 8])
            blur = sb1("blur", [P, L])
            blurT = sb1("blurT", [P, NT, P])
            V = sb1("V", [P, L])
            QV = sb1("QV", [P, L])
            qy = sb1("qy", [P, L])
            at0 = sb1("at0", [P, 2])
            means = sb1("means", [P, 2])
            tot = sb1("tot", [P, 8])
            w = sb1("w", [P, P + 1])
            w_hi = sb1("w_hi", [P, P])
            half = sb1("half", [P, P + 1])
            mf = sb1("mf", [B, C])
            allpad = sb1("allpad", [B, 2])
            film = sb1("film", [P, 2, NT, B])
            E = sb1("E", [P, 2, NT, 2, C])
            o = sb1("o", [P, 4, 2, C])
            sums = sb1("sums", [P, NT, B * NPAIR])
            squares = sb1("squares", [P, NT, B * NPAIR])
            st = sb1("st", [P, 8, NT])

            tables_in = sem1("tables_in")
            x_in = [sem1(f"x_in{i}") for i in range(2)]
            xT_ps, xT_sb, blur_in = sem1("xT_ps"), sem1("xT_sb"), sem1("blur_in")
            D_ps, D_sb = sem1("D_ps"), sem1("D_sb")
            consts = sem1("consts")
            q_ps, q_sb, qr_ps, qr_sb = sem1("q_ps"), sem1("q_sb"), sem1("qr_ps"), sem1("qr_sb")
            film_ps, film_th = sem1("film_ps"), sem1("film_th")
            mask_ok, maskT_ps, maskT_sb = sem1("mask_ok"), sem1("maskT_ps"), sem1("maskT_sb")
            q8_sb, s_sb, sb_ps = sem1("q8_sb"), sem1("s_sb"), sem1("sb_ps")
            step = sem1("step")
            gz_ok, ge_ok = sem1("gz_ok"), sem1("ge_ok")
            blur_ok, blurT_ps, blurT_sb = sem1("blur_ok"), sem1("blurT_ps"), sem1("blurT_sb")
            V_ps, at0_ok, mean_ps = sem1("V_ps"), sem1("at0_ok"), sem1("mean_ps")
            prod_ok, root_ok, th_ok = sem1("prod_ok"), sem1("root_ok"), sem1("th_ok")
            w_ok, wT_ps, wT_sb = sem1("w_ok"), sem1("wT_ps"), sem1("wT_sb")
            E_ok = sem1("E_ok")
            y_ps, o_ok = sem1("y_ps"), sem1("o_ok")
            abs_ok, o_free = sem1("abs_ok"), sem1("o_free")
            var_ok, rstd_ok, bn_ok, bn_ps = sem1("var_ok"), sem1("rstd_ok"), sem1("bn_ok"), sem1("bn_ps")

            small = [(q16[:], d["cond"]), (eye[:], d["t_eye"]), (FT[:], tiles(d["t_FT"])),
                     (Fm[:], tiles(d["t_F"])), (Wt[:], tiles(d["t_W"])), (taps[:], d["t_taps"]),
                     (avg[:], d["t_avg"]), (m8[:], d["mask"]),
                     (gamma[:], d["gamma"]), (beta[:], d["beta"]),
                     (n_attn[:], d["attn_norm_w"]), (filmW[:], tiles(d["film_wT"])),
                     (filmB[:], d["film_b"])]
            ALL_TABLES = 16 * len(small)

            block = first_ctx.enter_context(nc.Block())

            @block.sync
            def _(sp):
                for dst, src in small[0::2]:
                    sp.dma_start(dst, src).then_inc(tables_in, 16)
                for s in range(2):
                    sp.dma_start(xb[:, s], tiles(d["x"][s])).then_inc(x_in[s], 16)
                with sp.Fori(0, B // 2 - 1) as two:
                    for s in range(2):
                        sp.wait_ge(xT_ps, two * 2 + s + 1)
                        sp.dma_start(xb[:, s], tiles(d["x"][two * 2 + (s + 2)])).then_inc(x_in[s], 16)

            @block.gpsimd
            def _(pool):
                for i in range(KN):
                    pool.dma_start(sig[i * B:(i + 1) * B, :],
                                   d["sigmas"][i].partition_broadcast(B)).then_inc(blur_in, 16)
                    pool.dma_start(cen[i * B:(i + 1) * B, :],
                                   d["centers"][i].partition_broadcast(B)).then_inc(blur_in, 16)
                nc.gpsimd.memset(mhalf[:], -0.5).then_inc(consts, 1)
                pool.wait_ge(tables_in, ALL_TABLES)
                for dst, src in layer1:
                    pool.dma_start(dst, src).then_inc(weights_in, 16)

                pool.wait_ge(var_ok, 1)
                pool.wait_ge(consts, 1)
                nc.gpsimd.tensor_tensor(st[:, 4, :], st[:, 3, :], mhalf[:], ALU.pow).then_inc(rstd_ok, 1)

            @block.scalar
            def _(act):
                for dst, src in small[1::2]:
                    act.dma_start(dst, src).then_inc(tables_in, 16)
                act.wait_ge(tables_in, ALL_TABLES)
                act.wait_ge(film_ps, 1)
                for ft in range(NT):
                    nc.scalar.activation(film[:, 0, ft, :], ps[6][:, ft * B:(ft + 1) * B], ACT.Tanh,
                                         bias=filmB[:, ft:ft + 1]).then_inc(film_th, 1)
                for ft in range(NT):
                    a = nc.scalar.activation(filmS[:, ft, :], ps[6][:, (2 + ft) * B:(3 + ft) * B], ACT.Identity,
                                             bias=filmB[:, 2 + ft:3 + ft])
                a.then_inc(film_th, 1)

                act.wait_ge(gz_ok, 1)
                nc.scalar.activation(g[:], g[:], ACT.Exp, scale=-0.5, accum_out=gs[:, 3:4]).then_inc(ge_ok, 1)
                with act.Fori(0, B // 2) as two:
                    for s in range(2):
                        act.wait_ge(xT_ps, two * 2 + s + 1)
                        for lt in range(NT):
                            nc.scalar.activation(xT[:, bass.ds(two * 2 + s, 1), lt, :], ps[s][:, lt * C:(lt + 1) * C], ACT.Copy,
                                                 accum_out=csum[:, lt, bass.ds(two * 2 + s, 1)]).then_inc(xT_sb, 1)
                act.wait_ge(prod_ok, 1)
                nc.scalar.activation(w[:], w[:], ACT.Sqrt).then_inc(root_ok, 1)
                act.wait_ge(root_ok, 1)
                nc.scalar.activation(w[:], w[:], ACT.Tanh, scale=0.05).then_inc(th_ok, 1)

                with act.Fori(0, B) as b:
                    for n in range(2 * NPAIR + 1):
                        if n < 2 * NPAIR:
                            act.wait_ge(y_ps, at(b, 8, n + 1) + 4)
                            act.wait_ge(o_free, at(b, 8, n + 1))
                            nc.scalar.activation(o[:, n % 4], ps[n % 4][:], ACT.Abs).then_inc(abs_ok, 1)
                        if n >= 1:
                            act.wait_ge(o_ok, at(b, 8, n))
                            nc.scalar.activation(
                                o[:, (n - 1) % 4], o[:, (n - 1) % 4], ACT.Square,
                                accum_out=squares[:, (n - 1) % 2, bass.ds(b * NPAIR + (n - 1) // 2, 1)]).then_inc(o_free, 1)

            @block.tensor
            def _(pe):
                pe.wait_ge(tables_in, ALL_TABLES)
                for lt in range(NT):
                    m = nc.tensor.transpose(ps[7][:, lt * B:(lt + 1) * B], q16[:, lt * P:(lt + 1) * P], eye[0:B, 0:B])
                m.then_inc(q_ps, 1)
                pe.wait_ge(mask_ok, 1)
                for t in range(NT):
                    m = nc.tensor.transpose(ps[5][:, t * B:(t + 1) * B], mf[:, t * P:(t + 1) * P], eye[0:B, 0:B])
                m = nc.tensor.matmul(ps[5][:, 2 * B:3 * B], allpad[:, 1:2].broadcast_to([B, P]), eye[0:B, 0:B],
                                     start=True, stop=True)
                m.then_inc(maskT_ps, 1)
                pe.wait_ge(q_sb, 1)
                for mt in range(4):
                    for kt in range(NT):
                        m = nc.tensor.matmul(ps[6][:, mt * B:(mt + 1) * B], filmW[:, kt, mt * P:(mt + 1) * P],
                                             qT[:, kt, :], start=(kt == 0), stop=(kt == 1))
                m.then_inc(film_ps, 1)
                for rt in range(NT):
                    for kt in range(NT):
                        m = nc.tensor.matmul(ps[4][:, rt * B:(rt + 1) * B], FT[:, kt, rt * P:(rt + 1) * P],
                                             qT[:, kt, :], start=(kt == 0), stop=(kt == 1))
                m.then_inc(qr_ps, 1)

                pe.wait_ge(q8_sb, 1)
                for lt in range(NT):
                    m = nc.tensor.matmul(ps[6][:, 256:256 + L], qT8[:, lt].rearrange("p i b -> p (i b)"),
                                         Wt[:, lt, :], start=(lt == 0), stop=(lt == 1))
                m = nc.tensor.matmul(ps[7][:, 256:257], qT8[:, 0].rearrange("p i b -> p (i b)"), eye[:, 0:1],
                                     start=True, stop=True)
                m.then_inc(V_ps, 1)

                with pe.Fori(0, B // 2) as two:
                    for s in range(2):
                        xbank, Dbank = ps[s], ps[2 + s]
                        pe.wait_ge(x_in[s], at(two, 16, 16))
                        pe.wait_ge(D_sb, two * 2 + s + 1)
                        for lt in range(NT):
                            for ct in range(NT):
                                m = nc.tensor.transpose(xbank[:, lt * C + ct * P:lt * C + (ct + 1) * P],
                                                        xb[:, s, ct, lt * P:(lt + 1) * P], eye[:])
                        m.then_inc(xT_ps, 1)
                        pe.wait_ge(xT_sb, two * 4 + (2 * s + 2))
                        for rt in range(NT):
                            for kt in range(NT):
                                m = nc.tensor.matmul(Dbank[:, rt * C:(rt + 1) * C], FT[:, kt, rt * P:(rt + 1) * P],
                                                     xT[:, bass.ds(two * 2 + s, 1), kt, :], start=(kt == 0), stop=(kt == 1))
                        m.then_inc(D_ps, 1)
                pe.wait_ge(s_sb, 1)
                for lt in range(NT):
                    m = nc.tensor.matmul(ps[3][:, lt * P:(lt + 1) * P],
                                         sT8[:, lt].rearrange("p i b -> p (i b)"), eye[:],
                                         start=True, stop=True)
                m.then_inc(sb_ps, 1)
                pe.wait_ge(blur_ok, 1)
                for lt in range(NT):
                    m = nc.tensor.transpose(ps[4][:, lt * P:(lt + 1) * P], blur[:, lt * P:(lt + 1) * P], eye[:])
                m.then_inc(blurT_ps, 1)
                pe.wait_ge(blurT_sb, 1)
                for lt in range(NT):
                    m = nc.tensor.matmul(ps[5][:, 0:L], blurT[:, lt, :], Wt[:, lt, :], start=(lt == 0), stop=(lt == 1))
                m.then_inc(V_ps, 1)
                pe.wait_ge(at0_ok, 2)
                m = nc.tensor.matmul(ps[4][:, 0:2], avg[:], at0[:], start=True, stop=True)
                m.then_inc(mean_ps, 1)
                pe.wait_ge(w_ok, 3)
                nc.tensor.transpose(ps[3][:, 0:P], w[:, 0:P], eye[:])
                m = nc.tensor.transpose(ps[3][:, P:2 * P], w_hi[:], eye[:])
                m.then_inc(wT_ps, 1)

                pe.wait_ge(wT_sb, 2)
                with pe.Fori(0, B) as b:
                    for pr in range(NPAIR):
                        pe.wait_ge(E_ok, at(b, NPAIR, pr + 1))
                        for lt in range(NT):
                            pe.wait_ge(abs_ok, at(b, 8, 2 * pr + lt + 1))
                            for kt in range(NT):
                                m = nc.tensor.matmul(ps[(pr % 2) * 2 + lt][:], Fm[:, kt, lt * P:(lt + 1) * P],
                                                     E[:, pr % 2, kt, :, :], start=(kt == 0), stop=(kt == 1))
                            m.then_inc(y_ps, 1)

                pe.wait_ge(bn_ok, 2)
                for n in range(2):
                    for lt in range(NT):
                        m = nc.tensor.matmul(ps[4 + n][:, lt * P:(lt + 1) * P],
                                             st[:, 5 + n, lt:lt + 1].broadcast_to([P, P]), eye[:],
                                             start=True, stop=True)
                m.then_inc(bn_ps, 1)

            @block.vector
            def _(dve):
                n = [0]

                def link(ins):
                    n[0] += 1
                    ins.then_inc(step, 1)
                    dve.wait_ge(step, n[0])

                dve.sem_inc(D_sb, 2)
                dve.sem_inc(y_ps, 4)
                dve.sem_inc(abs_ok, 4)
                dve.sem_inc(o_free, 4)
                dve.wait_ge(tables_in, ALL_TABLES)
                link(nc.vector.tensor_copy(mf[:], m8[:]))
                link(nc.vector.tensor_reduce(allpad[:, 0:1], mf[:], AX.X, ALU.min))
                link(nc.vector.tensor_scalar(allpad[:, 1:2], allpad[:, 0:1], -1.0, 1.0, ALU.mult, ALU.add))
                nc.vector.tensor_scalar(mf[:], mf[:], allpad[:, 1:2], NEG, ALU.mult, ALU.mult).then_inc(mask_ok, 1)
                dve.wait_ge(q_ps, 1)
                nc.vector.tensor_copy(qT[:], ps[7][:, 0:2 * B]).then_inc(q_sb, 1)
                dve.wait_ge(maskT_ps, 1)
                nc.vector.tensor_copy(keybias[:], ps[5][:, 0:2 * B]).then_inc(maskT_sb, 1)
                nc.vector.tensor_copy(vrow[:], ps[5][:, 2 * B:3 * B]).then_inc(maskT_sb, 1)
                dve.wait_ge(qr_ps, 1)
                nc.vector.tensor_copy(QR[:], ps[4][:, 0:2 * B]).then_inc(qr_sb, 1)
                dve.wait_ge(film_th, 3)
                link(nc.vector.tensor_scalar(film[:, 1], film[:, 0], 0.1, 1.0, ALU.mult, ALU.add))
                for ft in range(NT):
                    nc.vector.tensor_scalar(filmG[:, ft, :], film[:, 1, ft, :], n_attn[:, ft:ft + 1], None, ALU.mult)
                dve.wait_ge(q_sb, 1)
                for lt in range(NT):
                    v = nc.vector.tensor_copy(qT8[:, lt], qT[:, lt, :].unsqueeze(1).broadcast_to([P, KN, B]))
                v.then_inc(q8_sb, 1)
                dve.wait_ge(blur_in, 16 * 2 * KN)
                link(nc.vector.tensor_scalar(gs[:, 0:1], sig[:], 0.001, None, ALU.add))
                link(nc.vector.reciprocal(gs[:, 1:2], gs[:, 0:1]))
                link(nc.vector.tensor_scalar(g[:], taps[:], cen[:, 0:1], gs[:, 1:2], ALU.subtract, ALU.mult))
                nc.vector.tensor_tensor(g[:], g[:], g[:], ALU.mult).then_inc(gz_ok, 1)
                dve.wait_ge(ge_ok, 1)
                link(nc.vector.tensor_scalar(gs[:, 4:5], gs[:, 3:4], 0.01, None, ALU.add))
                link(nc.vector.reciprocal(gs[:, 5:6], gs[:, 4:5]))
                link(nc.vector.tensor_scalar(g[:], g[:], gs[:, 5:6], None, ALU.mult))

                dve.wait_ge(qr_sb, 1)
                with dve.Fori(0, B // 2) as two:
                    for s in range(2):
                        dve.wait_ge(D_ps, two * 2 + s + 1)
                        for rt in range(NT):
                            v = nc.vector.tensor_scalar(D[:, bass.ds(two * 2 + s, 1), rt, :],
                                                        ps[2 + s][:, rt * C:(rt + 1) * C],
                                                        QR[:, rt, bass.ds(two * 2 + s, 1)], None, ALU.subtract)
                        v.then_inc(D_sb, 1)

                dve.wait_ge(xT_sb, 2 * B)
                for lt in range(NT):
                    v = nc.vector.tensor_copy(sT8[:, lt], csum[:, lt, :].unsqueeze(1).broadcast_to([P, KN, B]))
                v.then_inc(s_sb, 1)
                dve.wait_ge(sb_ps, 1)
                half_k = TAPS // 2
                link(nc.vector.tensor_copy(spad[:, half_k:half_k + L], ps[3][:, 0:L]))
                nc.vector.tensor_copy(spad[:, 0:half_k], spad[:, half_k:half_k + 1].broadcast_to([P, half_k]))
                link(nc.vector.tensor_copy(spad[:, half_k + L:], spad[:, half_k + L - 1:half_k + L].broadcast_to([P, half_k])))
                link(nc.vector.tensor_scalar(blur[:], spad[:, 0:L], g[:, 0:1], None, ALU.mult))
                for t in range(1, TAPS):
                    v = nc.vector.scalar_tensor_tensor(out=blur[:], in0=spad[:, t:t + L], scalar=g[:, t:t + 1],
                                                       in1=blur[:], op0=ALU.mult, op1=ALU.add)
                    if t < TAPS - 1:
                        link(v)
                v.then_inc(blur_ok, 1)
                dve.wait_ge(blurT_ps, 1)
                nc.vector.tensor_copy(blurT[:], ps[4][:, 0:2 * P]).then_inc(blurT_sb, 1)
                dve.wait_ge(blur_ok, 1)
                nc.vector.tensor_copy(at0[:, 0:1], blur[:, 0:1]).then_inc(at0_ok, 1)
                dve.wait_ge(V_ps, 2)
                nc.vector.tensor_copy(at0[:, 1:2], ps[7][:, 256:257]).then_inc(at0_ok, 1)
                dve.wait_ge(mean_ps, 1)
                link(nc.vector.tensor_copy(means[:], ps[4][:, 0:2]))
                NC = P + 1
                nc.vector.tensor_scalar(V[:, 0:NC], ps[5][:, 0:NC], means[:, 0:1], None, ALU.subtract)
                nc.vector.tensor_copy(V[:, NC:L], ps[5][:, NC:L])
                nc.vector.tensor_scalar(QV[:, 0:NC], ps[6][:, 256:256 + NC], means[:, 0:1], None, ALU.subtract)
                nc.vector.tensor_copy(QV[:, NC:L], ps[6][:, 256 + NC:256 + L])
                link(nc.vector.tensor_scalar(qy[:, 0:NC], ps[6][:, 256:256 + NC], means[:, 1:2], None, ALU.subtract))
                nc.vector.tensor_tensor(V[:], V[:], V[:], ALU.mult)
                nc.vector.tensor_tensor(QV[:], QV[:], QV[:], ALU.mult)
                link(nc.vector.tensor_tensor(qy[:, 0:NC], qy[:, 0:NC], qy[:, 0:NC], ALU.mult))
                for m, z in enumerate((V, QV)):
                    nc.vector.tensor_reduce(tot[:, 4 * m:4 * m + 1], z[:, 1:P], AX.X, ALU.add)
                    nc.vector.tensor_reduce(tot[:, 4 * m + 1:4 * m + 2], z[:, NC:L], AX.X, ALU.add)
                    link(nc.vector.tensor_tensor(tot[:, 4 * m + 2:4 * m + 3], z[:, 0:1], z[:, P:NC], ALU.add))
                for m in range(2):
                    link(nc.vector.tensor_tensor(tot[:, 4 * m:4 * m + 1], tot[:, 4 * m:4 * m + 1],
                                                 tot[:, 4 * m + 1:4 * m + 2], ALU.subtract))
                    link(nc.vector.scalar_tensor_tensor(out=tot[:, 4 * m + 3:4 * m + 4], in0=tot[:, 4 * m:4 * m + 1],
                                                        scalar=2.0, in1=tot[:, 4 * m + 2:4 * m + 3],
                                                        op0=ALU.mult, op1=ALU.add))
                link(nc.vector.tensor_tensor(gs[:, 6:7], tot[:, 3:4], tot[:, 7:8], ALU.mult))
                link(nc.vector.tensor_scalar(gs[:, 6:7], gs[:, 6:7], 0.001, None, ALU.add))
                link(nc.vector.reciprocal(gs[:, 7:8], gs[:, 6:7]))
                nc.vector.tensor_tensor(V[:, 1:P], V[:, 1:P], V[:, NC:L], ALU.add)
                link(nc.vector.tensor_tensor(qy[:, 1:P], qy[:, 1:P], QV[:, NC:L], ALU.add))
                nc.vector.tensor_scalar(V[:, 0:NC], V[:, 0:NC], gs[:, 7:8], None, ALU.mult)
                link(nc.vector.tensor_scalar(qy[:, 0:NC], qy[:, 0:NC], gs[:, 7:8], None, ALU.mult))
                nc.vector.tensor_tensor(w[:], V[:, 0:NC], qy[:, 0:NC], ALU.mult).then_inc(prod_ok, 1)
                dve.wait_ge(th_ok, 1)
                link(nc.vector.tensor_scalar(half[:], w[:], 1.0, None, ALU.add))
                link(nc.vector.reciprocal(V[:, 0:NC], half[:]))
                nc.vector.scalar_tensor_tensor(out=w[:], in0=w[:], scalar=2.0, in1=V[:, 0:NC],
                                               op0=ALU.mult, op1=ALU.mult).then_inc(w_ok, 1)
                dve.wait_ge(w_ok, 1)
                nc.vector.tensor_copy(w_hi[:, 0:1], w[:, P:P + 1]).then_inc(w_ok, 1)
                nc.vector.tensor_copy(w_hi[:, 1:P], w[:, 1:P]).then_inc(w_ok, 1)
                dve.wait_ge(wT_ps, 1)
                nc.vector.tensor_copy(wT[:, 0], ps[3][:, 0:P]).then_inc(wT_sb, 1)
                nc.vector.tensor_copy(wT[:, 1], ps[3][:, P:2 * P]).then_inc(wT_sb, 1)

                dve.wait_ge(qr_sb, 1)
                dve.wait_ge(wT_sb, 2)
                dve.wait_ge(D_sb, B + 2)
                def spectrum(b, pr, batch):
                    dve.wait_ge(y_ps, at(b, 8, 2 * pr + 2))
                    for kt in range(NT):
                        for j in range(2):
                            e = nc.vector.tensor_scalar(
                                E[:, pr % 2, kt, j, :], D[:, bass.ds(batch, 1), kt, :],
                                wT[:, kt, 2 * pr + j, bass.ds(batch, 1)], QR[:, kt, bass.ds(batch, 1)],
                                ALU.mult, ALU.add)
                    e.then_inc(E_ok, 1)

                def turn(b, last=False):
                    for pr in range(NPAIR):
                        if pr < NPAIR - 1:
                            spectrum(b, pr + 1, b)
                        elif not last:
                            spectrum(b + 1, 0, b + 1)
                        for lt in range(NT):
                            slot = 2 * (pr % 2) + lt
                            dve.wait_ge(abs_ok, at(b, 8, 2 * pr + lt + 1) + 4)
                            nc.vector.scalar_tensor_tensor(
                                out=o[:, slot], in0=o[:, slot], scalar=1.0,
                                in1=xT[:, bass.ds(b, 1), lt, :].broadcast_to([P, 2, C]),
                                op0=ALU.mult, op1=ALU.add,
                                accum_out=sums[:, lt, bass.ds(b * NPAIR + pr, 1)]).then_inc(o_ok, 1)

                spectrum(0, 0, 0)
                with dve.Fori(0, B - 1) as b:
                    turn(b)
                turn(B - 1, last=True)
                dve.wait_ge(o_free, 4 + 8 * B)
                N = float(B * C * KN)
                nc.vector.tensor_reduce(st[:, 0, :], sums[:], AX.X, ALU.add)
                link(nc.vector.tensor_reduce(st[:, 1, :], squares[:], AX.X, ALU.add))
                nc.vector.tensor_scalar(st[:, 0, :], st[:, 0, :], 1.0 / N, None, ALU.mult)
                link(nc.vector.tensor_scalar(st[:, 1, :], st[:, 1, :], 1.0 / N, BN_EPS, ALU.mult, ALU.add))
                link(nc.vector.tensor_tensor(st[:, 2, :], st[:, 0, :], st[:, 0, :], ALU.mult))
                nc.vector.tensor_tensor(st[:, 3, :], st[:, 1, :], st[:, 2, :], ALU.subtract).then_inc(var_ok, 1)
                dve.wait_ge(rstd_ok, 1)
                nc.vector.tensor_tensor(st[:, 5, :], st[:, 4, :], gamma[:], ALU.mult).then_inc(bn_ok, 1)
                dve.wait_ge(bn_ok, 1)
                link(nc.vector.tensor_tensor(st[:, 7, :], st[:, 0, :], st[:, 5, :], ALU.mult))
                nc.vector.tensor_tensor(st[:, 6, :], beta[:], st[:, 7, :], ALU.subtract).then_inc(bn_ok, 1)
                for lt in range(NT):
                    nc.vector.tensor_scalar(qg[:, lt, :], qT[:, lt, :], st[:, 5, lt:lt + 1], None, ALU.mult)
                dve.wait_ge(bn_ps, 1)
                nc.vector.tensor_copy(RG[:], ps[4][:, 0:L])
                nc.vector.tensor_copy(BP[:], ps[5][:, 0:L])
                dve.wait_ge(weights_in, 16 * len(layer1))
                nc.vector.tensor_scalar(b_guh[:], b_gu[:], 0.5, None, ALU.mult)
                nc.vector.tensor_scalar(b_min[:, 0:L], b_min[:, 0:L], 0.25, None, ALU.mult)

        with ExitStack() as second_ctx:
            def sb2(name, shape, dt=F32):
                return second_ctx.enter_context(nc.sbuf_tensor(name, shape, dt))

            def sem2(name):
                return second_ctx.enter_context(nc.semaphore(name))

            rope_cos = sb2("rope_cos", [P, NT, 2 * L])
            rope_sin = sb2("rope_sin", [P, NT, 2 * L])
            x2 = sb2("x2", [P, NT, L])
            src = sb2("src", [P, NT, L])
            E2 = sb2("E2", [P, 4, NT, C])
            o2 = sb2("o2", [P, KN, NT, L])
            dead = sb2("dead", [P, NT, L])
            deadA = sb2("deadA", [P, NT, L])
            qgs = sb2("qgs", [P, NT])
            QGB = sb2("QGB", [P, L])
            score = sb2("score", [P, NT, KN])
            smax = sb2("smax", [P, NT])
            ssum = sb2("ssum", [P, NT])
            srec = sb2("srec", [P, NT])
            tok0 = sb2("tok0", [P, NT, L])
            tok0b = sb2("tok0b", [P, NT, L])
            tok1 = sb2("tok1", [P, NT, L])
            tok2 = sb2("tok2", [P, NT, L])
            tok2b = sb2("tok2b", [P, NT, L])
            X = sb2("X", [P, NT, L])
            XT = sb2("XT", [P, NT, C])
            srcT = sb2("srcT", [P, NT, C])
            tok1T = sb2("tok1T", [P, NT, C])
            updT = sb2("updT", [P, NT, C])
            upd = sb2("upd", [P, NT, L])
            z = sb2("z", [P, NT, L])
            res = sb2("res", [P, NT, L])
            ms = sb2("ms", [P, 4, NT])
            mse = sb2("mse", [P, 4, NT])
            rms_eps = sb2("rms_eps", [P, NT])
            rstd = sb2("rstd", [P, 4, NT])
            rq = sb2("rq", [P, NT])
            mobv = sb2("mobv", [P, L])
            QP = sb2("QP", [P, NT, 2 * H, HP])
            VP = [sb2(f"VP{a}", [P, NT, H * VW + HP - VW]) for a in range(2)]
            QKT = sb2("QKT", [P, 4, 2 * C])
            QK, QKr = QKT[:, 0:2, :], QKT[:, 2:4, :]
            hid = QKT[:].rearrange("p g (m c) -> p (g m) c", c=C)
            nmax = sb2("nmax", [P, 4, NT])
            Pr = sb2("Pr", [P, 2, NT, C])
            PrT = sb2("PrT", [P, 2, NT, C])
            Oh = sb2("Oh", [P, 2, C])
            orec = sb2("orec", [P, 4, NT * 4])
            O = sb2("O", [P, NT, L])
            OT = sb2("OT", [P, NT, C])
            th = sb2("th", [P, 2, C])
            val = sb2("val", [P, 2, C])

            rope_in, x2_in, src_in, out_done = sem2("rope_in"), sem2("x2_in"), sem2("src_in"), sem2("out_done")
            pads_ok, qgs_ok, QGB_ps, QGB_ok = sem2("pads_ok"), sem2("qgs_ok"), sem2("QGB_ps"), sem2("QGB_ok")
            E2_ok, y2_ps, abs2_ok, o2_ok = sem2("E2_ok"), sem2("y2_ps"), sem2("abs2_ok"), sem2("o2_ok")
            dot_ok, score_ok, sexp_ok = sem2("dot_ok"), sem2("score_ok"), sem2("sexp_ok")
            wsum_ok, tok0_ok = sem2("wsum_ok"), sem2("tok0_ok")
            step2 = sem2("step2")
            poolstep = sem2("poolstep")
            ms_ok = [sem2(f"ms_ok{i}") for i in range(4)]
            mse_ok = [sem2(f"mse_ok{i}") for i in range(4)]
            rs_ok = [sem2(f"rs_ok{i}") for i in range(4)]
            kb_ok, mobv_ok, tok0b_ok, tok2b_ok = sem2("kb_ok"), sem2("mobv_ok"), sem2("tok0b_ok"), sem2("tok2b_ok")
            srcT_ps, srcT_ok, kv_ps, kv_ok = sem2("srcT_ps"), sem2("srcT_ok"), sem2("kv_ps"), sem2("kv_ok")
            X1_ok, X1T_ps, X1T_ok = sem2("X1_ok"), sem2("X1T_ps"), sem2("X1T_ok")
            qkv_ps, qk_ok, v_ok, rsin_ok, rcos_ok, qp_ok = (sem2(n) for n in
                ("qkv_ps", "qk_ok", "v_ok", "rsin_ok", "rcos_ok", "qp_ok"))
            QKT_ps, QKT_ok = sem2("QKT_ps"), sem2("QKT_ok")
            S_ps, max_ok, Pr_ok, PrT_ps, PrT_ok, O_ps = (sem2(n) for n in
                ("S_ps", "max_ok", "Pr_ok", "PrT_ps", "PrT_ok", "O_ps"))
            Oh_ok, Og_ps, div_ok, O_ok = (sem2(n) for n in
                ("Oh_ok", "Og_ps", "div_ok", "O_ok"))
            OT_ps, OT_ok = sem2("OT_ps"), sem2("OT_ok")
            att_ps, tok1_ok, tok1T_ps, tok1T_ok = sem2("att_ps"), sem2("tok1_ok"), sem2("tok1T_ps"), sem2("tok1T_ok")
            X2T_ok, cq_ps, cq_ok = sem2("X2T_ok"), sem2("cq_ps"), sem2("cq_ok")
            upd_ps, upd_ok, updT_ps, updT_ok = sem2("upd_ps"), sem2("upd_ok"), sem2("updT_ps"), sem2("updT_ok")
            gate_ps, z_ok, zt_ok, tok2_ok = sem2("gate_ps"), sem2("z_ok"), sem2("zt_ok"), sem2("tok2_ok")
            X3_ok, X3T_ps, X3T_ok = sem2("X3_ok"), sem2("X3T_ps"), sem2("X3T_ok")
            gu_ps, act_ok, prod2_ok, hid_ok, down_ps, res_ok = (sem2(n) for n in
                ("gu_ps", "act_ok", "prod2_ok", "hid_ok", "down_ps", "res_ok"))
            NH = 2 * H
            FIRST_MIX_BANKS = (0, 1, 2, 3, 0, 1, 2, 3)
            MIX_BANKS = (6, 7, 6, 3, 6, 7, 0, 1)

            def after(b):
                return (b + 1) % B

            block = second_ctx.enter_context(nc.Block())

            @block.sync
            def _(sp):
                sp.dma_start(x2[:], tiles(d["x"][0])).then_inc(x2_in, 16)
                sp.dma_start(src[:], tiles(d["fside"][0])).then_inc(src_in, 16)
                sp.dma_start(rope_cos[:], tiles(d["t_cos"])).then_inc(rope_in, 16)
                sp.dma_start(rope_sin[:], tiles(d["t_sin"])).then_inc(rope_in, 16)
                with sp.Fori(0, B) as b:
                    sp.wait_ge(o2_ok, at(b, KN, KN))
                    sp.dma_start(x2[:], tiles(d["x"][after(b)])).then_inc(x2_in, 16)
                    sp.wait_ge(kv_ok, at(b, 2, 2))
                    sp.dma_start(src[:], tiles(d["fside"][after(b)])).then_inc(src_in, 16)
                sp.wait_ge(src_in, 16 * (B + 1))

            @block.gpsimd
            def _(pool):
                nc.gpsimd.memset(QP[:], 0.0).then_inc(poolstep, 1)
                for a in range(2):
                    nc.gpsimd.memset(VP[a][:], 0.0).then_inc(poolstep, 1)
                nc.gpsimd.memset(rms_eps[:], RMS_EPS).then_inc(pads_ok, 1)
                pool.wait_ge(poolstep, 3)
                nc.gpsimd.memset(QP[:, :, 0:H, ONE_COL:ONE_COL + 1], 1.0).then_inc(pads_ok, 1)
                for a in range(2):
                    ones_v = VP[a][:, :, 0:H * VW].rearrange("p t (h e) -> p t h e", e=VW)[:, :, :, ONE_COL:VW]
                    nc.gpsimd.memset(ones_v, 1.0).then_inc(pads_ok, 1)

                def add_x(m, i):
                    if i == 0:
                        pool.wait_ge(x2_in, at(m, 16, 16))
                    pool.wait_ge(abs2_ok, at(m, KN, i + 1))
                    nc.gpsimd.tensor_tensor(o2[:, i], o2[:, i], x2[:], ALU.add).then_inc(o2_ok, 1)

                def mean_to_rstd(m, n):
                    pool.wait_ge(ms_ok[n], at(m, 2, 2))
                    nc.gpsimd.tensor_tensor(mse[:, n], ms[:, n], rms_eps[:], ALU.add).then_inc(mse_ok[n], 1)
                    pool.wait_ge(mse_ok[n], m + 1)
                    nc.gpsimd.tensor_tensor(rstd[:, n], mse[:, n], mhalf[:], ALU.pow).then_inc(rs_ok[n], 1)

                for i in range(KN):
                    add_x(0, i)
                pool.wait_ge(pads_ok, 4)
                mean_to_rstd(0, 1)
                with pool.Fori(0, B) as b:
                    nb = b + 1
                    pool.wait_ge(tok0_ok, b + 1)
                    nc.gpsimd.tensor_tensor(tok0b[:], tok0[:], b_out[:].unsqueeze(1).broadcast_to([P, NT, L]),
                                            ALU.add).then_inc(tok0b_ok, 1)
                    pool.wait_ge(rope_in, 32)
                    for t in range(NT):
                        pool.wait_ge(qk_ok, at(b, 2, t + 1))
                        for e in range(2):
                            qk = QK[:, t, :].rearrange("p (n e) -> p n e", e=2)
                            r = nc.gpsimd.tensor_tensor(
                                QKr[:, t, :].rearrange("p (n e) -> p n e", e=2)[:, :, e], qk[:, :, 1 - e],
                                rope_sin[:, t, :].rearrange("p (n e) -> p n e", e=2)[:, :, e], ALU.mult)
                        r.then_inc(rsin_ok, 1)
                    for t in range(NT):
                        c = nc.gpsimd.tensor_copy(
                            QP[:, t, H:2 * H, ONE_COL:ONE_COL + 1],
                            keybias[:, t, bass.ds(b, 1)].unsqueeze(1).broadcast_to([P, H, 1]))
                    c.then_inc(kb_ok, 1)
                    for i in range(3):
                        add_x(nb, i)
                    mean_to_rstd(b, 0)
                    add_x(nb, 3)
                    mean_to_rstd(b, 2)
                    for i in range(4, 8):
                        add_x(nb, i)
                    mean_to_rstd(b, 3)
                    pool.wait_ge(tok2_ok, b + 1)
                    nc.gpsimd.tensor_tensor(tok2b[:], tok2[:], b_down[:].unsqueeze(1).broadcast_to([P, NT, L]),
                                            ALU.add).then_inc(tok2b_ok, 1)
                    mean_to_rstd(nb, 1)

            @block.scalar
            def _(act):
                def squares_of(n, t):
                    for tt in range(NT):
                        nc.scalar.activation(deadA[:, tt], t[:, tt, :], ACT.Square, scale=L ** -0.5,
                                             accum_out=ms[:, n, tt:tt + 1]).then_inc(ms_ok[n], 1)

                def spectrum(m, batch, i, first=False):
                    if not first:
                        act.wait_ge(y2_ps, at(m, KN, i - 3))
                    for kt in range(NT):
                        e = nc.scalar.activation(E2[:, i % 4, kt, :], D[:, bass.ds(batch, 1), kt, :], ACT.Identity,
                                                 scale=wT[:, kt, i, bass.ds(batch, 1)],
                                                 bias=QR[:, kt, bass.ds(batch, 1)])
                    e.then_inc(E2_ok, 1)

                def abs_y(m, i, bank):
                    act.wait_ge(y2_ps, at(m, KN, i + 1))
                    nc.scalar.activation(o2[:, i], ps[bank][:], ACT.Abs).then_inc(abs2_ok, 1)

                def softmax_kernels(m):
                    act.wait_ge(score_ok, m + 1)
                    for ct in range(NT):
                        a_ = nc.scalar.activation(score[:, ct, :], score[:, ct, :], ACT.Exp, bias=smax[:, ct:ct + 1],
                                                  accum_out=ssum[:, ct:ct + 1])
                    a_.then_inc(sexp_ok, 1)

                def heads_T_out(b, a):
                    for g4 in range(4):
                        act.wait_ge(QKT_ps, at(b, 8, 4 * a + g4 + 1))
                        nc.scalar.activation(QKT[:, g4, :], ps[4 + g4 % 2][:], ACT.Copy).then_inc(QKT_ok, 1)

                def values_out(b, a, g4):
                    act.wait_ge(O_ps, at(b, NH, a * H + 4 * g4 + 4))
                    nc.scalar.activation(Oh[:, g4 % 2], ps[6 + g4 % 2][:, 0:C], ACT.Copy).then_inc(Oh_ok, 1)

                def attention(b, a, between):
                    for h in range(H):
                        act.wait_ge(max_ok, at(b, NH, a * H + h + 1))
                        if h >= 2:
                            act.wait_ge(PrT_ps, at(b, NH, a * H + h - 1))
                        for qt in range(NT):
                            e = nc.scalar.activation(Pr[:, h % 2, qt, :], ps[h % 4][:, qt * C:(qt + 1) * C], ACT.Exp,
                                                     bias=nmax[:, h % 4, qt:qt + 1])
                        e.then_inc(Pr_ok, 1)
                        if h in (7, 11, 15):
                            values_out(b, a, h // 4 - 1)
                        between(h)
                    values_out(b, a, 3)

                for i in range(-4, KN):
                    if i >= 0:
                        abs_y(0, i, FIRST_MIX_BANKS[i])
                    if 0 <= i + 4 < KN:
                        spectrum(0, 0, i + 4, first=(i < 0))
                for i in range(4):
                    spectrum(1, 1, i)
                softmax_kernels(0)
                act.wait_ge(tok0_ok, 1)
                squares_of(1, tok0)

                with act.Fori(0, B) as b:
                    nb, nxt, nxt2 = b + 1, after(b), after(b + 1)
                    act.wait_ge(X1T_ps, b + 1)
                    for ft in range(NT):
                        a_ = nc.scalar.activation(XT[:, ft, :], ps[4][:, ft * C:(ft + 1) * C], ACT.Identity,
                                                  scale=filmG[:, ft, bass.ds(b, 1)], bias=filmS[:, ft, bass.ds(b, 1)])
                    a_.then_inc(X1T_ok, 1)
                    for i in range(2):
                        abs_y(nb, i, MIX_BANKS[i])
                    heads_T_out(b, 0)

                    def self_between(h):
                        if h == 0:
                            abs_y(nb, 2, MIX_BANKS[2])
                        if h in (2, 8, 10):
                            spectrum(nb, nxt, {2: 4, 8: 5, 10: 6}[h])
                        if h == 3:
                            act.wait_ge(src_in, at(b, 16, 16))
                            squares_of(0, src)
                        if h == 4:
                            act.wait_ge(srcT_ps, b + 1)
                            for ft in range(NT):
                                s_ = nc.scalar.activation(srcT[:, ft, :], ps[7][:, ft * C:(ft + 1) * C], ACT.Copy,
                                                          scale=n_s[:, ft:ft + 1])
                            s_.then_inc(srcT_ok, 1)
                    attention(b, 0, self_between)
                    act.wait_ge(OT_ps, at(b, 2, 1))
                    nc.scalar.activation(OT[:], ps[4][:], ACT.Copy).then_inc(OT_ok, 1)
                    abs_y(nb, 3, MIX_BANKS[3])
                    act.wait_ge(tok1_ok, b + 1)
                    squares_of(2, tok1)
                    act.wait_ge(tok1T_ps, b + 1)
                    nc.scalar.activation(tok1T[:], ps[5][:], ACT.Copy).then_inc(tok1T_ok, 1)
                    abs_y(nb, 4, MIX_BANKS[4])
                    heads_T_out(b, 1)

                    def cross_between(h):
                        if h == 0:
                            abs_y(nb, 5, MIX_BANKS[5])
                        if h == 2:
                            spectrum(nb, nxt, 7)
                        if h in (4, 6):
                            spectrum(b + 2, nxt2, h // 2 - 2)
                    attention(b, 1, cross_between)
                    act.wait_ge(OT_ps, at(b, 2, 2))
                    nc.scalar.activation(OT[:], ps[4][:], ACT.Copy).then_inc(OT_ok, 1)
                    abs_y(nb, 6, MIX_BANKS[6])
                    act.wait_ge(updT_ps, b + 1)
                    nc.scalar.activation(updT[:], ps[5][:], ACT.Copy).then_inc(updT_ok, 1)
                    act.wait_ge(z_ok, b + 1)
                    nc.scalar.activation(z[:], z[:], ACT.Tanh, scale=0.5).then_inc(zt_ok, 1)
                    abs_y(nb, 7, MIX_BANKS[7])
                    act.wait_ge(tok2_ok, b + 1)
                    squares_of(3, tok2)
                    act.wait_ge(X3T_ps, b + 1)
                    for ft in range(NT):
                        a_ = nc.scalar.activation(XT[:, ft, :], ps[7][:, ft * C:(ft + 1) * C], ACT.Copy,
                                                  scale=n_ffn[:, ft:ft + 1])
                    a_.then_inc(X3T_ok, 1)
                    for m in range(MT):
                        act.wait_ge(gu_ps, at(b, MT, m + 1))
                        if m >= 2:
                            act.wait_ge(hid_ok, at(b, MT, m - 1))
                        nc.scalar.activation(th[:, m % 2, :], ps[m % 4][:, 0:C], ACT.Tanh, scale=0.5,
                                             bias=b_guh[:, m:m + 1])
                        nc.scalar.activation(val[:, m % 2, :], ps[m % 4][:, C:2 * C], ACT.Identity, scale=0.5,
                                             bias=b_guh[:, MT + m:MT + m + 1]).then_inc(act_ok, 1)
                        if m == 0:
                            softmax_kernels(nb)
                        if m in (2, 4):
                            spectrum(b + 2, nxt2, m // 2 + 1)
                        if m == 6:
                            act.wait_ge(tok0_ok, nb + 1)
                            squares_of(1, tok0)
                    act.wait_ge(res_ok, b + 2)
                    act.dma_start(tiles(out[b]), res[:]).then_inc(out_done, 16)
                act.wait_ge(out_done, 16 * B + 16)

            @block.tensor
            def _(pe):
                def turn(bank, t, done):
                    for ft in range(NT):
                        for tt in range(NT):
                            m = nc.tensor.transpose(ps[bank][:, ft * C + tt * P:ft * C + (tt + 1) * P],
                                                    t[:, tt, ft * P:(ft + 1) * P], eye[:])
                    m.then_inc(done, 1)

                def project(bank, col, tt, xT, wt, lo, n):
                    for kt in range(NT):
                        m = nc.tensor.matmul(ps[bank][:, col:col + n], xT[:, kt, tt * P:(tt + 1) * P],
                                             wt[:, kt, lo:lo + n], start=(kt == 0), stop=(kt == NT - 1))
                    return m

                def gain_rows(m):
                    pe.wait_ge(qgs_ok, m + 1)
                    for lt in range(NT):
                        i_ = nc.tensor.matmul(ps[5][:, lt * P:(lt + 1) * P], qgs[:, lt:lt + 1].broadcast_to([P, P]),
                                              eye[:], start=True, stop=True)
                    i_.then_inc(QGB_ps, 1)

                def mix(m, i, bank):
                    pe.wait_ge(E2_ok, at(m, KN, i + 1))
                    for ct in range(NT):
                        for kt in range(NT):
                            i_ = nc.tensor.matmul(ps[bank][:, ct * L:(ct + 1) * L],
                                                  E2[:, i % 4, kt, ct * P:(ct + 1) * P], Fm[:, kt, :],
                                                  start=(kt == 0), stop=(kt == 1))
                    i_.then_inc(y2_ps, 1)

                def turn_heads(b, a):
                    for g4 in range(4):
                        if g4 >= 2:
                            pe.wait_ge(QKT_ok, at(b, 8, 4 * a + g4 - 1))
                        for part in range(2):
                            for tt in range(NT):
                                h0 = part * H + 4 * g4
                                m = nc.tensor.transpose(
                                    ps[4 + g4 % 2][:, part * C + tt * P:part * C + (tt + 1) * P],
                                    QP[:, tt, h0:h0 + 4, :].rearrange("p h e -> p (h e)"), eye[:])
                        m.then_inc(QKT_ps, 1)

                def attention(b, a, between):
                    pe.wait_ge(QKT_ok, at(b, 8, 4 * a + 4))
                    for n in range(H + 5):
                        if n < H:
                            g4, j = n // 4, n % 4
                            if n >= 4:
                                pe.wait_ge(Pr_ok, at(b, NH, a * H + n - 3))
                            for qt in range(NT):
                                m = nc.tensor.matmul(ps[j][:, qt * C:(qt + 1) * C],
                                                     QKT[j * HP:(j + 1) * HP, g4, qt * P:(qt + 1) * P],
                                                     QKT[j * HP:(j + 1) * HP, g4, C:2 * C], start=True, stop=True)
                            m.then_inc(S_ps, 1)
                        between(n)
                        h = n - 2
                        if 0 <= h < H:
                            pe.wait_ge(Pr_ok, at(b, NH, a * H + h + 1))
                            if h >= 2:
                                pe.wait_ge(PrT_ok, at(b, NH, a * H + h - 1))
                            for kt in range(NT):
                                for qt in range(NT):
                                    m = nc.tensor.transpose(ps[4 + h % 2][:, kt * C + qt * P:kt * C + (qt + 1) * P],
                                                            Pr[:, h % 2, qt, kt * P:(kt + 1) * P], eye[:])
                            m.then_inc(PrT_ps, 1)
                        h = n - 3
                        if 0 <= h < H:
                            g4, j = h // 4, h % 4
                            pe.wait_ge(PrT_ok, at(b, NH, a * H + h + 1))
                            if j == 0 and g4 >= 2:
                                pe.wait_ge(O_ok, at(b, 8, 4 * a + g4 - 1))
                            for kt in range(NT):
                                m = nc.tensor.matmul(ps[6 + g4 % 2][j * HP:(j + 1) * HP, 0:C],
                                                     VP[a][:, kt, h * VW:h * VW + HP], PrT[:, h % 2, kt, :],
                                                     start=(kt == 0), stop=(kt == 1))
                            m.then_inc(O_ps, 1)
                        if n in (9, 13, 17, 20):
                            g4 = min((n - 9) // 4, 3) if n < 20 else 3
                            pe.wait_ge(Oh_ok, at(b, 8, 4 * a + g4 + 1))
                            for qt in range(NT):
                                m = nc.tensor.transpose(ps[6 + g4 % 2][:, C + qt * P:C + (qt + 1) * P],
                                                        Oh[:, g4 % 2, qt * P:(qt + 1) * P], eye[:])
                            m.then_inc(Og_ps, 1)

                gain_rows(0)
                for i in range(KN):
                    if i >= 4:
                        pe.wait_ge(abs2_ok, i - 3)
                    mix(0, i, FIRST_MIX_BANKS[i])

                with pe.Fori(0, B) as b:
                    nb = b + 1
                    pe.wait_ge(X1_ok, b + 1)
                    turn(4, X, X1T_ps)
                    gain_rows(nb)
                    pe.wait_ge(res_ok, b + 1)
                    mix(nb, 0, MIX_BANKS[0])
                    pe.wait_ge(X1T_ok, b + 1)
                    for tt in range(NT):
                        project(2 * tt, 0, tt, XT, w_qkv, 0, 2 * L).then_inc(qkv_ps, 1)
                        project(2 * tt + 1, 0, tt, XT, w_qkv, 2 * L, L).then_inc(qkv_ps, 1)
                    mix(nb, 1, MIX_BANKS[1])
                    pe.wait_ge(QGB_ok, nb + 1)
                    pe.wait_ge(qp_ok, at(b, 2, 2))
                    pe.wait_ge(kb_ok, b + 1)
                    pe.wait_ge(v_ok, at(b, 2, 2))
                    turn_heads(b, 0)
                    pe.wait_ge(abs2_ok, at(nb, KN, 1))
                    mix(nb, 2, MIX_BANKS[2])

                    def self_between(n):
                        if n == 3:
                            pe.wait_ge(abs2_ok, at(nb, KN, 3))
                        if n == 4:
                            pe.wait_ge(src_in, at(b, 16, 16))
                            turn(7, src, srcT_ps)
                        if n == 7:
                            pe.wait_ge(srcT_ok, b + 1)
                        if n in (17, 18):
                            project(n - 17, 0, n - 17, srcT, w_min, L, 2 * L).then_inc(kv_ps, 1)
                    attention(b, 0, self_between)
                    pe.wait_ge(O_ok, at(b, 8, 4))
                    turn(4, O, OT_ps)
                    mix(nb, 3, MIX_BANKS[3])
                    pe.wait_ge(OT_ok, at(b, 2, 1))
                    for tt in range(NT):
                        m = project(2, tt * L, tt, OT, w_out, 0, L)
                    m.then_inc(att_ps, 1)
                    pe.wait_ge(tok1_ok, b + 1)
                    turn(5, tok1, tok1T_ps)
                    mix(nb, 4, MIX_BANKS[4])
                    pe.wait_ge(X2T_ok, b + 1)
                    for tt in range(NT):
                        m = project(2, tt * L, tt, XT, w_min, 0, L)
                    m.then_inc(cq_ps, 1)
                    pe.wait_ge(cq_ok, b + 1)
                    pe.wait_ge(kv_ok, at(b, 2, 2))
                    turn_heads(b, 1)
                    mix(nb, 5, MIX_BANKS[5])

                    def cross_between(n):
                        if n == 3:
                            pe.wait_ge(abs2_ok, at(nb, KN, 6))
                        if n == 17:
                            mix(nb, 6, MIX_BANKS[6])
                    attention(b, 1, cross_between)
                    pe.wait_ge(O_ok, at(b, 8, 8))
                    turn(4, O, OT_ps)
                    pe.wait_ge(OT_ok, at(b, 2, 2))
                    for tt in range(NT):
                        m = project(2, tt * L, tt, OT, w_mout, 0, L)
                    m.then_inc(upd_ps, 1)
                    pe.wait_ge(upd_ok, b + 1)
                    turn(5, upd, updT_ps)
                    for tt in range(NT):
                        for kt in range(4):
                            if (tt, kt) == (0, 2):
                                pe.wait_ge(updT_ok, b + 1)
                            xT_ = tok1T if kt < 2 else updT
                            m = nc.tensor.matmul(ps[3][:, tt * L:(tt + 1) * L], xT_[:, kt % 2, tt * P:(tt + 1) * P],
                                                 w_gate[:, kt, :], start=(kt == 0), stop=(kt == 3))
                    m.then_inc(gate_ps, 1)
                    mix(nb, 7, MIX_BANKS[7])
                    pe.wait_ge(X3_ok, b + 1)
                    turn(7, X, X3T_ps)
                    pe.wait_ge(X3T_ok, b + 1)
                    pe.wait_ge(abs2_ok, at(nb, KN, 8))
                    for m_ in range(MT + 2):
                        if m_ < MT:
                            if m_ >= 4:
                                pe.wait_ge(hid_ok, at(b, MT, m_ - 3))
                            for part in range(2):
                                for kt in range(NT):
                                    c0 = part * HID + m_ * P
                                    m = nc.tensor.matmul(ps[m_ % 4][:, part * C:(part + 1) * C],
                                                         w_gu[:, kt, c0:c0 + P], XT[:, kt, :],
                                                         start=(kt == 0), stop=(kt == 1))
                            m.then_inc(gu_ps, 1)
                        k_ = m_ - 2
                        if k_ >= 0:
                            pe.wait_ge(hid_ok, at(b, MT, k_ + 1))
                            for tt in range(NT):
                                m = nc.tensor.matmul(ps[6 + tt][:, 0:L], hid[:, k_, tt * P:(tt + 1) * P],
                                                     w_down[:, k_, :], start=(k_ == 0), stop=(k_ == MT - 1))
                    m.then_inc(down_ps, 1)

            @block.vector
            def _(dve):
                def gain(m, batch):
                    nc.vector.tensor_copy(qgs[:], qg[:, :, bass.ds(batch, 1)]).then_inc(qgs_ok, 1)

                def gain_out(m):
                    dve.wait_ge(QGB_ps, m + 1)
                    nc.vector.tensor_copy(QGB[:], ps[5][:, 0:L]).then_inc(QGB_ok, 1)

                def scores_of(m, i):
                    dve.wait_ge(o2_ok, at(m, KN, i + 1))
                    if i == 0:
                        dve.wait_ge(QGB_ok, m + 1)
                    for ct in range(NT):
                        if i >= 1:
                            dve.wait_ge(dot_ok, at(m, NT * KN, NT * (i - 1) + ct + 1))
                        nc.vector.tensor_tensor_reduce(dead[:, ct], o2[:, i, ct, :], QGB[:], 1.0, 0.0, ALU.mult,
                                                       ALU.add, score[:, ct, i:i + 1]).then_inc(dot_ok, 1)

                def scores_max(m):
                    dve.wait_ge(dot_ok, at(m, NT * KN, NT * KN))
                    nc.vector.tensor_reduce(smax[:], score[:], AX.X, ALU.max, negate=True).then_inc(score_ok, 1)

                def weigh(m, i):
                    if i == 0:
                        dve.wait_ge(sexp_ok, m + 1)
                        nc.vector.reciprocal(srec[:], ssum[:]).then_inc(wsum_ok, 1)
                    for ct in range(NT):
                        if i == 0:
                            nc.vector.tensor_scalar(tok0[:, ct, :], o2[:, 0, ct, :], score[:, ct, 0:1], None,
                                                    ALU.mult).then_inc(wsum_ok, 1)
                        else:
                            dve.wait_ge(wsum_ok, at(m, 19, NT * i + ct))
                            nc.vector.scalar_tensor_tensor(out=tok0[:, ct, :], in0=o2[:, i, ct, :],
                                                           scalar=score[:, ct, i:i + 1], in1=tok0[:, ct, :],
                                                           op0=ALU.mult, op1=ALU.add).then_inc(wsum_ok, 1)

                def normalise(m):
                    for ct in range(NT):
                        dve.wait_ge(wsum_ok, at(m, 19, 16 + ct))
                        nc.vector.scalar_tensor_tensor(out=tok0[:, ct, :], in0=tok0[:, ct, :],
                                                       scalar=srec[:, ct:ct + 1], in1=RG[:],
                                                       op0=ALU.mult, op1=ALU.mult).then_inc(wsum_ok, 1)
                    dve.wait_ge(wsum_ok, at(m, 19, 19))
                    nc.vector.tensor_tensor(tok0[:], tok0[:], BP[:].unsqueeze(1).broadcast_to([P, NT, L]),
                                            ALU.add).then_inc(tok0_ok, 1)

                def first_norm(m):
                    dve.wait_ge(rs_ok[1], m + 1)
                    for tt in range(NT):
                        v = nc.vector.tensor_scalar(X[:, tt, :], tok0[:, tt, :], rstd[:, 1, tt:tt + 1], None, ALU.mult)
                    v.then_inc(X1_ok, 1)

                def heads(view, w=HD):
                    return view.rearrange("p (h e) -> p h e", e=w)

                def kv_out(b, tt):
                    dve.wait_ge(kv_ps, at(b, 2, tt + 1))
                    nc.vector.scalar_tensor_tensor(
                        out=QP[:, tt, H:2 * H, 0:HD], in0=heads(ps[tt][:, 0:L]), scalar=rstd[:, 0, tt:tt + 1],
                        in1=heads(b_min[:, L:2 * L]), op0=ALU.mult, op1=ALU.add)
                    nc.vector.scalar_tensor_tensor(
                        out=heads(VP[1][:, tt, 0:H * VW], VW)[:, :, 0:HD], in0=heads(ps[tt][:, L:2 * L]),
                        scalar=rstd[:, 0, tt:tt + 1], in1=heads(b_min[:, 2 * L:3 * L]),
                        op0=ALU.mult, op1=ALU.add).then_inc(kv_ok, 1)

                def attention(b, a, between):
                    for n in range(H + 5):
                        if n < H:
                            dve.wait_ge(S_ps, at(b, NH, a * H + n + 1))
                            nc.vector.tensor_reduce(nmax[:, n % 4, :], ps[n % 4][:].rearrange("p (t k) -> p t k", t=NT),
                                                    AX.X, ALU.max, negate=True).then_inc(max_ok, 1)
                        h = n - 2
                        if 0 <= h < H:
                            dve.wait_ge(PrT_ps, at(b, NH, a * H + h + 1))
                            if h >= 2:
                                dve.wait_ge(O_ps, at(b, NH, a * H + h - 1))
                            nc.vector.tensor_copy(PrT[:, h % 2], ps[4 + h % 2][:]).then_inc(PrT_ok, 1)
                        if n in (10, 14, 18, 20):
                            g4 = 3 if n == 20 else (n - 10) // 4
                            k_ = at(b, 8, 4 * a + g4 + 1)
                            dve.wait_ge(Og_ps, k_)
                            og = ps[6 + g4 % 2][:, C:2 * C].rearrange("p (n e) -> p n e", e=HP)
                            nc.vector.reciprocal(orec[:, g4, :], og[:, :, ONE_COL]).then_inc(div_ok, 1)
                            dve.wait_ge(div_ok, k_)
                            for qt in range(NT):
                                v = nc.vector.tensor_tensor(
                                    heads(O[:, qt, g4 * 4 * HD:(g4 + 1) * 4 * HD]), og[:, 4 * qt:4 * qt + 4, 0:HD],
                                    orec[:, g4, 4 * qt:4 * qt + 4].unsqueeze(2).broadcast_to([P, 4, HD]), ALU.mult)
                            v.then_inc(O_ok, 1)
                        between(n)

                dve.sem_inc(out_done, 16)
                dve.sem_inc(res_ok, 1)
                gain(0, 0)
                gain_out(0)
                for i in range(KN):
                    scores_of(0, i)
                scores_max(0)
                for i in range(KN):
                    weigh(0, i)
                normalise(0)
                first_norm(0)

                dve.wait_ge(pads_ok, 4)
                dve.wait_ge(rope_in, 32)
                with dve.Fori(0, B) as b:
                    nb = b + 1
                    gain(nb, after(b))
                    nc.vector.tensor_scalar(mobv[:], b_mout[:], vrow[:, bass.ds(b, 1)], None, ALU.mult).then_inc(mobv_ok, 1)

                    for tt in range(NT):
                        dve.wait_ge(qkv_ps, at(b, 4, 2 * tt + 1))
                        nc.vector.tensor_tensor(QK[:, tt, :], ps[2 * tt][:], b_qkv[:, 0:2 * L], ALU.add).then_inc(qk_ok, 1)
                        dve.wait_ge(qkv_ps, at(b, 4, 2 * tt + 2))
                        nc.vector.tensor_tensor(heads(VP[0][:, tt, 0:H * VW], VW)[:, :, 0:HD],
                                                heads(ps[2 * tt + 1][:, 0:L]), heads(b_qkv[:, 2 * L:3 * L]),
                                                ALU.add).then_inc(v_ok, 1)
                    gain_out(nb)
                    for tt in range(NT):
                        dve.wait_ge(qk_ok, at(b, 2, tt + 1))
                        dve.wait_ge(rsin_ok, at(b, 2, tt + 1))
                        nc.vector.tensor_tensor(QK[:, tt, :], QK[:, tt, :], rope_cos[:, tt, :], ALU.mult).then_inc(rcos_ok, 1)
                        dve.wait_ge(rcos_ok, at(b, 2, tt + 1))
                        nc.vector.tensor_tensor(QP[:, tt, :, 0:HD], heads(QK[:, tt, :]), heads(QKr[:, tt, :]),
                                                ALU.add).then_inc(qp_ok, 1)

                    def self_between(n):
                        if n in (7, 9, 11):
                            scores_of(nb, (n - 7) // 2)
                    attention(b, 0, self_between)
                    dve.wait_ge(rs_ok[0], b + 1)
                    kv_out(b, 0)
                    dve.wait_ge(tok0b_ok, b + 1)
                    dve.wait_ge(att_ps, b + 1)
                    nc.vector.tensor_tensor(tok1[:], ps[2][:], tok0b[:], ALU.add).then_inc(tok1_ok, 1)
                    kv_out(b, 1)

                    dve.wait_ge(tok1T_ok, b + 1)
                    for ft in range(NT):
                        v = nc.vector.tensor_scalar(XT[:, ft, :], tok1T[:, ft, :], n_sq[:, ft:ft + 1], None, ALU.mult)
                    v.then_inc(X2T_ok, 1)
                    dve.wait_ge(rs_ok[2], b + 1)
                    nc.vector.tensor_scalar(rq[:], rstd[:, 2], HD ** -0.5, None, ALU.mult).then_inc(step2, 1)
                    dve.wait_ge(step2, at(b, 2, 1))
                    dve.wait_ge(cq_ps, b + 1)
                    for tt in range(NT):
                        v = nc.vector.scalar_tensor_tensor(
                            out=QP[:, tt, 0:H, 0:HD], in0=heads(ps[2][:, tt * L:(tt + 1) * L]),
                            scalar=rq[:, tt:tt + 1], in1=heads(b_min[:, 0:L]), op0=ALU.mult, op1=ALU.add)
                    v.then_inc(cq_ok, 1)

                    def cross_between(n):
                        if n in (5, 7, 9):
                            scores_of(nb, (n - 5) // 2 + 3)
                    attention(b, 1, cross_between)
                    dve.wait_ge(upd_ps, b + 1)
                    dve.wait_ge(mobv_ok, b + 1)
                    for tt in range(NT):
                        v = nc.vector.scalar_tensor_tensor(out=upd[:, tt, :], in0=ps[2][:, tt * L:(tt + 1) * L],
                                                           scalar=vrow[:, bass.ds(b, 1)], in1=mobv[:],
                                                           op0=ALU.mult, op1=ALU.add)
                    v.then_inc(upd_ok, 1)
                    scores_of(nb, 6)
                    dve.wait_ge(gate_ps, b + 1)
                    nc.vector.tensor_tensor(z[:], ps[3][:].rearrange("p (t l) -> p t l", t=NT),
                                            b_gate[:].unsqueeze(1).broadcast_to([P, NT, L]), ALU.add).then_inc(z_ok, 1)
                    dve.wait_ge(zt_ok, b + 1)
                    nc.vector.scalar_tensor_tensor(out=z[:], in0=z[:], scalar=1.0, in1=upd[:],
                                                   op0=ALU.add, op1=ALU.mult).then_inc(step2, 1)
                    dve.wait_ge(step2, at(b, 2, 2))
                    nc.vector.scalar_tensor_tensor(out=tok2[:], in0=z[:], scalar=0.5, in1=tok1[:],
                                                   op0=ALU.mult, op1=ALU.add).then_inc(tok2_ok, 1)

                    scores_of(nb, 7)
                    scores_max(nb)
                    dve.wait_ge(rs_ok[3], b + 1)
                    dve.wait_ge(tok2_ok, b + 1)
                    for tt in range(NT):
                        v = nc.vector.tensor_scalar(X[:, tt, :], tok2[:, tt, :], rstd[:, 3, tt:tt + 1], None, ALU.mult)
                    v.then_inc(X3_ok, 1)
                    for m in range(MT):
                        dve.wait_ge(act_ok, at(b, MT, m + 1))
                        nc.vector.scalar_tensor_tensor(out=th[:, m % 2, :], in0=th[:, m % 2, :], scalar=1.0,
                                                       in1=val[:, m % 2, :], op0=ALU.add, op1=ALU.mult).then_inc(prod2_ok, 1)
                        dve.wait_ge(prod2_ok, at(b, MT, m + 1))
                        nc.vector.scalar_tensor_tensor(out=hid[:, m, :], in0=ps[m % 4][:, 0:C], scalar=b_gu[:, m:m + 1],
                                                       in1=th[:, m % 2, :], op0=ALU.add, op1=ALU.mult).then_inc(hid_ok, 1)
                        if 1 <= m <= 4:
                            weigh(nb, 2 * m - 2)
                            weigh(nb, 2 * m - 1)
                        if m == 5:
                            normalise(nb)
                    first_norm(nb)
                    dve.wait_ge(tok2b_ok, b + 1)
                    dve.wait_ge(down_ps, b + 1)
                    dve.wait_ge(out_done, at(b, 16, 16))
                    for tt in range(NT):
                        v = nc.vector.tensor_tensor(res[:, tt, :], ps[6 + tt][:, 0:L], tok2b[:, tt, :], ALU.add)
                    v.then_inc(res_ok, 1)


_PLAIN = {"x": "x", "cond": "cond_1024", "fside": "fside_BxSxS_0", "sigmas": "L0_cond_sigmas",
          "centers": "L0_cond_center_shift", "gamma": "L0_cond_gamma", "beta": "L0_cond_beta",
          "attn_norm_w": "L1_cond_attn_norm_w", "qkv_b": "L1_cond_qkv_b", "out_b": "L1_cond_out_b",
          "film_b": "L1_cond_film_b", "sq_norm_w": "L1_cond_sq_norm_w", "s_norm_w": "L1_cond_s_norm_w",
          "mha_in_b": "L1_cond_mha_in_b", "mha_out_b": "L1_cond_mha_out_b", "gate_b": "L1_cond_gate_b",
          "ffn_norm_w": "L1_cond_ffn_norm_w", "gu_b": "L1_cond_gu_b", "down_b": "L1_cond_down_b"}
_COLUMNS = ("gamma", "beta", "attn_norm_w", "film_b", "gu_b", "sq_norm_w", "s_norm_w", "ffn_norm_w")
_TURNED = {"qkv_wT": "L1_cond_qkv_w", "out_wT": "L1_cond_out_w", "film_wT": "L1_cond_film_w",
           "mha_in_wT": "L1_cond_mha_in_w", "mha_out_wT": "L1_cond_mha_out_w",
           "gate_wT": "L1_cond_gate_w", "gu_wT": "L1_cond_gu_w", "down_wT": "L1_cond_down_w"}


def kernel(**inputs):
    import numpy as _np
    import concourse.bacc as _bacc
    from concourse import mybir as _mybir
    from concourse.bass_utils import run_bass_kernel_spmd as _run

    nc = _bacc.Bacc("TRN2", target_bir_lowering=False, num_devices=1)
    arrays = {n: _np.ascontiguousarray(inputs[s]) for n, s in _PLAIN.items()}
    arrays.update({n: _np.ascontiguousarray(_np.asarray(inputs[s]).T) for n, s in _TURNED.items()})
    for n in _COLUMNS:
        arrays[n] = _np.ascontiguousarray(arrays[n].reshape(-1, P).T)
    arrays["mask"] = _np.ascontiguousarray(inputs["mask_BxS_bk0"])
    arrays.update(shape_tables())
    feed, d = {}, {}
    for n, a in arrays.items():
        feed[f"in_{n}"] = a
        d[n] = nc.dram_tensor(f"in_{n}", a.shape, _mybir.dt.from_np(a.dtype), kind="ExternalInput").ap()
    out = nc.dram_tensor("out_dram", (B, C, L), _mybir.dt.float32, kind="ExternalOutput").ap()
    build(nc, d, out)
    r = _run(nc, [feed], core_ids=[0])
    return r.results[0]["out_dram"]
```

```python
import math
from contextlib import ExitStack

import numpy as np
import concourse.bass as bass
from concourse import mybir

F32 = mybir.dt.float32
U8 = mybir.dt.uint8
ALU = mybir.AluOpType
ACT = mybir.ActivationFunctionType
AX = mybir.AxisListType

P = 128
B = 16
L = 256
C = 256
KN = 8
TAPS = 15
NT = 2
H = 16
HD = 16
HP = 32
HID = 1024
MT = HID // P
NPAIR = KN // 2
BN_EPS = 1e-5
RMS_EPS = 1e-6
NEG = -1e30
ONE_COL, VW = 16, 17


def shape_tables():
    l = np.arange(L)
    F = np.zeros((L, L))
    k = np.arange(P)
    F[:P] = np.cos(2 * np.pi * ((k[:, None] * l[None]) % L) / L) * math.sqrt(2.0 / L)
    F[0] = math.sqrt(1.0 / L)
    F[P] = np.where(l % 2, -1.0, 1.0) * math.sqrt(1.0 / L)
    F[P + 1:] = np.sin(2 * np.pi * ((k[1:, None] * l[None]) % L) / L) * math.sqrt(2.0 / L)
    W = np.zeros((L, L))
    kk = np.arange(P + 1)
    W[:, :P + 1] = np.cos(2 * np.pi * ((l[:, None] * kk[None]) % L) / L)
    W[:, P + 1:] = np.sin(2 * np.pi * ((l[:, None] * kk[None, 1:P]) % L) / L)
    taps = np.broadcast_to(np.linspace(-7.0, 7.0, TAPS), (P, TAPS))
    avg = np.kron(np.eye(KN), np.full((B, B), 1.0 / B))
    pos = np.arange(C, dtype=np.float32)[:, None]
    freq = np.exp(np.arange(0, HD, 2, dtype=np.float32) * np.float32(-math.log(10000.0) / HD))
    ang = (pos * freq[None]).astype(np.float32)
    cos, sin = np.cos(ang), np.sin(ang)
    c16 = np.repeat(cos, 2, axis=1)
    s16 = np.stack((-sin, sin), axis=-1).reshape(C, HD)

    def rope(t):
        return np.concatenate([np.tile(t, (1, H)) * 0.25, np.tile(t, (1, H))], axis=1)

    out = {"t_F": F, "t_FT": F.T, "t_W": W, "t_taps": taps, "t_avg": avg, "t_eye": np.eye(P),
           "t_cos": rope(c16), "t_sin": rope(s16)}
    return {n: np.ascontiguousarray(a.astype(np.float32)) for n, a in out.items()}


def tiles(v):
    return v.rearrange("(t p) n -> p t n", p=P)


def at(b, per, n):
    return b * per + n


def build(nc, d, out):
    with ExitStack() as ctx:
        ps = [ctx.enter_context(nc.psum_tensor(f"bank{i}", [P, 512], F32)) for i in range(8)]

        def sb(name, shape, dt=F32):
            return ctx.enter_context(nc.sbuf_tensor(name, shape, dt))

        def sem(name):
            return ctx.enter_context(nc.semaphore(name))

        D = sb("D", [P, B, NT, C])
        Fm = sb("Fm", [P, NT, L])
        eye = sb("eye", [P, P])
        wT = sb("wT", [P, NT, KN, B])
        QR = sb("QR", [P, NT, B])
        qg = sb("qg", [P, NT, B])
        RG = sb("RG", [P, L])
        BP = sb("BP", [P, L])
        filmG = sb("filmG", [P, NT, B])
        filmS = sb("filmS", [P, NT, B])
        keybias = sb("keybias", [P, NT, B])
        vrow = sb("vrow", [P, B])
        w_qkv = sb("w_qkv", [P, NT, 3 * L])
        w_out = sb("w_out", [P, NT, L])
        w_min = sb("w_min", [P, NT, 3 * L])
        w_mout = sb("w_mout", [P, NT, L])
        w_gate = sb("w_gate", [P, 4, L])
        w_gu = sb("w_gu", [P, NT, 2 * HID])
        w_down = sb("w_down", [P, MT, L])
        b_qkv = sb("b_qkv", [P, 3 * L])
        b_out = sb("b_out", [P, L])
        b_min = sb("b_min", [P, 3 * L])
        b_mout = sb("b_mout", [P, L])
        b_gate = sb("b_gate", [P, L])
        b_gu = sb("b_gu", [P, 2 * MT])
        b_guh = sb("b_guh", [P, 2 * MT])
        b_down = sb("b_down", [P, L])
        n_sq = sb("n_sq", [P, NT])
        n_s = sb("n_s", [P, NT])
        n_ffn = sb("n_ffn", [P, NT])
        mhalf = sb("mhalf", [P, NT])

        weights_in = sem("weights_in")
        layer1 = [(w_qkv[:], tiles(d["qkv_wT"])), (w_out[:], tiles(d["out_wT"])),
                  (w_min[:], tiles(d["mha_in_wT"])), (w_mout[:], tiles(d["mha_out_wT"])),
                  (w_gate[:], tiles(d["gate_wT"])), (w_gu[:], tiles(d["gu_wT"])),
                  (w_down[:], tiles(d["down_wT"])),
                  (b_qkv[:], d["qkv_b"].partition_broadcast(P)), (b_out[:], d["out_b"].partition_broadcast(P)),
                  (b_min[:], d["mha_in_b"].partition_broadcast(P)), (b_mout[:], d["mha_out_b"].partition_broadcast(P)),
                  (b_gate[:], d["gate_b"].partition_broadcast(P)), (b_down[:], d["down_b"].partition_broadcast(P)),
                  (b_gu[:], d["gu_b"]), (n_sq[:], d["sq_norm_w"]),
                  (n_s[:], d["s_norm_w"]), (n_ffn[:], d["ffn_norm_w"])]

        with ExitStack() as first_ctx:
            def sb1(name, shape, dt=F32):
                return first_ctx.enter_context(nc.sbuf_tensor(name, shape, dt))

            def sem1(name):
                return first_ctx.enter_context(nc.semaphore(name))

            FT = sb1("FT", [P, NT, L])
            Wt = sb1("Wt", [P, NT, L])
            taps = sb1("taps", [P, TAPS])
            avg = sb1("avg", [P, P])
            q16 = sb1("q16", [B, L])
            m8 = sb1("m8", [B, C], U8)
            sig = sb1("sig", [P, 1])
            cen = sb1("cen", [P, 1])
            gamma = sb1("gamma", [P, NT])
            beta = sb1("beta", [P, NT])
            n_attn = sb1("n_attn", [P, NT])
            filmW = sb1("filmW", [P, NT, 2 * L])
            filmB = sb1("filmB", [P, 4])
            xb = sb1("xb", [P, 2, NT, L])
            xT = sb1("xT", [P, B, NT, C])
            csum = sb1("csum", [P, NT, B])
            qT = sb1("qT", [P, NT, B])
            sT8 = sb1("sT8", [P, NT, KN, B])
            qT8 = sb1("qT8", [P, NT, KN, B])
            spad = sb1("spad", [P, L + TAPS - 1])
            g = sb1("g", [P, TAPS])
            gs = sb1("gs", [P, 8])
            blur = sb1("blur", [P, L])
            blurT = sb1("blurT", [P, NT, P])
            V = sb1("V", [P, L])
            QV = sb1("QV", [P, L])
            qy = sb1("qy", [P, L])
            at0 = sb1("at0", [P, 2])
            means = sb1("means", [P, 2])
            tot = sb1("tot", [P, 8])
            w = sb1("w", [P, P + 1])
            w_hi = sb1("w_hi", [P, P])
            half = sb1("half", [P, P + 1])
            mf = sb1("mf", [B, C])
            allpad = sb1("allpad", [B, 2])
            film = sb1("film", [P, 2, NT, B])
            E = sb1("E", [P, 2, NT, 2, C])
            o = sb1("o", [P, 4, 2, C])
            sums = sb1("sums", [P, NT, B * NPAIR])
            squares = sb1("squares", [P, NT, B * NPAIR])
            st = sb1("st", [P, 8, NT])

            tables_in = sem1("tables_in")
            x_in = [sem1(f"x_in{i}") for i in range(2)]
            xT_ps, xT_sb, blur_in = sem1("xT_ps"), sem1("xT_sb"), sem1("blur_in")
            D_ps, D_sb = sem1("D_ps"), sem1("D_sb")
            consts = sem1("consts")
            q_ps, q_sb, qr_ps, qr_sb = sem1("q_ps"), sem1("q_sb"), sem1("qr_ps"), sem1("qr_sb")
            film_ps, film_th = sem1("film_ps"), sem1("film_th")
            mask_ok, maskT_ps, maskT_sb = sem1("mask_ok"), sem1("maskT_ps"), sem1("maskT_sb")
            q8_sb, s_sb, sb_ps = sem1("q8_sb"), sem1("s_sb"), sem1("sb_ps")
            step = sem1("step")
            gz_ok, ge_ok = sem1("gz_ok"), sem1("ge_ok")
            blur_ok, blurT_ps, blurT_sb = sem1("blur_ok"), sem1("blurT_ps"), sem1("blurT_sb")
            V_ps, at0_ok, mean_ps = sem1("V_ps"), sem1("at0_ok"), sem1("mean_ps")
            prod_ok, root_ok, th_ok = sem1("prod_ok"), sem1("root_ok"), sem1("th_ok")
            w_ok, wT_ps, wT_sb = sem1("w_ok"), sem1("wT_ps"), sem1("wT_sb")
            E_ok = sem1("E_ok")
            y_ps, o_ok = sem1("y_ps"), sem1("o_ok")
            abs_ok, o_free = sem1("abs_ok"), sem1("o_free")
            var_ok, rstd_ok, bn_ok, bn_ps = sem1("var_ok"), sem1("rstd_ok"), sem1("bn_ok"), sem1("bn_ps")

            small = [(q16[:], d["cond"]), (eye[:], d["t_eye"]), (FT[:], tiles(d["t_FT"])),
                     (Fm[:], tiles(d["t_F"])), (Wt[:], tiles(d["t_W"])), (taps[:], d["t_taps"]),
                     (avg[:], d["t_avg"]), (m8[:], d["mask"]),
                     (gamma[:], d["gamma"]), (beta[:], d["beta"]),
                     (n_attn[:], d["attn_norm_w"]), (filmW[:], tiles(d["film_wT"])),
                     (filmB[:], d["film_b"])]
            ALL_TABLES = 16 * len(small)

            block = first_ctx.enter_context(nc.Block())

            @block.sync
            def _(sp):
                for dst, src in small[0::2]:
                    sp.dma_start(dst, src).then_inc(tables_in, 16)
                for s in range(2):
                    sp.dma_start(xb[:, s], tiles(d["x"][s])).then_inc(x_in[s], 16)
                with sp.Fori(0, B // 2 - 1) as two:
                    for s in range(2):
                        sp.wait_ge(xT_ps, two * 2 + s + 1)
                        sp.dma_start(xb[:, s], tiles(d["x"][two * 2 + (s + 2)])).then_inc(x_in[s], 16)

            @block.gpsimd
            def _(pool):
                for i in range(KN):
                    pool.dma_start(sig[i * B:(i + 1) * B, :],
                                   d["sigmas"][i].partition_broadcast(B)).then_inc(blur_in, 16)
                    pool.dma_start(cen[i * B:(i + 1) * B, :],
                                   d["centers"][i].partition_broadcast(B)).then_inc(blur_in, 16)
                nc.gpsimd.memset(mhalf[:], -0.5).then_inc(consts, 1)
                pool.wait_ge(xT_ps, B)
                for dst, src in layer1:
                    pool.dma_start(dst, src).then_inc(weights_in, 16)

                pool.wait_ge(var_ok, 1)
                pool.wait_ge(consts, 1)
                nc.gpsimd.tensor_tensor(st[:, 4, :], st[:, 3, :], mhalf[:], ALU.pow).then_inc(rstd_ok, 1)

            @block.scalar
            def _(act):
                for dst, src in small[1::2]:
                    act.dma_start(dst, src).then_inc(tables_in, 16)
                act.wait_ge(tables_in, ALL_TABLES)
                act.wait_ge(film_ps, 1)
                for ft in range(NT):
                    nc.scalar.activation(film[:, 0, ft, :], ps[6][:, ft * B:(ft + 1) * B], ACT.Tanh,
                                         bias=filmB[:, ft:ft + 1]).then_inc(film_th, 1)
                for ft in range(NT):
                    a = nc.scalar.activation(filmS[:, ft, :], ps[6][:, (2 + ft) * B:(3 + ft) * B], ACT.Identity,
                                             bias=filmB[:, 2 + ft:3 + ft])
                a.then_inc(film_th, 1)

                act.wait_ge(gz_ok, 1)
                nc.scalar.activation(g[:], g[:], ACT.Exp, scale=-0.5, accum_out=gs[:, 3:4]).then_inc(ge_ok, 1)
                with act.Fori(0, B // 2) as two:
                    for s in range(2):
                        act.wait_ge(xT_ps, two * 2 + s + 1)
                        for lt in range(NT):
                            nc.scalar.activation(xT[:, bass.ds(two * 2 + s, 1), lt, :], ps[s][:, lt * C:(lt + 1) * C], ACT.Copy,
                                                 accum_out=csum[:, lt, bass.ds(two * 2 + s, 1)]).then_inc(xT_sb, 1)
                act.wait_ge(prod_ok, 1)
                nc.scalar.activation(w[:], w[:], ACT.Sqrt).then_inc(root_ok, 1)
                act.wait_ge(root_ok, 1)
                nc.scalar.activation(w[:], w[:], ACT.Tanh, scale=0.05).then_inc(th_ok, 1)

                with act.Fori(0, B) as b:
                    for n in range(2 * NPAIR + 1):
                        if n < 2 * NPAIR:
                            act.wait_ge(y_ps, at(b, 8, n + 1) + 4)
                            act.wait_ge(o_free, at(b, 8, n + 1))
                            nc.scalar.activation(o[:, n % 4], ps[n % 4][:], ACT.Abs).then_inc(abs_ok, 1)
                        if n >= 1:
                            act.wait_ge(o_ok, at(b, 8, n))
                            nc.scalar.activation(
                                o[:, (n - 1) % 4], o[:, (n - 1) % 4], ACT.Square,
                                accum_out=squares[:, (n - 1) % 2, bass.ds(b * NPAIR + (n - 1) // 2, 1)]).then_inc(o_free, 1)

            @block.tensor
            def _(pe):
                pe.wait_ge(tables_in, ALL_TABLES)
                for lt in range(NT):
                    m = nc.tensor.transpose(ps[7][:, lt * B:(lt + 1) * B], q16[:, lt * P:(lt + 1) * P], eye[0:B, 0:B])
                m.then_inc(q_ps, 1)
                pe.wait_ge(mask_ok, 1)
                for t in range(NT):
                    m = nc.tensor.transpose(ps[5][:, t * B:(t + 1) * B], mf[:, t * P:(t + 1) * P], eye[0:B, 0:B])
                m = nc.tensor.matmul(ps[5][:, 2 * B:3 * B], allpad[:, 1:2].broadcast_to([B, P]), eye[0:B, 0:B],
                                     start=True, stop=True)
                m.then_inc(maskT_ps, 1)
                pe.wait_ge(q_sb, 1)
                for mt in range(4):
                    for kt in range(NT):
                        m = nc.tensor.matmul(ps[6][:, mt * B:(mt + 1) * B], filmW[:, kt, mt * P:(mt + 1) * P],
                                             qT[:, kt, :], start=(kt == 0), stop=(kt == 1))
                m.then_inc(film_ps, 1)
                for rt in range(NT):
                    for kt in range(NT):
                        m = nc.tensor.matmul(ps[4][:, rt * B:(rt + 1) * B], FT[:, kt, rt * P:(rt + 1) * P],
                                             qT[:, kt, :], start=(kt == 0), stop=(kt == 1))
                m.then_inc(qr_ps, 1)

                pe.wait_ge(q8_sb, 1)
                for lt in range(NT):
                    m = nc.tensor.matmul(ps[6][:, 256:256 + L], qT8[:, lt].rearrange("p i b -> p (i b)"),
                                         Wt[:, lt, :], start=(lt == 0), stop=(lt == 1))
                m = nc.tensor.matmul(ps[7][:, 256:257], qT8[:, 0].rearrange("p i b -> p (i b)"), eye[:, 0:1],
                                     start=True, stop=True)
                m.then_inc(V_ps, 1)

                def turn_x(s, n, loads):
                    pe.wait_ge(x_in[s], loads * 16)
                    pe.wait_ge(xT_sb, n * 2)
                    for lt in range(NT):
                        for ct in range(NT):
                            m = nc.tensor.transpose(ps[s][:, lt * C + ct * P:lt * C + (ct + 1) * P],
                                                    xb[:, s, ct, lt * P:(lt + 1) * P], eye[:])
                    m.then_inc(xT_ps, 1)

                def spectrum_x(s, batch):
                    pe.wait_ge(xT_sb, batch * 2 + 6)
                    pe.wait_ge(D_sb, batch + 1)
                    for rt in range(NT):
                        for kt in range(NT):
                            m = nc.tensor.matmul(ps[2 + s][:, rt * C:(rt + 1) * C], FT[:, kt, rt * P:(rt + 1) * P],
                                                 xT[:, bass.ds(batch, 1), kt, :], start=(kt == 0), stop=(kt == 1))
                    m.then_inc(D_ps, 1)

                turn_x(0, 1, 1)
                with pe.Fori(0, B // 2 - 1) as two:
                    turn_x(1, two * 2 + 2, two + 1)
                    spectrum_x(0, two * 2)
                    turn_x(0, two * 2 + 3, two + 2)
                    spectrum_x(1, two * 2 + 1)
                turn_x(1, B, B // 2)
                spectrum_x(0, B - 2)
                spectrum_x(1, B - 1)
                pe.wait_ge(s_sb, 1)
                for lt in range(NT):
                    m = nc.tensor.matmul(ps[3][:, lt * P:(lt + 1) * P],
                                         sT8[:, lt].rearrange("p i b -> p (i b)"), eye[:],
                                         start=True, stop=True)
                m.then_inc(sb_ps, 1)
                pe.wait_ge(blur_ok, 1)
                for lt in range(NT):
                    m = nc.tensor.transpose(ps[4][:, lt * P:(lt + 1) * P], blur[:, lt * P:(lt + 1) * P], eye[:])
                m.then_inc(blurT_ps, 1)
                pe.wait_ge(blurT_sb, 1)
                for lt in range(NT):
                    m = nc.tensor.matmul(ps[5][:, 0:L], blurT[:, lt, :], Wt[:, lt, :], start=(lt == 0), stop=(lt == 1))
                m.then_inc(V_ps, 1)
                pe.wait_ge(at0_ok, 2)
                m = nc.tensor.matmul(ps[4][:, 0:2], avg[:], at0[:], start=True, stop=True)
                m.then_inc(mean_ps, 1)
                pe.wait_ge(w_ok, 3)
                nc.tensor.transpose(ps[3][:, 0:P], w[:, 0:P], eye[:])
                m = nc.tensor.transpose(ps[3][:, P:2 * P], w_hi[:], eye[:])
                m.then_inc(wT_ps, 1)

                pe.wait_ge(wT_sb, 2)
                with pe.Fori(0, B) as b:
                    for pr in range(NPAIR):
                        pe.wait_ge(E_ok, at(b, NPAIR, pr + 1))
                        for lt in range(NT):
                            pe.wait_ge(abs_ok, at(b, 8, 2 * pr + lt + 1))
                            for kt in range(NT):
                                m = nc.tensor.matmul(ps[(pr % 2) * 2 + lt][:], Fm[:, kt, lt * P:(lt + 1) * P],
                                                     E[:, pr % 2, kt, :, :], start=(kt == 0), stop=(kt == 1))
                            m.then_inc(y_ps, 1)

                pe.wait_ge(bn_ok, 2)
                for n in range(2):
                    for lt in range(NT):
                        m = nc.tensor.matmul(ps[4 + n][:, lt * P:(lt + 1) * P],
                                             st[:, 5 + n, lt:lt + 1].broadcast_to([P, P]), eye[:],
                                             start=True, stop=True)
                m.then_inc(bn_ps, 1)

            @block.vector
            def _(dve):
                n = [0]

                def link(ins):
                    n[0] += 1
                    ins.then_inc(step, 1)
                    dve.wait_ge(step, n[0])

                dve.sem_inc(D_sb, 2)
                dve.sem_inc(xT_sb, 4)
                dve.sem_inc(y_ps, 4)
                dve.sem_inc(abs_ok, 4)
                dve.sem_inc(o_free, 4)
                dve.wait_ge(tables_in, ALL_TABLES)
                link(nc.vector.tensor_copy(mf[:], m8[:]))
                link(nc.vector.tensor_reduce(allpad[:, 0:1], mf[:], AX.X, ALU.min))
                link(nc.vector.tensor_scalar(allpad[:, 1:2], allpad[:, 0:1], -1.0, 1.0, ALU.mult, ALU.add))
                nc.vector.tensor_scalar(mf[:], mf[:], allpad[:, 1:2], NEG, ALU.mult, ALU.mult).then_inc(mask_ok, 1)
                dve.wait_ge(q_ps, 1)
                nc.vector.tensor_copy(qT[:], ps[7][:, 0:2 * B]).then_inc(q_sb, 1)
                dve.wait_ge(maskT_ps, 1)
                nc.vector.tensor_copy(keybias[:], ps[5][:, 0:2 * B]).then_inc(maskT_sb, 1)
                nc.vector.tensor_copy(vrow[:], ps[5][:, 2 * B:3 * B]).then_inc(maskT_sb, 1)
                dve.wait_ge(qr_ps, 1)
                nc.vector.tensor_copy(QR[:], ps[4][:, 0:2 * B]).then_inc(qr_sb, 1)
                dve.wait_ge(film_th, 3)
                link(nc.vector.tensor_scalar(film[:, 1], film[:, 0], 0.1, 1.0, ALU.mult, ALU.add))
                for ft in range(NT):
                    nc.vector.tensor_scalar(filmG[:, ft, :], film[:, 1, ft, :], n_attn[:, ft:ft + 1], None, ALU.mult)
                dve.wait_ge(q_sb, 1)
                for lt in range(NT):
                    v = nc.vector.tensor_copy(qT8[:, lt], qT[:, lt, :].unsqueeze(1).broadcast_to([P, KN, B]))
                v.then_inc(q8_sb, 1)
                dve.wait_ge(blur_in, 16 * 2 * KN)
                link(nc.vector.tensor_scalar(gs[:, 0:1], sig[:], 0.001, None, ALU.add))
                link(nc.vector.reciprocal(gs[:, 1:2], gs[:, 0:1]))
                link(nc.vector.tensor_scalar(g[:], taps[:], cen[:, 0:1], gs[:, 1:2], ALU.subtract, ALU.mult))
                nc.vector.tensor_tensor(g[:], g[:], g[:], ALU.mult).then_inc(gz_ok, 1)
                dve.wait_ge(ge_ok, 1)
                link(nc.vector.tensor_scalar(gs[:, 4:5], gs[:, 3:4], 0.01, None, ALU.add))
                link(nc.vector.reciprocal(gs[:, 5:6], gs[:, 4:5]))
                link(nc.vector.tensor_scalar(g[:], g[:], gs[:, 5:6], None, ALU.mult))

                dve.wait_ge(qr_sb, 1)
                with dve.Fori(0, B // 2) as two:
                    for s in range(2):
                        dve.wait_ge(D_ps, two * 2 + s + 1)
                        for rt in range(NT):
                            v = nc.vector.tensor_scalar(D[:, bass.ds(two * 2 + s, 1), rt, :],
                                                        ps[2 + s][:, rt * C:(rt + 1) * C],
                                                        QR[:, rt, bass.ds(two * 2 + s, 1)], None, ALU.subtract)
                        v.then_inc(D_sb, 1)

                dve.wait_ge(xT_sb, 2 * B + 4)
                for lt in range(NT):
                    v = nc.vector.tensor_copy(sT8[:, lt], csum[:, lt, :].unsqueeze(1).broadcast_to([P, KN, B]))
                v.then_inc(s_sb, 1)
                dve.wait_ge(sb_ps, 1)
                half_k = TAPS // 2
                link(nc.vector.tensor_copy(spad[:, half_k:half_k + L], ps[3][:, 0:L]))
                nc.vector.tensor_copy(spad[:, 0:half_k], spad[:, half_k:half_k + 1].broadcast_to([P, half_k]))
                link(nc.vector.tensor_copy(spad[:, half_k + L:], spad[:, half_k + L - 1:half_k + L].broadcast_to([P, half_k])))
                link(nc.vector.tensor_scalar(blur[:], spad[:, 0:L], g[:, 0:1], None, ALU.mult))
                for t in range(1, TAPS):
                    v = nc.vector.scalar_tensor_tensor(out=blur[:], in0=spad[:, t:t + L], scalar=g[:, t:t + 1],
                                                       in1=blur[:], op0=ALU.mult, op1=ALU.add)
                    if t < TAPS - 1:
                        link(v)
                v.then_inc(blur_ok, 1)
                dve.wait_ge(blurT_ps, 1)
                nc.vector.tensor_copy(blurT[:], ps[4][:, 0:2 * P]).then_inc(blurT_sb, 1)
                dve.wait_ge(blur_ok, 1)
                nc.vector.tensor_copy(at0[:, 0:1], blur[:, 0:1]).then_inc(at0_ok, 1)
                dve.wait_ge(V_ps, 2)
                nc.vector.tensor_copy(at0[:, 1:2], ps[7][:, 256:257]).then_inc(at0_ok, 1)
                dve.wait_ge(mean_ps, 1)
                link(nc.vector.tensor_copy(means[:], ps[4][:, 0:2]))
                NC = P + 1
                nc.vector.tensor_scalar(V[:, 0:NC], ps[5][:, 0:NC], means[:, 0:1], None, ALU.subtract)
                nc.vector.tensor_copy(V[:, NC:L], ps[5][:, NC:L])
                nc.vector.tensor_scalar(QV[:, 0:NC], ps[6][:, 256:256 + NC], means[:, 0:1], None, ALU.subtract)
                nc.vector.tensor_copy(QV[:, NC:L], ps[6][:, 256 + NC:256 + L])
                link(nc.vector.tensor_scalar(qy[:, 0:NC], ps[6][:, 256:256 + NC], means[:, 1:2], None, ALU.subtract))
                nc.vector.tensor_tensor(V[:], V[:], V[:], ALU.mult)
                nc.vector.tensor_tensor(QV[:], QV[:], QV[:], ALU.mult)
                link(nc.vector.tensor_tensor(qy[:, 0:NC], qy[:, 0:NC], qy[:, 0:NC], ALU.mult))
                for m, z in enumerate((V, QV)):
                    nc.vector.tensor_reduce(tot[:, 4 * m:4 * m + 1], z[:, 1:P], AX.X, ALU.add)
                    nc.vector.tensor_reduce(tot[:, 4 * m + 1:4 * m + 2], z[:, NC:L], AX.X, ALU.add)
                    link(nc.vector.tensor_tensor(tot[:, 4 * m + 2:4 * m + 3], z[:, 0:1], z[:, P:NC], ALU.add))
                for m in range(2):
                    link(nc.vector.tensor_tensor(tot[:, 4 * m:4 * m + 1], tot[:, 4 * m:4 * m + 1],
                                                 tot[:, 4 * m + 1:4 * m + 2], ALU.subtract))
                    link(nc.vector.scalar_tensor_tensor(out=tot[:, 4 * m + 3:4 * m + 4], in0=tot[:, 4 * m:4 * m + 1],
                                                        scalar=2.0, in1=tot[:, 4 * m + 2:4 * m + 3],
                                                        op0=ALU.mult, op1=ALU.add))
                link(nc.vector.tensor_tensor(gs[:, 6:7], tot[:, 3:4], tot[:, 7:8], ALU.mult))
                link(nc.vector.tensor_scalar(gs[:, 6:7], gs[:, 6:7], 0.001, None, ALU.add))
                link(nc.vector.reciprocal(gs[:, 7:8], gs[:, 6:7]))
                nc.vector.tensor_tensor(V[:, 1:P], V[:, 1:P], V[:, NC:L], ALU.add)
                link(nc.vector.tensor_tensor(qy[:, 1:P], qy[:, 1:P], QV[:, NC:L], ALU.add))
                nc.vector.tensor_scalar(V[:, 0:NC], V[:, 0:NC], gs[:, 7:8], None, ALU.mult)
                link(nc.vector.tensor_scalar(qy[:, 0:NC], qy[:, 0:NC], gs[:, 7:8], None, ALU.mult))
                nc.vector.tensor_tensor(w[:], V[:, 0:NC], qy[:, 0:NC], ALU.mult).then_inc(prod_ok, 1)
                dve.wait_ge(th_ok, 1)
                link(nc.vector.tensor_scalar(half[:], w[:], 1.0, None, ALU.add))
                link(nc.vector.reciprocal(V[:, 0:NC], half[:]))
                nc.vector.scalar_tensor_tensor(out=w[:], in0=w[:], scalar=2.0, in1=V[:, 0:NC],
                                               op0=ALU.mult, op1=ALU.mult).then_inc(w_ok, 1)
                dve.wait_ge(w_ok, 1)
                nc.vector.tensor_copy(w_hi[:, 0:1], w[:, P:P + 1]).then_inc(w_ok, 1)
                nc.vector.tensor_copy(w_hi[:, 1:P], w[:, 1:P]).then_inc(w_ok, 1)
                dve.wait_ge(wT_ps, 1)
                nc.vector.tensor_copy(wT[:, 0], ps[3][:, 0:P]).then_inc(wT_sb, 1)
                nc.vector.tensor_copy(wT[:, 1], ps[3][:, P:2 * P]).then_inc(wT_sb, 1)

                dve.wait_ge(qr_sb, 1)
                dve.wait_ge(wT_sb, 2)
                dve.wait_ge(D_sb, B + 2)
                def spectrum(b, pr, batch):
                    dve.wait_ge(y_ps, at(b, 8, 2 * pr + 2))
                    for kt in range(NT):
                        for j in range(2):
                            e = nc.vector.tensor_scalar(
                                E[:, pr % 2, kt, j, :], D[:, bass.ds(batch, 1), kt, :],
                                wT[:, kt, 2 * pr + j, bass.ds(batch, 1)], QR[:, kt, bass.ds(batch, 1)],
                                ALU.mult, ALU.add)
                    e.then_inc(E_ok, 1)

                def turn(b, last=False):
                    for pr in range(NPAIR):
                        if pr < NPAIR - 1:
                            spectrum(b, pr + 1, b)
                        elif not last:
                            spectrum(b + 1, 0, b + 1)
                        for lt in range(NT):
                            slot = 2 * (pr % 2) + lt
                            dve.wait_ge(abs_ok, at(b, 8, 2 * pr + lt + 1) + 4)
                            nc.vector.scalar_tensor_tensor(
                                out=o[:, slot], in0=o[:, slot], scalar=1.0,
                                in1=xT[:, bass.ds(b, 1), lt, :].broadcast_to([P, 2, C]),
                                op0=ALU.mult, op1=ALU.add,
                                accum_out=sums[:, lt, bass.ds(b * NPAIR + pr, 1)]).then_inc(o_ok, 1)

                spectrum(0, 0, 0)
                with dve.Fori(0, B - 1) as b:
                    turn(b)
                turn(B - 1, last=True)
                dve.wait_ge(o_free, 4 + 8 * B)
                N = float(B * C * KN)
                nc.vector.tensor_reduce(st[:, 0, :], sums[:], AX.X, ALU.add)
                link(nc.vector.tensor_reduce(st[:, 1, :], squares[:], AX.X, ALU.add))
                nc.vector.tensor_scalar(st[:, 0, :], st[:, 0, :], 1.0 / N, None, ALU.mult)
                link(nc.vector.tensor_scalar(st[:, 1, :], st[:, 1, :], 1.0 / N, BN_EPS, ALU.mult, ALU.add))
                link(nc.vector.tensor_tensor(st[:, 2, :], st[:, 0, :], st[:, 0, :], ALU.mult))
                nc.vector.tensor_tensor(st[:, 3, :], st[:, 1, :], st[:, 2, :], ALU.subtract).then_inc(var_ok, 1)
                dve.wait_ge(rstd_ok, 1)
                nc.vector.tensor_tensor(st[:, 5, :], st[:, 4, :], gamma[:], ALU.mult).then_inc(bn_ok, 1)
                dve.wait_ge(bn_ok, 1)
                link(nc.vector.tensor_tensor(st[:, 7, :], st[:, 0, :], st[:, 5, :], ALU.mult))
                nc.vector.tensor_tensor(st[:, 6, :], beta[:], st[:, 7, :], ALU.subtract).then_inc(bn_ok, 1)
                for lt in range(NT):
                    nc.vector.tensor_scalar(qg[:, lt, :], qT[:, lt, :], st[:, 5, lt:lt + 1], None, ALU.mult)
                dve.wait_ge(bn_ps, 1)
                nc.vector.tensor_copy(RG[:], ps[4][:, 0:L])
                nc.vector.tensor_copy(BP[:], ps[5][:, 0:L])
                dve.wait_ge(weights_in, 16 * len(layer1))
                nc.vector.tensor_scalar(b_guh[:], b_gu[:], 0.5, None, ALU.mult)
                nc.vector.tensor_scalar(b_min[:, 0:L], b_min[:, 0:L], 0.25, None, ALU.mult)

        with ExitStack() as second_ctx:
            def sb2(name, shape, dt=F32):
                return second_ctx.enter_context(nc.sbuf_tensor(name, shape, dt))

            def sem2(name):
                return second_ctx.enter_context(nc.semaphore(name))

            rope_cos = sb2("rope_cos", [P, NT, 2 * L])
            rope_sin = sb2("rope_sin", [P, NT, 2 * L])
            x2 = sb2("x2", [P, NT, L])
            src = sb2("src", [P, NT, L])
            E2 = sb2("E2", [P, 4, NT, C])
            o2 = sb2("o2", [P, KN, NT, L])
            dead = sb2("dead", [P, NT, L])
            deadA = sb2("deadA", [P, NT, L])
            qgs = sb2("qgs", [P, NT])
            QGB = sb2("QGB", [P, L])
            score = sb2("score", [P, NT, KN])
            smax = sb2("smax", [P, NT])
            ssum = sb2("ssum", [P, NT])
            srec = sb2("srec", [P, NT])
            tok0 = sb2("tok0", [P, NT, L])
            tok0b = sb2("tok0b", [P, NT, L])
            tok1 = sb2("tok1", [P, NT, L])
            tok2 = sb2("tok2", [P, NT, L])
            tok2b = sb2("tok2b", [P, NT, L])
            X = sb2("X", [P, NT, L])
            XT = sb2("XT", [P, NT, C])
            srcT = sb2("srcT", [P, NT, C])
            tok1T = sb2("tok1T", [P, NT, C])
            updT = sb2("updT", [P, NT, C])
            upd = sb2("upd", [P, NT, L])
            z = sb2("z", [P, NT, L])
            res = sb2("res", [P, NT, L])
            ms = sb2("ms", [P, 4, NT])
            mse = sb2("mse", [P, 4, NT])
            rms_eps = sb2("rms_eps", [P, NT])
            rstd = sb2("rstd", [P, 4, NT])
            rq = sb2("rq", [P, NT])
            mobv = sb2("mobv", [P, L])
            QP = sb2("QP", [P, NT, 2 * H, HP])
            VP = [sb2(f"VP{a}", [P, NT, H * VW + HP - VW]) for a in range(2)]
            QKT = sb2("QKT", [P, 4, 2 * C])
            QK, QKr = QKT[:, 0:2, :], QKT[:, 2:4, :]
            hid = QKT[:].rearrange("p g (m c) -> p (g m) c", c=C)
            nmax = sb2("nmax", [P, 4, NT])
            Pr = sb2("Pr", [P, 2, NT, C])
            QKc = Pr[:].rearrange("p s t c -> p s (t c)")
            PrT = sb2("PrT", [P, 2, NT, C])
            Oh = sb2("Oh", [P, 2, C])
            orec = sb2("orec", [P, 4, NT * 4])
            O = sb2("O", [P, NT, L])
            OT = sb2("OT", [P, NT, C])
            th = sb2("th", [P, 2, C])
            val = sb2("val", [P, 2, C])

            rope_in, x2_in, src_in, out_done = sem2("rope_in"), sem2("x2_in"), sem2("src_in"), sem2("out_done")
            pads_ok, qgs_ok, QGB_ps, QGB_ok = sem2("pads_ok"), sem2("qgs_ok"), sem2("QGB_ps"), sem2("QGB_ok")
            E2_ok, y2_ps, abs2_ok, o2_ok = sem2("E2_ok"), sem2("y2_ps"), sem2("abs2_ok"), sem2("o2_ok")
            dot_ok, score_ok, sexp_ok = sem2("dot_ok"), sem2("score_ok"), sem2("sexp_ok")
            wsum_ok, tok0_ok = sem2("wsum_ok"), sem2("tok0_ok")
            step2 = sem2("step2")
            poolstep = sem2("poolstep")
            ms_ok = [sem2(f"ms_ok{i}") for i in range(4)]
            mse_ok = [sem2(f"mse_ok{i}") for i in range(4)]
            rs_ok = [sem2(f"rs_ok{i}") for i in range(4)]
            kb_ok, mobv_ok, tok0b_ok, tok2b_ok = sem2("kb_ok"), sem2("mobv_ok"), sem2("tok0b_ok"), sem2("tok2b_ok")
            srcT_ps, srcT_ok, kv_ps, kv_ok = sem2("srcT_ps"), sem2("srcT_ok"), sem2("kv_ps"), sem2("kv_ok")
            X1_ok, X1T_ps, X1T_ok = sem2("X1_ok"), sem2("X1T_ps"), sem2("X1T_ok")
            qkv_ps, qk_ok, v_ok, rsin_ok, rcos_ok, qp_ok = (sem2(n) for n in
                ("qkv_ps", "qk_ok", "v_ok", "rsin_ok", "rcos_ok", "qp_ok"))
            QKT_ps, QKT_ok = sem2("QKT_ps"), sem2("QKT_ok")
            S_ps, max_ok, Pr_ok, PrT_ps, PrT_ok, O_ps = (sem2(n) for n in
                ("S_ps", "max_ok", "Pr_ok", "PrT_ps", "PrT_ok", "O_ps"))
            Oh_ok, Og_ps, div_ok, O_ok = (sem2(n) for n in
                ("Oh_ok", "Og_ps", "div_ok", "O_ok"))
            OT_ps, OT_ok = sem2("OT_ps"), sem2("OT_ok")
            att_ps, tok1_ok, tok1T_ps, tok1T_ok = sem2("att_ps"), sem2("tok1_ok"), sem2("tok1T_ps"), sem2("tok1T_ok")
            X2T_ok, cq_ps, cq_ok = sem2("X2T_ok"), sem2("cq_ps"), sem2("cq_ok")
            upd_ps, upd_ok, updT_ps, updT_ok = sem2("upd_ps"), sem2("upd_ok"), sem2("updT_ps"), sem2("updT_ok")
            gate_ps, z_ok, zt_ok, tok2_ok = sem2("gate_ps"), sem2("z_ok"), sem2("zt_ok"), sem2("tok2_ok")
            X3_ok, X3T_ps, X3T_ok = sem2("X3_ok"), sem2("X3T_ps"), sem2("X3T_ok")
            gu_ps, act_ok, prod2_ok, hid_ok, down_ps, res_ok = (sem2(n) for n in
                ("gu_ps", "act_ok", "prod2_ok", "hid_ok", "down_ps", "res_ok"))
            NH = 2 * H
            FIRST_MIX_BANKS = (0, 1, 2, 3, 0, 1, 2, 3)
            MIX_BANKS = (5, 6, 7, 3, 6, 7, 0, 1)

            OUT_BANKS, QUERY_BANKS, MOUT_BANKS, GATE_BANKS = (2, 0), (2, 1), (2, 1), (3, 0)
            HEAD_BANKS = (4, 5, 2, 3)

            def after(b):
                return (b + 1) % B

            def turned(engine, t, e):
                def places(v, odd):
                    return v[:, t, :].rearrange("p (n e) -> p n e", e=2)[:, :, odd]
                return engine.tensor_tensor(places(QKr, e), places(QK, 1 - e), places(rope_sin, e), ALU.mult)

            block = second_ctx.enter_context(nc.Block())

            @block.sync
            def _(sp):
                sp.dma_start(x2[:], tiles(d["x"][0])).then_inc(x2_in, 16)
                sp.dma_start(src[:], tiles(d["fside"][0])).then_inc(src_in, 16)
                sp.dma_start(rope_cos[:], tiles(d["t_cos"])).then_inc(rope_in, 16)
                sp.dma_start(rope_sin[:], tiles(d["t_sin"])).then_inc(rope_in, 16)
                sp.wait_ge(o2_ok, KN)
                sp.dma_start(x2[:], tiles(d["x"][1])).then_inc(x2_in, 16)
                with sp.Fori(0, B) as b:
                    sp.wait_ge(kv_ok, at(b, 2, 2))
                    sp.dma_start(src[:], tiles(d["fside"][after(b)])).then_inc(src_in, 16)
                    sp.wait_ge(o2_ok, at(b + 1, KN, KN))
                    sp.dma_start(x2[:], tiles(d["x"][after(b + 1)])).then_inc(x2_in, 16)
                    sp.wait_ge(res_ok, b + 2)
                    sp.dma_start(tiles(out[b]), res[:]).then_inc(out_done, 16)
                sp.wait_ge(src_in, 16 * (B + 1))
                sp.wait_ge(x2_in, 16 * (B + 2))
                sp.wait_ge(out_done, 16 * B + 16)

            @block.gpsimd
            def _(pool):
                nc.gpsimd.memset(QP[:], 0.0).then_inc(poolstep, 1)
                for a in range(2):
                    nc.gpsimd.memset(VP[a][:], 0.0).then_inc(poolstep, 1)
                nc.gpsimd.memset(rms_eps[:], RMS_EPS).then_inc(pads_ok, 1)
                pool.wait_ge(poolstep, 3)
                nc.gpsimd.memset(QP[:, :, 0:H, ONE_COL:ONE_COL + 1], 1.0).then_inc(pads_ok, 1)
                for a in range(2):
                    ones_v = VP[a][:, :, 0:H * VW].rearrange("p t (h e) -> p t h e", e=VW)[:, :, :, ONE_COL:VW]
                    nc.gpsimd.memset(ones_v, 1.0).then_inc(pads_ok, 1)

                def add_x(m, i):
                    if i == 0:
                        pool.wait_ge(x2_in, at(m, 16, 16))
                    pool.wait_ge(abs2_ok, at(m, KN, i + 1))
                    nc.gpsimd.tensor_tensor(o2[:, i], o2[:, i], x2[:], ALU.add).then_inc(o2_ok, 1)

                def mean_to_rstd(m, n):
                    pool.wait_ge(ms_ok[n], at(m, 2, 2))
                    nc.gpsimd.tensor_tensor(mse[:, n], ms[:, n], rms_eps[:], ALU.add).then_inc(mse_ok[n], 1)
                    pool.wait_ge(mse_ok[n], m + 1)
                    nc.gpsimd.tensor_tensor(rstd[:, n], mse[:, n], mhalf[:], ALU.pow).then_inc(rs_ok[n], 1)

                for i in range(KN):
                    add_x(0, i)
                pool.wait_ge(pads_ok, 4)
                mean_to_rstd(0, 1)
                with pool.Fori(0, B) as b:
                    nb = b + 1
                    pool.wait_ge(tok0_ok, b + 1)
                    nc.gpsimd.tensor_tensor(tok0b[:], tok0[:], b_out[:].unsqueeze(1).broadcast_to([P, NT, L]),
                                            ALU.add).then_inc(tok0b_ok, 1)
                    pool.wait_ge(rope_in, 32)
                    for t in range(NT):
                        pool.wait_ge(qk_ok, at(b, 2, t + 1))
                        for e in range(2 - t):
                            r = turned(nc.gpsimd, t, e)
                        r.then_inc(rsin_ok, 1)
                    for t in range(NT):
                        c = nc.gpsimd.tensor_copy(
                            QP[:, t, H:2 * H, ONE_COL:ONE_COL + 1],
                            keybias[:, t, bass.ds(b, 1)].unsqueeze(1).broadcast_to([P, H, 1]))
                    c.then_inc(kb_ok, 1)
                    for i in range(3):
                        add_x(nb, i)
                    mean_to_rstd(b, 0)
                    add_x(nb, 3)
                    mean_to_rstd(b, 2)
                    for i in range(4, 7):
                        add_x(nb, i)
                    for tt in range(NT):
                        pool.wait_ge(mse_ok[3], at(b, 2, tt + 1))
                        nc.gpsimd.tensor_tensor(rstd[:, 3, tt:tt + 1], mse[:, 3, tt:tt + 1], mhalf[:, tt:tt + 1],
                                                ALU.pow).then_inc(rs_ok[3], 1)
                    add_x(nb, 7)
                    pool.wait_ge(tok2_ok, at(b, 2, 2))
                    nc.gpsimd.tensor_tensor(tok2b[:], tok2[:], b_down[:].unsqueeze(1).broadcast_to([P, NT, L]),
                                            ALU.add).then_inc(tok2b_ok, 1)
                    mean_to_rstd(nb, 1)

            @block.scalar
            def _(act):
                def squares_of(n, t, ready=None):
                    for tt in range(NT):
                        if ready:
                            act.wait_ge(ready[0], at(ready[1], NT, tt + 1))
                        nc.scalar.activation(deadA[:, tt], t[:, tt, :], ACT.Square, scale=L ** -0.5,
                                             accum_out=ms[:, n, tt:tt + 1]).then_inc(ms_ok[n], 1)

                def spectrum(m, batch, i, first=False):
                    if not first:
                        act.wait_ge(y2_ps, at(m, KN, i - 3))
                    for kt in range(NT):
                        e = nc.scalar.activation(E2[:, i % 4, kt, :], D[:, bass.ds(batch, 1), kt, :], ACT.Identity,
                                                 scale=wT[:, kt, i, bass.ds(batch, 1)],
                                                 bias=QR[:, kt, bass.ds(batch, 1)])
                    e.then_inc(E2_ok, 1)

                def abs_y(m, i, bank):
                    act.wait_ge(y2_ps, at(m, KN, i + 1))
                    nc.scalar.activation(o2[:, i], ps[bank][:], ACT.Abs).then_inc(abs2_ok, 1)

                def softmax_kernels(m):
                    act.wait_ge(score_ok, m + 1)
                    for ct in range(NT):
                        a_ = nc.scalar.activation(score[:, ct, :], score[:, ct, :], ACT.Exp, bias=smax[:, ct:ct + 1],
                                                  accum_out=ssum[:, ct:ct + 1])
                    a_.then_inc(sexp_ok, 1)

                def heads_T_out(b, a):
                    for g4 in range(4):
                        act.wait_ge(QKT_ps, at(b, 8, 4 * a + g4 + 1))
                        nc.scalar.activation(QKT[:, g4, :], ps[HEAD_BANKS[g4]][:], ACT.Copy).then_inc(QKT_ok, 1)

                def values_out(b, a, g4):
                    act.wait_ge(O_ps, at(b, NH, a * H + 4 * g4 + 4))
                    nc.scalar.activation(Oh[:, g4 % 2], ps[6 + g4 % 2][:, 0:C], ACT.Copy).then_inc(Oh_ok, 1)

                def attention(b, a, between):
                    for h in range(H):
                        act.wait_ge(max_ok, at(b, NH, a * H + h + 1))
                        if h >= 2:
                            act.wait_ge(PrT_ps, at(b, NH, a * H + h - 1))
                        for qt in range(NT):
                            e = nc.scalar.activation(Pr[:, h % 2, qt, :], ps[h % 4][:, qt * C:(qt + 1) * C], ACT.Exp,
                                                     bias=nmax[:, h % 4, qt:qt + 1])
                        e.then_inc(Pr_ok, 1)
                        if h in (6, 10, 14):
                            values_out(b, a, h // 4 - 1)
                        between(h)
                    values_out(b, a, 3)

                for i in range(-4, KN):
                    if i >= 0:
                        abs_y(0, i, FIRST_MIX_BANKS[i])
                    if 0 <= i + 4 < KN:
                        spectrum(0, 0, i + 4, first=(i < 0))
                for i in range(4):
                    spectrum(1, 1, i)
                softmax_kernels(0)
                act.wait_ge(tok0_ok, 1)
                squares_of(1, tok0)

                with act.Fori(0, B) as b:
                    nb, nxt, nxt2 = b + 1, after(b), after(b + 1)
                    act.wait_ge(X1T_ps, b + 1)
                    for ft in range(NT):
                        a_ = nc.scalar.activation(XT[:, ft, :], ps[4][:, ft * C:(ft + 1) * C], ACT.Identity,
                                                  scale=filmG[:, ft, bass.ds(b, 1)], bias=filmS[:, ft, bass.ds(b, 1)])
                    a_.then_inc(X1T_ok, 1)
                    for i in range(2):
                        abs_y(nb, i, MIX_BANKS[i])
                    heads_T_out(b, 0)

                    def self_between(h):
                        if h == 1:
                            abs_y(nb, 2, MIX_BANKS[2])
                        if h in (2, 8, 10):
                            spectrum(nb, nxt, {2: 4, 8: 5, 10: 6}[h])
                        if h == 3:
                            act.wait_ge(src_in, at(b, 16, 16))
                            squares_of(0, src)
                        if h == 4:
                            act.wait_ge(srcT_ps, b + 1)
                            for ft in range(NT):
                                s_ = nc.scalar.activation(srcT[:, ft, :], ps[7][:, ft * C:(ft + 1) * C], ACT.Copy,
                                                          scale=n_s[:, ft:ft + 1])
                            s_.then_inc(srcT_ok, 1)
                    attention(b, 0, self_between)
                    act.wait_ge(OT_ps, at(b, 2, 1))
                    nc.scalar.activation(OT[:], ps[4][:], ACT.Copy).then_inc(OT_ok, 1)
                    abs_y(nb, 3, MIX_BANKS[3])
                    squares_of(2, tok1, ready=(tok1_ok, b))
                    act.wait_ge(tok1T_ps, b + 1)
                    for ft in range(NT):
                        a_ = nc.scalar.activation(XT[:, ft, :], ps[5][:, ft * C:(ft + 1) * C], ACT.Copy,
                                                  scale=n_sq[:, ft:ft + 1])
                    a_.then_inc(X2T_ok, 1)
                    nc.scalar.activation(tok1T[:], ps[5][:], ACT.Copy).then_inc(tok1T_ok, 1)
                    abs_y(nb, 4, MIX_BANKS[4])
                    heads_T_out(b, 1)

                    def cross_between(h):
                        if h == 1:
                            abs_y(nb, 5, MIX_BANKS[5])
                        if h == 2:
                            spectrum(nb, nxt, 7)
                        if h in (4, 6):
                            spectrum(b + 2, nxt2, h // 2 - 2)
                    attention(b, 1, cross_between)
                    act.wait_ge(OT_ps, at(b, 2, 2))
                    nc.scalar.activation(OT[:], ps[4][:], ACT.Copy).then_inc(OT_ok, 1)
                    abs_y(nb, 6, MIX_BANKS[6])
                    act.wait_ge(updT_ps, b + 1)
                    nc.scalar.activation(updT[:], ps[5][:], ACT.Copy).then_inc(updT_ok, 1)
                    for tt in range(NT):
                        act.wait_ge(z_ok, at(b, 2, tt + 1))
                        nc.scalar.activation(z[:, tt, :], z[:, tt, :], ACT.Tanh, scale=0.5).then_inc(zt_ok, 1)
                    abs_y(nb, 7, MIX_BANKS[7])
                    act.wait_ge(X3T_ps, b + 1)
                    for ft in range(NT):
                        nc.scalar.activation(XT[:, ft, :], ps[7][:, ft * C:(ft + 1) * C], ACT.Copy,
                                             scale=n_ffn[:, ft:ft + 1]).then_inc(X3T_ok, 1)
                    for m in range(MT):
                        act.wait_ge(gu_ps, at(b, MT, m + 1))
                        if m >= 2:
                            act.wait_ge(hid_ok, at(b, MT, m - 1))
                        nc.scalar.activation(th[:, m % 2, :], ps[m % 4][:, 0:C], ACT.Tanh, scale=0.5,
                                             bias=b_guh[:, m:m + 1])
                        nc.scalar.activation(val[:, m % 2, :], ps[m % 4][:, C:2 * C], ACT.Identity, scale=0.5,
                                             bias=b_guh[:, MT + m:MT + m + 1]).then_inc(act_ok, 1)
                        if m == 0:
                            softmax_kernels(nb)
                        if m in (2, 4):
                            spectrum(b + 2, nxt2, m // 2 + 1)
                        if m == 6:
                            act.wait_ge(tok0_ok, nb + 1)
                            squares_of(1, tok0)

            @block.tensor
            def _(pe):
                def turn(bank, t, done, ready=None):
                    for tt in range(NT):
                        if ready:
                            pe.wait_ge(ready[0], at(ready[1], NT, tt + 1))
                        for ft in range(NT):
                            m = nc.tensor.transpose(ps[bank][:, ft * C + tt * P:ft * C + (tt + 1) * P],
                                                    t[:, tt, ft * P:(ft + 1) * P], eye[:])
                    m.then_inc(done, 1)

                def project(bank, col, tt, xT, wt, lo, n):
                    for kt in range(NT):
                        m = nc.tensor.matmul(ps[bank][:, col:col + n], xT[:, kt, tt * P:(tt + 1) * P],
                                             wt[:, kt, lo:lo + n], start=(kt == 0), stop=(kt == NT - 1))
                    return m

                def gain_rows(m):
                    pe.wait_ge(qgs_ok, m + 1)
                    for lt in range(NT):
                        i_ = nc.tensor.matmul(ps[4][:, lt * P:(lt + 1) * P], qgs[:, lt:lt + 1].broadcast_to([P, P]),
                                              eye[:], start=True, stop=True)
                    i_.then_inc(QGB_ps, 1)

                def mix(m, i, bank, halves=(0, 1)):
                    pe.wait_ge(E2_ok, at(m, KN, i + 1))
                    for ct in halves:
                        for kt in range(NT):
                            i_ = nc.tensor.matmul(ps[bank][:, ct * L:(ct + 1) * L],
                                                  E2[:, i % 4, kt, ct * P:(ct + 1) * P], Fm[:, kt, :],
                                                  start=(kt == 0), stop=(kt == 1))
                    if ct == 1:
                        i_.then_inc(y2_ps, 1)

                def turn_heads(b, a):
                    for g4 in range(4):
                        for part in range(2):
                            for tt in range(NT):
                                h0 = part * H + 4 * g4
                                m = nc.tensor.transpose(
                                    ps[HEAD_BANKS[g4]][:, part * C + tt * P:part * C + (tt + 1) * P],
                                    QP[:, tt, h0:h0 + 4, :].rearrange("p h e -> p (h e)"), eye[:])
                        m.then_inc(QKT_ps, 1)

                def attention(b, a, between):
                    pe.wait_ge(QKT_ok, at(b, 8, 4 * a + 4))
                    for n in range(H + 5):
                        if n < H:
                            g4, j = n // 4, n % 4
                            if n >= 4:
                                pe.wait_ge(Pr_ok, at(b, NH, a * H + n - 3))
                            for qt in range(NT):
                                m = nc.tensor.matmul(ps[j][:, qt * C:(qt + 1) * C],
                                                     QKT[j * HP:(j + 1) * HP, g4, qt * P:(qt + 1) * P],
                                                     QKT[j * HP:(j + 1) * HP, g4, C:2 * C], start=True, stop=True)
                            m.then_inc(S_ps, 1)
                        between(n)
                        h = n - 2
                        if 0 <= h < H:
                            pe.wait_ge(Pr_ok, at(b, NH, a * H + h + 1))
                            if h >= 2:
                                pe.wait_ge(PrT_ok, at(b, NH, a * H + h - 1))
                            for kt in range(NT):
                                for qt in range(NT):
                                    m = nc.tensor.transpose(ps[4 + h % 2][:, kt * C + qt * P:kt * C + (qt + 1) * P],
                                                            Pr[:, h % 2, qt, kt * P:(kt + 1) * P], eye[:])
                            m.then_inc(PrT_ps, 1)
                        h = n - 3
                        if 0 <= h < H:
                            g4, j = h // 4, h % 4
                            pe.wait_ge(PrT_ok, at(b, NH, a * H + h + 1))
                            if j == 0 and g4 >= 2:
                                pe.wait_ge(O_ok, at(b, 8, 4 * a + g4 - 1))
                            for kt in range(NT):
                                m = nc.tensor.matmul(ps[6 + g4 % 2][j * HP:(j + 1) * HP, 0:C],
                                                     VP[a][:, kt, h * VW:h * VW + HP], PrT[:, h % 2, kt, :],
                                                     start=(kt == 0), stop=(kt == 1))
                            m.then_inc(O_ps, 1)
                        if n in (8, 12, 16, 20):
                            g4 = (n - 8) // 4
                            pe.wait_ge(Oh_ok, at(b, 8, 4 * a + g4 + 1))
                            for qt in range(NT):
                                m = nc.tensor.transpose(ps[6 + g4 % 2][:, C + qt * P:C + (qt + 1) * P],
                                                        Oh[:, g4 % 2, qt * P:(qt + 1) * P], eye[:])
                            m.then_inc(Og_ps, 1)

                gain_rows(0)
                for i in range(KN):
                    if i >= 4:
                        pe.wait_ge(abs2_ok, i - 3)
                    mix(0, i, FIRST_MIX_BANKS[i])

                with pe.Fori(0, B) as b:
                    nb = b + 1
                    pe.wait_ge(X1_ok, b + 1)
                    turn(4, X, X1T_ps)
                    mix(nb, 0, MIX_BANKS[0])
                    pe.wait_ge(X1T_ok, b + 1)
                    for tt in range(NT):
                        project(2 * tt, 0, tt, XT, w_qkv, 0, 2 * L).then_inc(qkv_ps, 1)
                        project(2 * tt + 1, 0, tt, XT, w_qkv, 2 * L, L).then_inc(qkv_ps, 1)
                    gain_rows(nb)
                    pe.wait_ge(res_ok, b + 1)
                    mix(nb, 1, MIX_BANKS[1])
                    pe.wait_ge(abs2_ok, at(nb, KN, 1))
                    pe.wait_ge(QGB_ok, nb + 1)
                    pe.wait_ge(qp_ok, at(b, 2, 2))
                    pe.wait_ge(kb_ok, b + 1)
                    pe.wait_ge(v_ok, at(b, 2, 2))
                    turn_heads(b, 0)
                    mix(nb, 2, MIX_BANKS[2], halves=(0,))

                    def self_between(n):
                        if n == 1:
                            mix(nb, 2, MIX_BANKS[2], halves=(1,))
                        if n == 3:
                            pe.wait_ge(abs2_ok, at(nb, KN, 2))
                        if n == 4:
                            pe.wait_ge(abs2_ok, at(nb, KN, 3))
                            pe.wait_ge(src_in, at(b, 16, 16))
                            turn(7, src, srcT_ps)
                        if n == 7:
                            pe.wait_ge(srcT_ok, b + 1)
                        if n == 20:
                            mix(nb, 3, MIX_BANKS[3], halves=(0,))
                        if n in (17, 18):
                            project(n - 17, 0, n - 17, srcT, w_min, L, 2 * L).then_inc(kv_ps, 1)
                    attention(b, 0, self_between)
                    pe.wait_ge(O_ok, at(b, 8, 4))
                    turn(4, O, OT_ps)
                    mix(nb, 3, MIX_BANKS[3], halves=(1,))
                    pe.wait_ge(OT_ok, at(b, 2, 1))
                    pe.wait_ge(kv_ok, at(b, 2, 1))
                    for tt in range(NT):
                        project(OUT_BANKS[tt], 0, tt, OT, w_out, 0, L).then_inc(att_ps, 1)
                    turn(5, tok1, tok1T_ps, ready=(tok1_ok, b))
                    mix(nb, 4, MIX_BANKS[4], halves=(0,))
                    pe.wait_ge(X2T_ok, b + 1)
                    pe.wait_ge(kv_ok, at(b, 2, 2))
                    for tt in range(NT):
                        project(QUERY_BANKS[tt], 0, tt, XT, w_min, 0, L).then_inc(cq_ps, 1)
                    mix(nb, 4, MIX_BANKS[4], halves=(1,))
                    pe.wait_ge(cq_ok, at(b, 2, 2))
                    pe.wait_ge(abs2_ok, at(nb, KN, 4))
                    pe.wait_ge(tok1T_ok, b + 1)
                    turn_heads(b, 1)
                    mix(nb, 5, MIX_BANKS[5], halves=(0,))

                    def cross_between(n):
                        if n == 1:
                            mix(nb, 5, MIX_BANKS[5], halves=(1,))
                        if n == 3:
                            pe.wait_ge(abs2_ok, at(nb, KN, 5))
                        if n == 7:
                            pe.wait_ge(abs2_ok, at(nb, KN, 6))
                        if n == 17:
                            mix(nb, 6, MIX_BANKS[6], halves=(0,))
                    attention(b, 1, cross_between)
                    pe.wait_ge(O_ok, at(b, 8, 8))
                    turn(4, O, OT_ps)
                    mix(nb, 6, MIX_BANKS[6], halves=(1,))
                    pe.wait_ge(OT_ok, at(b, 2, 2))
                    for tt in range(NT):
                        project(MOUT_BANKS[tt], 0, tt, OT, w_mout, 0, L).then_inc(upd_ps, 1)
                    turn(5, upd, updT_ps, ready=(upd_ok, b))
                    pe.wait_ge(abs2_ok, at(nb, KN, 7))
                    for tt in range(NT):
                        for kt in range(4):
                            if (tt, kt) == (0, 2):
                                pe.wait_ge(updT_ok, b + 1)
                            xT_ = tok1T if kt < 2 else updT
                            m = nc.tensor.matmul(ps[GATE_BANKS[tt]][:, 0:L], xT_[:, kt % 2, tt * P:(tt + 1) * P],
                                                 w_gate[:, kt, :], start=(kt == 0), stop=(kt == 3))
                        m.then_inc(gate_ps, 1)
                    mix(nb, 7, MIX_BANKS[7])
                    turn(7, X, X3T_ps, ready=(X3_ok, b))
                    pe.wait_ge(abs2_ok, at(nb, KN, 8))
                    for m_ in range(MT + 2):
                        if m_ < MT:
                            if m_ >= 4:
                                pe.wait_ge(hid_ok, at(b, MT, m_ - 3))
                            for part in range(2):
                                for kt in range(NT):
                                    if m_ == 0 and part == 0:
                                        pe.wait_ge(X3T_ok, at(b, NT, kt + 1))
                                    c0 = part * HID + m_ * P
                                    m = nc.tensor.matmul(ps[m_ % 4][:, part * C:(part + 1) * C],
                                                         w_gu[:, kt, c0:c0 + P], XT[:, kt, :],
                                                         start=(kt == 0), stop=(kt == 1))
                            m.then_inc(gu_ps, 1)
                        k_ = m_ - 2
                        if k_ >= 0:
                            pe.wait_ge(hid_ok, at(b, MT, k_ + 1))
                            for tt in range(NT):
                                m = nc.tensor.matmul(ps[6 + tt][:, 0:L], hid[:, k_, tt * P:(tt + 1) * P],
                                                     w_down[:, k_, :], start=(k_ == 0), stop=(k_ == MT - 1))
                    m.then_inc(down_ps, 1)

            @block.vector
            def _(dve):
                def gain(m, batch):
                    nc.vector.tensor_copy(qgs[:], qg[:, :, bass.ds(batch, 1)]).then_inc(qgs_ok, 1)

                def gain_out(m):
                    dve.wait_ge(QGB_ps, m + 1)
                    nc.vector.tensor_copy(QGB[:], ps[4][:, 0:L]).then_inc(QGB_ok, 1)

                def scores_of(m, i):
                    dve.wait_ge(o2_ok, at(m, KN, i + 1))
                    if i == 0:
                        dve.wait_ge(QGB_ok, m + 1)
                    for ct in range(NT):
                        if i >= 1:
                            dve.wait_ge(dot_ok, at(m, NT * KN, NT * (i - 1) + ct + 1))
                        nc.vector.tensor_tensor_reduce(dead[:, ct], o2[:, i, ct, :], QGB[:], 1.0, 0.0, ALU.mult,
                                                       ALU.add, score[:, ct, i:i + 1]).then_inc(dot_ok, 1)

                def scores_max(m):
                    dve.wait_ge(dot_ok, at(m, NT * KN, NT * KN))
                    nc.vector.tensor_reduce(smax[:], score[:], AX.X, ALU.max, negate=True).then_inc(score_ok, 1)

                def weigh(m, i):
                    if i == 0:
                        dve.wait_ge(sexp_ok, m + 1)
                        nc.vector.reciprocal(srec[:], ssum[:]).then_inc(wsum_ok, 1)
                    for ct in range(NT):
                        if i == 0:
                            nc.vector.tensor_scalar(tok0[:, ct, :], o2[:, 0, ct, :], score[:, ct, 0:1], None,
                                                    ALU.mult).then_inc(wsum_ok, 1)
                        else:
                            dve.wait_ge(wsum_ok, at(m, 19, NT * i + ct))
                            nc.vector.scalar_tensor_tensor(out=tok0[:, ct, :], in0=o2[:, i, ct, :],
                                                           scalar=score[:, ct, i:i + 1], in1=tok0[:, ct, :],
                                                           op0=ALU.mult, op1=ALU.add).then_inc(wsum_ok, 1)

                def normalise(m):
                    for ct in range(NT):
                        dve.wait_ge(wsum_ok, at(m, 19, 16 + ct))
                        nc.vector.scalar_tensor_tensor(out=tok0[:, ct, :], in0=tok0[:, ct, :],
                                                       scalar=srec[:, ct:ct + 1], in1=RG[:],
                                                       op0=ALU.mult, op1=ALU.mult).then_inc(wsum_ok, 1)
                    dve.wait_ge(wsum_ok, at(m, 19, 19))
                    nc.vector.tensor_tensor(tok0[:], tok0[:], BP[:].unsqueeze(1).broadcast_to([P, NT, L]),
                                            ALU.add).then_inc(tok0_ok, 1)

                def first_norm(m):
                    dve.wait_ge(rs_ok[1], m + 1)
                    for tt in range(NT):
                        v = nc.vector.tensor_scalar(X[:, tt, :], tok0[:, tt, :], rstd[:, 1, tt:tt + 1], None, ALU.mult)
                    v.then_inc(X1_ok, 1)

                def heads(view, w=HD):
                    return view.rearrange("p (h e) -> p h e", e=w)

                def kv_out(b, tt):
                    dve.wait_ge(kv_ps, at(b, 2, tt + 1))
                    nc.vector.scalar_tensor_tensor(
                        out=QP[:, tt, H:2 * H, 0:HD], in0=heads(ps[tt][:, 0:L]), scalar=rstd[:, 0, tt:tt + 1],
                        in1=heads(b_min[:, L:2 * L]), op0=ALU.mult, op1=ALU.add)
                    nc.vector.scalar_tensor_tensor(
                        out=heads(VP[1][:, tt, 0:H * VW], VW)[:, :, 0:HD], in0=heads(ps[tt][:, L:2 * L]),
                        scalar=rstd[:, 0, tt:tt + 1], in1=heads(b_min[:, 2 * L:3 * L]),
                        op0=ALU.mult, op1=ALU.add).then_inc(kv_ok, 1)

                def attention(b, a, between):
                    for n in range(H + 5):
                        if n < H:
                            dve.wait_ge(S_ps, at(b, NH, a * H + n + 1))
                            nc.vector.tensor_reduce(nmax[:, n % 4, :], ps[n % 4][:].rearrange("p (t k) -> p t k", t=NT),
                                                    AX.X, ALU.max, negate=True).then_inc(max_ok, 1)
                        h = n - 2
                        if 0 <= h < H:
                            dve.wait_ge(PrT_ps, at(b, NH, a * H + h + 1))
                            if h >= 2:
                                dve.wait_ge(O_ps, at(b, NH, a * H + h - 1))
                            nc.vector.tensor_copy(PrT[:, h % 2], ps[4 + h % 2][:]).then_inc(PrT_ok, 1)
                        if n in (9, 13, 17, 20):
                            g4 = 3 if n == 20 else (n - 9) // 4
                            k_ = at(b, 8, 4 * a + g4 + 1)
                            dve.wait_ge(Og_ps, k_)
                            og = ps[6 + g4 % 2][:, C:2 * C].rearrange("p (n e) -> p n e", e=HP)
                            nc.vector.reciprocal(orec[:, g4, :], og[:, :, ONE_COL]).then_inc(div_ok, 1)
                            dve.wait_ge(div_ok, k_)
                            for qt in range(NT):
                                v = nc.vector.tensor_tensor(
                                    heads(O[:, qt, g4 * 4 * HD:(g4 + 1) * 4 * HD]), og[:, 4 * qt:4 * qt + 4, 0:HD],
                                    orec[:, g4, 4 * qt:4 * qt + 4].unsqueeze(2).broadcast_to([P, 4, HD]), ALU.mult)
                            v.then_inc(O_ok, 1)
                        between(n)

                dve.sem_inc(out_done, 16)
                dve.sem_inc(res_ok, 1)
                gain(0, 0)
                gain_out(0)
                for i in range(KN):
                    scores_of(0, i)
                scores_max(0)
                for i in range(KN):
                    weigh(0, i)
                normalise(0)
                first_norm(0)

                dve.wait_ge(pads_ok, 4)
                dve.wait_ge(rope_in, 32)
                with dve.Fori(0, B) as b:
                    nb = b + 1
                    gain(nb, after(b))
                    nc.vector.tensor_scalar(mobv[:], b_mout[:], vrow[:, bass.ds(b, 1)], None, ALU.mult).then_inc(mobv_ok, 1)

                    for tt in range(NT):
                        dve.wait_ge(qkv_ps, at(b, 4, 2 * tt + 1))
                        nc.vector.tensor_tensor(QK[:, tt, :], ps[2 * tt][:], b_qkv[:, 0:2 * L], ALU.add).then_inc(qk_ok, 1)
                        dve.wait_ge(qk_ok, at(b, 2, tt + 1))
                        if tt == 1:
                            turned(nc.vector, 1, 1)
                        nc.vector.tensor_tensor(QKc[:, tt, :], QK[:, tt, :], rope_cos[:, tt, :], ALU.mult).then_inc(rcos_ok, 1)
                        dve.wait_ge(qkv_ps, at(b, 4, 2 * tt + 2))
                        nc.vector.tensor_tensor(heads(VP[0][:, tt, 0:H * VW], VW)[:, :, 0:HD],
                                                heads(ps[2 * tt + 1][:, 0:L]), heads(b_qkv[:, 2 * L:3 * L]),
                                                ALU.add).then_inc(v_ok, 1)
                    for tt in range(NT):
                        dve.wait_ge(rcos_ok, at(b, 2, tt + 1))
                        dve.wait_ge(rsin_ok, at(b, 2, tt + 1))
                        nc.vector.tensor_tensor(QP[:, tt, :, 0:HD], heads(QKc[:, tt, :]), heads(QKr[:, tt, :]),
                                                ALU.add).then_inc(qp_ok, 1)
                        if tt == 0:
                            gain_out(nb)

                    def self_between(n):
                        if n in (6, 8, 11):
                            scores_of(nb, {6: 0, 8: 1, 11: 2}[n])
                    attention(b, 0, self_between)
                    dve.wait_ge(rs_ok[0], b + 1)
                    kv_out(b, 0)
                    dve.wait_ge(tok0b_ok, b + 1)
                    for tt in range(NT):
                        dve.wait_ge(att_ps, at(b, 2, tt + 1))
                        nc.vector.tensor_tensor(tok1[:, tt, :], ps[OUT_BANKS[tt]][:, 0:L], tok0b[:, tt, :],
                                                ALU.add).then_inc(tok1_ok, 1)
                    kv_out(b, 1)

                    dve.wait_ge(rs_ok[2], b + 1)
                    nc.vector.tensor_scalar(rq[:], rstd[:, 2], HD ** -0.5, None, ALU.mult).then_inc(step2, 1)
                    dve.wait_ge(step2, at(b, 3, 1))
                    for tt in range(NT):
                        dve.wait_ge(cq_ps, at(b, 2, tt + 1))
                        nc.vector.scalar_tensor_tensor(
                            out=QP[:, tt, 0:H, 0:HD], in0=heads(ps[QUERY_BANKS[tt]][:, 0:L]),
                            scalar=rq[:, tt:tt + 1], in1=heads(b_min[:, 0:L]), op0=ALU.mult,
                            op1=ALU.add).then_inc(cq_ok, 1)

                    def cross_between(n):
                        if n in (6, 8, 11):
                            scores_of(nb, {6: 3, 8: 4, 11: 5}[n])
                    attention(b, 1, cross_between)
                    dve.wait_ge(mobv_ok, b + 1)
                    for tt in range(NT):
                        dve.wait_ge(upd_ps, at(b, 2, tt + 1))
                        nc.vector.scalar_tensor_tensor(out=upd[:, tt, :], in0=ps[MOUT_BANKS[tt]][:, 0:L],
                                                       scalar=vrow[:, bass.ds(b, 1)], in1=mobv[:],
                                                       op0=ALU.mult, op1=ALU.add).then_inc(upd_ok, 1)
                    scores_of(nb, 6)
                    for tt in range(NT):
                        dve.wait_ge(gate_ps, at(b, 2, tt + 1))
                        nc.vector.tensor_tensor(z[:, tt, :], ps[GATE_BANKS[tt]][:, 0:L], b_gate[:],
                                                ALU.add).then_inc(z_ok, 1)
                        dve.wait_ge(zt_ok, at(b, 2, tt + 1))
                        nc.vector.scalar_tensor_tensor(out=z[:, tt, :], in0=z[:, tt, :], scalar=1.0, in1=upd[:, tt, :],
                                                       op0=ALU.add, op1=ALU.mult).then_inc(step2, 1)
                        dve.wait_ge(step2, at(b, 3, 2 + tt))
                        nc.vector.scalar_tensor_tensor(out=tok2[:, tt, :], in0=z[:, tt, :], scalar=0.5,
                                                       in1=tok1[:, tt, :], op0=ALU.mult, op1=ALU.add).then_inc(tok2_ok, 1)
                        dve.wait_ge(tok2_ok, at(b, 2, tt + 1))
                        nc.vector.tensor_tensor_reduce(X[:, tt, :], tok2[:, tt, :], tok2[:, tt, :], 1.0 / L, RMS_EPS,
                                                       ALU.mult, ALU.add, mse[:, 3, tt:tt + 1]).then_inc(mse_ok[3], 1)

                    for tt in range(NT):
                        dve.wait_ge(rs_ok[3], at(b, 2, tt + 1))
                        nc.vector.tensor_scalar(X[:, tt, :], tok2[:, tt, :], rstd[:, 3, tt:tt + 1], None,
                                                ALU.mult).then_inc(X3_ok, 1)
                    scores_of(nb, 7)
                    scores_max(nb)
                    for m in range(MT):
                        dve.wait_ge(act_ok, at(b, MT, m + 1))
                        nc.vector.scalar_tensor_tensor(out=th[:, m % 2, :], in0=th[:, m % 2, :], scalar=1.0,
                                                       in1=val[:, m % 2, :], op0=ALU.add, op1=ALU.mult).then_inc(prod2_ok, 1)
                        dve.wait_ge(prod2_ok, at(b, MT, m + 1))
                        nc.vector.scalar_tensor_tensor(out=hid[:, m, :], in0=ps[m % 4][:, 0:C], scalar=b_gu[:, m:m + 1],
                                                       in1=th[:, m % 2, :], op0=ALU.add, op1=ALU.mult).then_inc(hid_ok, 1)
                        if 1 <= m <= 4:
                            weigh(nb, 2 * m - 2)
                            weigh(nb, 2 * m - 1)
                        if m == 5:
                            normalise(nb)
                    first_norm(nb)
                    dve.wait_ge(tok2b_ok, b + 1)
                    dve.wait_ge(down_ps, b + 1)
                    dve.wait_ge(out_done, at(b, 16, 16))
                    for tt in range(NT):
                        v = nc.vector.tensor_tensor(res[:, tt, :], ps[6 + tt][:, 0:L], tok2b[:, tt, :], ALU.add)
                    v.then_inc(res_ok, 1)


_PLAIN = {"x": "x", "cond": "cond_1024", "fside": "fside_BxSxS_0", "sigmas": "L0_cond_sigmas",
          "centers": "L0_cond_center_shift", "gamma": "L0_cond_gamma", "beta": "L0_cond_beta",
          "attn_norm_w": "L1_cond_attn_norm_w", "qkv_b": "L1_cond_qkv_b", "out_b": "L1_cond_out_b",
          "film_b": "L1_cond_film_b", "sq_norm_w": "L1_cond_sq_norm_w", "s_norm_w": "L1_cond_s_norm_w",
          "mha_in_b": "L1_cond_mha_in_b", "mha_out_b": "L1_cond_mha_out_b", "gate_b": "L1_cond_gate_b",
          "ffn_norm_w": "L1_cond_ffn_norm_w", "gu_b": "L1_cond_gu_b", "down_b": "L1_cond_down_b"}
_COLUMNS = ("gamma", "beta", "attn_norm_w", "film_b", "gu_b", "sq_norm_w", "s_norm_w", "ffn_norm_w")
_TURNED = {"qkv_wT": "L1_cond_qkv_w", "out_wT": "L1_cond_out_w", "film_wT": "L1_cond_film_w",
           "mha_in_wT": "L1_cond_mha_in_w", "mha_out_wT": "L1_cond_mha_out_w",
           "gate_wT": "L1_cond_gate_w", "gu_wT": "L1_cond_gu_w", "down_wT": "L1_cond_down_w"}


def kernel(**inputs):
    import numpy as _np
    import concourse.bacc as _bacc
    from concourse import mybir as _mybir
    from concourse.bass_utils import run_bass_kernel_spmd as _run

    nc = _bacc.Bacc("TRN2", target_bir_lowering=False, num_devices=1)
    arrays = {n: _np.ascontiguousarray(inputs[s]) for n, s in _PLAIN.items()}
    arrays.update({n: _np.ascontiguousarray(_np.asarray(inputs[s]).T) for n, s in _TURNED.items()})
    for n in _COLUMNS:
        arrays[n] = _np.ascontiguousarray(arrays[n].reshape(-1, P).T)
    arrays["mask"] = _np.ascontiguousarray(inputs["mask_BxS_bk0"])
    arrays.update(shape_tables())
    feed, d = {}, {}
    for n, a in arrays.items():
        feed[f"in_{n}"] = a
        d[n] = nc.dram_tensor(f"in_{n}", a.shape, _mybir.dt.from_np(a.dtype), kind="ExternalInput").ap()
    out = nc.dram_tensor("out_dram", (B, C, L), _mybir.dt.float32, kind="ExternalOutput").ap()
    build(nc, d, out)
    r = _run(nc, [feed], core_ids=[0])
    return r.results[0]["out_dram"]
```
